# Optimizing a Trainium2 kernel written in Bass

```python
import numpy as np
import jax
import jax.numpy as jnp

def _softmax(x, axis=-1):
    return jax.nn.softmax(x, axis=axis)

def _gelu(x):
    return jax.nn.gelu(x, approximate=True)

def _silu(x):
    return jax.nn.silu(x)

def _sigmoid(x):
    return jax.nn.sigmoid(x)

def _layernorm(x, axis=-1, eps=1e-05):
    m = jnp.mean(x, axis=axis, keepdims=True)
    v = jnp.var(x, axis=axis, keepdims=True)
    return (x - m) / jnp.sqrt(v + eps)

def _scatter_add(tgt, idx, src, axis=0):
    return tgt.at[idx].add(src)

def _segment_sum(src, seg, n):
    return jax.ops.segment_sum(src, seg, n)
kernel_name = 'mk_lm_tower_d1_tok_ids768_r4_4b4ba5'

def setup_inputs(seed: int=0):
    np.random.seed(seed)
    _w = jnp.asarray

    def _rec_inputs():
        import jax
        import jax.numpy as jnp
        _rk = jax.random.key(seed)
        x = jax.random.randint(jax.random.fold_in(_rk, 1), (128, 128), 0, 31921, jnp.int32)
        return x
    x = _rec_inputs()

    def _L0_tok_setup():
        import jax, jax.numpy as jnp
        import numpy as np
        B, L, V, D_MODEL = (1, 512, 8000, 192)
        N_LAYER, D_STATE, EXPAND, D_CONV = (2, 16, 2, 4)
        D_INNER = EXPAND * D_MODEL
        DT_RANK = -(-D_MODEL // D_STATE)
        EPS = 1e-05

        def _rmsnorm(x, w):
            return x * jax.lax.rsqrt(jnp.mean(x * x, axis=-1, keepdims=True) + EPS) * w

        def _selective_scan(u, delta, A, Bm, Cm, D):
            deltaA = jnp.exp(delta[..., None] * A)
            dBu = delta[..., None] * Bm[:, :, None, :] * u[..., None]

            def comb(c1, c2):
                a1, b1 = c1
                a2, b2 = c2
                return (a2 * a1, a2 * b1 + b2)
            _, h = jax.lax.associative_scan(comb, (deltaA, dBu), axis=1)
            y = jnp.einsum('bldn,bln->bld', h, Cm)
            return y + u * D

        def _mamba_block(x, in_proj_w, conv_w, conv_b, x_proj_w, dt_proj_w, dt_proj_b, A_log, D, out_proj_w):
            xz = x @ in_proj_w
            xr, res = jnp.split(xz, 2, axis=-1)
            xc = jax.lax.conv_general_dilated(jnp.swapaxes(xr, 1, 2), conv_w, (1,), [(D_CONV - 1, 0)], feature_group_count=D_INNER, dimension_numbers=('NCH', 'OIH', 'NCH'))
            xr = jax.nn.silu(jnp.swapaxes(xc + conv_b[:, None], 1, 2))
            A = -jnp.exp(A_log)
            x_dbl = xr @ x_proj_w
            dt, Bm, Cm = jnp.split(x_dbl, [DT_RANK, DT_RANK + D_STATE], axis=-1)
            delta = jax.nn.softplus(dt @ dt_proj_w + dt_proj_b)
            y = _selective_scan(xr, delta, A, Bm, Cm, D)
            return y * jax.nn.silu(res) @ out_proj_w
        key = jax.random.key(seed)
        ks = jax.random.split(key, 12)
        s = 0.02
        inp = {'input_ids': jax.random.randint(ks[0], (B, L), 0, V), 'emb': jax.random.normal(ks[1], (V, D_MODEL), jnp.float32) * s, 'norm_w': jnp.ones((N_LAYER, D_MODEL), jnp.float32), 'in_proj_w': jax.random.normal(ks[2], (N_LAYER, D_MODEL, 2 * D_INNER), jnp.float32) * s, 'conv_w': jax.random.normal(ks[3], (N_LAYER, D_INNER, 1, D_CONV), jnp.float32) * s, 'conv_b': jnp.zeros((N_LAYER, D_INNER), jnp.float32), 'x_proj_w': jax.random.normal(ks[4], (N_LAYER, D_INNER, DT_RANK + 2 * D_STATE), jnp.float32) * s, 'dt_proj_w': jax.random.normal(ks[5], (N_LAYER, DT_RANK, D_INNER), jnp.float32) * s, 'dt_proj_b': jax.random.normal(ks[6], (N_LAYER, D_INNER), jnp.float32) * s, 'A_log': jnp.tile(jnp.log(jnp.arange(1, D_STATE + 1, dtype=jnp.float32)), (N_LAYER, D_INNER, 1)), 'D': jnp.ones((N_LAYER, D_INNER), jnp.float32), 'out_proj_w': jax.random.normal(ks[7], (N_LAYER, D_INNER, D_MODEL), jnp.float32) * s}
        return inp
    _L0_tok_all = _L0_tok_setup()
    _L0_tok_in = {k: v for k, v in _L0_tok_all.items() if k in ('emb', 'norm_w', 'in_proj_w', 'conv_w', 'conv_b', 'x_proj_w', 'dt_proj_w', 'dt_proj_b', 'A_log', 'D', 'out_proj_w')}
    del _L0_tok_all

    def _L0_attn_setup():
        import jax, jax.numpy as jnp
        import numpy as np
        B, N, D, H = (4, 256, 192, 12)
        HD = D // H
        MLP = 4 * D
        LAMBDA_INIT = 0.1
        LAYER_IDX, MAX_LAYER = (0, 12)

        def _layernorm(x, w, b, eps=1e-05):
            m = x.mean(-1, keepdims=True)
            v = ((x - m) ** 2).mean(-1, keepdims=True)
            return (x - m) * jax.lax.rsqrt(v + eps) * w + b

        def _rmsnorm(x, w, eps=1e-06):
            return x * jax.lax.rsqrt((x * x).mean(-1, keepdims=True) + eps) * w

        def _split_qkv(h, w):
            qkv = (h @ w.T).reshape(h.shape[0], h.shape[1], 3, H, HD)
            qkv = qkv.transpose(2, 0, 3, 1, 4)
            return (qkv[0], qkv[1], qkv[2])

        def _diff_block(x, ln1_w, ln1_b, qkv1_w, qkv2_w, proj_w, proj_b, rms_w, lam1, lam2, ln2_w, ln2_b, fc1_w, fc1_b, fc2_w, fc2_b):
            Bx, Nx, Cx = x.shape
            scale = HD ** (-0.5)
            h = _layernorm(x, ln1_w, ln1_b)
            q1, k1, v1 = _split_qkv(h, qkv1_w)
            q2, k2, _ = _split_qkv(h, qkv2_w)
            a1 = jax.nn.softmax(jnp.einsum('bhnd,bhmd->bhnm', q1, k1) * scale, axis=-1)
            a2 = jax.nn.softmax(jnp.einsum('bhnd,bhmd->bhnm', q2, k2) * scale, axis=-1)
            lam = lam1 - lam2 + LAMBDA_INIT
            diff = a1 - lam * a2
            o = jnp.einsum('bhnm,bhmd->bhnd', diff, v1)
            o = o.transpose(0, 2, 1, 3).reshape(Bx, Nx, Cx)
            o = _rmsnorm(o, rms_w)
            attn_out = o @ proj_w.T + proj_b
            x = x + attn_out
            h2 = _layernorm(x, ln2_w, ln2_b)
            mlp = jax.nn.gelu(h2 @ fc1_w.T + fc1_b, approximate=False) @ fc2_w.T + fc2_b
            return x + mlp
        key = jax.random.key(seed)
        ks = jax.random.split(key, 8)
        s = 0.02
        lam2_init = 1.0 - LAMBDA_INIT * ((LAYER_IDX + 1) / MAX_LAYER)
        return {'x': jax.random.normal(ks[0], (B, N, D), dtype=jnp.float32), 'xpos': jax.random.randint(ks[1], (B, N), 0, N), 'ln1_w': jnp.ones((D,), jnp.float32), 'ln1_b': jnp.zeros((D,), jnp.float32), 'qkv1_w': jax.random.normal(ks[2], (3 * D, D), dtype=jnp.float32) * s, 'qkv2_w': jax.random.normal(ks[3], (3 * D, D), dtype=jnp.float32) * s, 'proj_w': jax.random.normal(ks[4], (D, D), dtype=jnp.float32) * s, 'proj_b': jnp.zeros((D,), jnp.float32), 'rms_w': jnp.ones((D,), jnp.float32), 'lam1': jnp.ones((1, H, 1, 1), jnp.float32), 'lam2': jnp.full((1, H, 1, 1), lam2_init, jnp.float32), 'ln2_w': jnp.ones((D,), jnp.float32), 'ln2_b': jnp.zeros((D,), jnp.float32), 'fc1_w': jax.random.normal(ks[5], (MLP, D), dtype=jnp.float32) * s, 'fc1_b': jnp.zeros((MLP,), jnp.float32), 'fc2_w': jax.random.normal(ks[6], (D, MLP), dtype=jnp.float32) * s, 'fc2_b': jnp.zeros((D,), jnp.float32)}
    _L0_attn_all = _L0_attn_setup()
    _L0_attn_in = {k: v for k, v in _L0_attn_all.items() if k in ('xpos', 'ln1_w', 'ln1_b', 'qkv1_w', 'qkv2_w', 'proj_w', 'proj_b', 'rms_w', 'lam1', 'lam2', 'ln2_w', 'ln2_b', 'fc1_w', 'fc1_b', 'fc2_w', 'fc2_b')}
    del _L0_attn_all

    def _L0_ffn_setup():
        import jax, jax.numpy as jnp
        import numpy as np
        H = 192
        R = 64
        E = 8
        B, S = (8, 512)
        key = jax.random.key(seed)
        ks = jax.random.split(key, 10)
        s_in = 1.0 / np.sqrt(H)
        s_r = 1.0 / np.sqrt(R)
        return {'x': jax.random.normal(ks[0], (B, S, H), dtype=jnp.float32), 'enc_w': jax.random.uniform(ks[1], (H, R), jnp.float32, -s_in, s_in), 'enc_b': jax.random.uniform(ks[2], (R,), jnp.float32, -s_in, s_in), 'sw_w': jax.random.uniform(ks[3], (R, E), jnp.float32, -s_r, s_r), 'sw_b': jax.random.uniform(ks[4], (E,), jnp.float32, -s_r, s_r), 'w1': jax.random.uniform(ks[5], (E, H, R), jnp.float32, -s_in, s_in), 'b1': jax.random.uniform(ks[6], (E, R), jnp.float32, -s_in, s_in), 'w2': jax.random.uniform(ks[7], (E, R, H), jnp.float32, -s_r, s_r), 'b2': jax.random.uniform(ks[8], (E, H), jnp.float32, -s_r, s_r)}
    _L0_ffn_all = _L0_ffn_setup()
    _L0_ffn_in = {k: v for k, v in _L0_ffn_all.items() if k in ('enc_w', 'enc_b', 'sw_w', 'sw_b', 'w1', 'b1', 'w2', 'b2')}
    del _L0_ffn_all
    return {'x': x, 'L0_tok_emb': _L0_tok_in['emb'], 'L0_tok_norm_w': _L0_tok_in['norm_w'], 'L0_tok_in_proj_w': _L0_tok_in['in_proj_w'], 'L0_tok_conv_w': _L0_tok_in['conv_w'], 'L0_tok_conv_b': _L0_tok_in['conv_b'], 'L0_tok_x_proj_w': _L0_tok_in['x_proj_w'], 'L0_tok_dt_proj_w': _L0_tok_in['dt_proj_w'], 'L0_tok_dt_proj_b': _L0_tok_in['dt_proj_b'], 'L0_tok_A_log': _L0_tok_in['A_log'], 'L0_tok_D': _L0_tok_in['D'], 'L0_tok_out_proj_w': _L0_tok_in['out_proj_w'], 'L0_attn_xpos': _L0_attn_in['xpos'], 'L0_attn_ln1_w': _L0_attn_in['ln1_w'], 'L0_attn_ln1_b': _L0_attn_in['ln1_b'], 'L0_attn_qkv1_w': _L0_attn_in['qkv1_w'], 'L0_attn_qkv2_w': _L0_attn_in['qkv2_w'], 'L0_attn_proj_w': _L0_attn_in['proj_w'], 'L0_attn_proj_b': _L0_attn_in['proj_b'], 'L0_attn_rms_w': _L0_attn_in['rms_w'], 'L0_attn_lam1': _L0_attn_in['lam1'], 'L0_attn_lam2': _L0_attn_in['lam2'], 'L0_attn_ln2_w': _L0_attn_in['ln2_w'], 'L0_attn_ln2_b': _L0_attn_in['ln2_b'], 'L0_attn_fc1_w': _L0_attn_in['fc1_w'], 'L0_attn_fc1_b': _L0_attn_in['fc1_b'], 'L0_attn_fc2_w': _L0_attn_in['fc2_w'], 'L0_attn_fc2_b': _L0_attn_in['fc2_b'], 'L0_ffn_enc_w': _L0_ffn_in['enc_w'], 'L0_ffn_enc_b': _L0_ffn_in['enc_b'], 'L0_ffn_sw_w': _L0_ffn_in['sw_w'], 'L0_ffn_sw_b': _L0_ffn_in['sw_b'], 'L0_ffn_w1': _L0_ffn_in['w1'], 'L0_ffn_b1': _L0_ffn_in['b1'], 'L0_ffn_w2': _L0_ffn_in['w2'], 'L0_ffn_b2': _L0_ffn_in['b2']}

def reference(x, L0_tok_emb, L0_tok_norm_w, L0_tok_in_proj_w, L0_tok_conv_w, L0_tok_conv_b, L0_tok_x_proj_w, L0_tok_dt_proj_w, L0_tok_dt_proj_b, L0_tok_A_log, L0_tok_D, L0_tok_out_proj_w, L0_attn_xpos, L0_attn_ln1_w, L0_attn_ln1_b, L0_attn_qkv1_w, L0_attn_qkv2_w, L0_attn_proj_w, L0_attn_proj_b, L0_attn_rms_w, L0_attn_lam1, L0_attn_lam2, L0_attn_ln2_w, L0_attn_ln2_b, L0_attn_fc1_w, L0_attn_fc1_b, L0_attn_fc2_w, L0_attn_fc2_b, L0_ffn_enc_w, L0_ffn_enc_b, L0_ffn_sw_w, L0_ffn_sw_b, L0_ffn_w1, L0_ffn_b1, L0_ffn_w2, L0_ffn_b2):
    import jax
    import jax.numpy as jnp

    def _L0_tok_ref(input_ids, emb, norm_w, in_proj_w, conv_w, conv_b, x_proj_w, dt_proj_w, dt_proj_b, A_log, D, out_proj_w):
        import jax, jax.numpy as jnp
        import numpy as np
        B, L, V, D_MODEL = (1, 512, 8000, 192)
        N_LAYER, D_STATE, EXPAND, D_CONV = (2, 16, 2, 4)
        D_INNER = EXPAND * D_MODEL
        DT_RANK = -(-D_MODEL // D_STATE)
        EPS = 1e-05

        def _rmsnorm(x, w):
            return x * jax.lax.rsqrt(jnp.mean(x * x, axis=-1, keepdims=True) + EPS) * w

        def _selective_scan(u, delta, A, Bm, Cm, D):
            deltaA = jnp.exp(delta[..., None] * A)
            dBu = delta[..., None] * Bm[:, :, None, :] * u[..., None]

            def comb(c1, c2):
                a1, b1 = c1
                a2, b2 = c2
                return (a2 * a1, a2 * b1 + b2)
            _, h = jax.lax.associative_scan(comb, (deltaA, dBu), axis=1)
            y = jnp.einsum('bldn,bln->bld', h, Cm)
            return y + u * D

        def _mamba_block(x, in_proj_w, conv_w, conv_b, x_proj_w, dt_proj_w, dt_proj_b, A_log, D, out_proj_w):
            xz = x @ in_proj_w
            xr, res = jnp.split(xz, 2, axis=-1)
            xc = jax.lax.conv_general_dilated(jnp.swapaxes(xr, 1, 2), conv_w, (1,), [(D_CONV - 1, 0)], feature_group_count=D_INNER, dimension_numbers=('NCH', 'OIH', 'NCH'))
            xr = jax.nn.silu(jnp.swapaxes(xc + conv_b[:, None], 1, 2))
            A = -jnp.exp(A_log)
            x_dbl = xr @ x_proj_w
            dt, Bm, Cm = jnp.split(x_dbl, [DT_RANK, DT_RANK + D_STATE], axis=-1)
            delta = jax.nn.softplus(dt @ dt_proj_w + dt_proj_b)
            y = _selective_scan(xr, delta, A, Bm, Cm, D)
            return y * jax.nn.silu(res) @ out_proj_w
        x = emb[input_ids]
        for i in range(N_LAYER):
            x = x + _mamba_block(_rmsnorm(x, norm_w[i]), in_proj_w[i], conv_w[i], conv_b[i], x_proj_w[i], dt_proj_w[i], dt_proj_b[i], A_log[i], D[i], out_proj_w[i])
        return x

    def _L0_attn_ref(x, xpos, ln1_w, ln1_b, qkv1_w, qkv2_w, proj_w, proj_b, rms_w, lam1, lam2, ln2_w, ln2_b, fc1_w, fc1_b, fc2_w, fc2_b):
        import jax, jax.numpy as jnp
        import numpy as np
        B, N, D, H = (4, 256, 192, 12)
        HD = D // H
        MLP = 4 * D
        LAMBDA_INIT = 0.1
        LAYER_IDX, MAX_LAYER = (0, 12)

        def _layernorm(x, w, b, eps=1e-05):
            m = x.mean(-1, keepdims=True)
            v = ((x - m) ** 2).mean(-1, keepdims=True)
            return (x - m) * jax.lax.rsqrt(v + eps) * w + b

        def _rmsnorm(x, w, eps=1e-06):
            return x * jax.lax.rsqrt((x * x).mean(-1, keepdims=True) + eps) * w

        def _split_qkv(h, w):
            qkv = (h @ w.T).reshape(h.shape[0], h.shape[1], 3, H, HD)
            qkv = qkv.transpose(2, 0, 3, 1, 4)
            return (qkv[0], qkv[1], qkv[2])

        def _diff_block(x, ln1_w, ln1_b, qkv1_w, qkv2_w, proj_w, proj_b, rms_w, lam1, lam2, ln2_w, ln2_b, fc1_w, fc1_b, fc2_w, fc2_b):
            Bx, Nx, Cx = x.shape
            scale = HD ** (-0.5)
            h = _layernorm(x, ln1_w, ln1_b)
            q1, k1, v1 = _split_qkv(h, qkv1_w)
            q2, k2, _ = _split_qkv(h, qkv2_w)
            a1 = jax.nn.softmax(jnp.einsum('bhnd,bhmd->bhnm', q1, k1) * scale, axis=-1)
            a2 = jax.nn.softmax(jnp.einsum('bhnd,bhmd->bhnm', q2, k2) * scale, axis=-1)
            lam = lam1 - lam2 + LAMBDA_INIT
            diff = a1 - lam * a2
            o = jnp.einsum('bhnm,bhmd->bhnd', diff, v1)
            o = o.transpose(0, 2, 1, 3).reshape(Bx, Nx, Cx)
            o = _rmsnorm(o, rms_w)
            attn_out = o @ proj_w.T + proj_b
            x = x + attn_out
            h2 = _layernorm(x, ln2_w, ln2_b)
            mlp = jax.nn.gelu(h2 @ fc1_w.T + fc1_b, approximate=False) @ fc2_w.T + fc2_b
            return x + mlp
        del xpos
        return _diff_block(x, ln1_w, ln1_b, qkv1_w, qkv2_w, proj_w, proj_b, rms_w, lam1, lam2, ln2_w, ln2_b, fc1_w, fc1_b, fc2_w, fc2_b)

    def _L0_ffn_ref(x, enc_w, enc_b, sw_w, sw_b, w1, b1, w2, b2):
        import jax, jax.numpy as jnp
        import numpy as np
        H = 192
        R = 64
        E = 8
        B, S = (8, 512)
        b, s, d = x.shape
        xt = x.reshape(-1, d)
        x_enc = xt @ enc_w + enc_b
        route_prob = jax.nn.softmax(x_enc @ sw_w + sw_b, axis=-1)
        route_prob_max = jnp.max(route_prob, axis=-1)
        routes = jnp.argmax(route_prob, axis=-1)
        onehot = jax.nn.one_hot(routes, E, dtype=xt.dtype)
        h = jnp.einsum('td,edr->ter', xt, w1) + b1[None]
        h = jax.nn.gelu(h, approximate=False)
        h = h * onehot[..., None]
        out = jnp.einsum('ter,erd->td', h, w2) + onehot @ b2
        out = out * route_prob_max[:, None]
        return out.reshape(b, s, d)
    h = _L0_tok_ref(x, L0_tok_emb, L0_tok_norm_w, L0_tok_in_proj_w, L0_tok_conv_w, L0_tok_conv_b, L0_tok_x_proj_w, L0_tok_dt_proj_w, L0_tok_dt_proj_b, L0_tok_A_log, L0_tok_D, L0_tok_out_proj_w)
    h = h + _L0_attn_ref(_layernorm(h, axis=-1), L0_attn_xpos, L0_attn_ln1_w, L0_attn_ln1_b, L0_attn_qkv1_w, L0_attn_qkv2_w, L0_attn_proj_w, L0_attn_proj_b, L0_attn_rms_w, L0_attn_lam1, L0_attn_lam2, L0_attn_ln2_w, L0_attn_ln2_b, L0_attn_fc1_w, L0_attn_fc1_b, L0_attn_fc2_w, L0_attn_fc2_b)
    h = h + _L0_ffn_ref(_layernorm(h, axis=-1), L0_ffn_enc_w, L0_ffn_enc_b, L0_ffn_sw_w, L0_ffn_sw_b, L0_ffn_w1, L0_ffn_b1, L0_ffn_w2, L0_ffn_b2)
    return h

_drawn_inputs = setup_inputs


def setup_inputs(seed=0):
    import zlib

    import numpy as np

    out = dict(_drawn_inputs(seed))
    spreads = {'L0_tok_norm_w': (1.0, 0.2),
     'L0_tok_conv_b': (0.0, 0.1),
     'L0_tok_D': (1.0, 0.2),
     'L0_attn_ln1_w': (1.0, 0.2),
     'L0_attn_ln1_b': (0.0, 0.1),
     'L0_attn_proj_b': (0.0, 0.1),
     'L0_attn_rms_w': (1.0, 0.2),
     'L0_attn_lam1': (1.0, 0.2),
     'L0_attn_lam2': (0.9916666746139526, 0.2),
     'L0_attn_ln2_w': (1.0, 0.577),
     'L0_attn_ln2_b': (0.0, 0.425),
     'L0_attn_fc1_b': (0.0, 0.1),
     'L0_attn_fc2_b': (0.0, 0.1)}
    factors = {'L0_tok_x_proj_w': 8.0,
     'L0_tok_dt_proj_w': 200.0,
     'L0_tok_dt_proj_b': 200.0,
     'L0_tok_A_log': 200.0,
     'L0_attn_qkv2_w': 7.49,
     'L0_ffn_enc_b': 3.87,
     'L0_ffn_b1': 24.936,
     'L0_ffn_b2': 4.947}
    for name, (base, spread) in spreads.items():
        noise = np.random.default_rng([zlib.crc32(name.encode()), seed]).standard_normal(out[name].shape)
        drawn = base * np.exp(spread * noise) if base else spread * noise
        out[name] = jnp.asarray(drawn.astype(out[name].dtype))
    for name, factor in factors.items():
        out[name] = (out[name] * factor).astype(out[name].dtype)
    return out
```

```python
from contextlib import ExitStack

import concourse.bass as bass
from concourse import mybir

F32 = mybir.dt.float32
BF16 = mybir.dt.bfloat16
I32 = mybir.dt.int32
ACT = mybir.ActivationFunctionType
ALU = mybir.AluOpType
AX = mybir.AxisListType

P = 128
SEQS, L = 128, 128
G = 4
GROUPS = SEQS // G
T = G * L
V, DM, DI, NS, RANK = 8000, 192, 384, 16, 12
LAYERS, TAPS = 2, 4
KC, KN = 96, 2
CN = DI // P
PAD = TAPS - 1
BCR = 2 * NS
XROWS = 3 * BCR + RANK
DT0 = 3 * BCR
H, HD = 12, 16
FC = 4 * DM // P
EX, ER = 8, 64
EC = EX * ER // P
BANK = 512
HEAD_SLOTS = H * 2
BATCH = 6
OW = HD + 1
SLOTS = LAYERS * NS
RING = 3
LOG_MAX = 78.0
DELTA_MIN = 1.2e-32

STEP_STATS, STEP_NORM, STEP_LN1, STEP_QK, STEP_V, STEP_HEADS = 0, 1, 2, 3, 6, 7
STEP_RMS = STEP_HEADS + HEAD_SLOTS + 3
STEP_OT = STEP_RMS + 1
STEP_PROJ = STEP_OT + 1
STEP_LN2 = STEP_PROJ + 1
STEP_FC1 = STEP_LN2 + 1
STEP_FC2 = STEP_FC1 + 3
STEP_XT = STEP_FC2 + 1
STEP_ENC = STEP_XT + 1
STEP_LOGITS = STEP_ENC + 1
STEP_ROUTE = STEP_LOGITS + 1
STEP_EXPERTS = STEP_ROUTE + 1
STEP_OUT = STEP_EXPERTS + EC
STEPS = STEP_OUT + 1
STEPS_OF_SLOT = [range(s * STEPS // SLOTS, (s + 1) * STEPS // SLOTS) for s in range(SLOTS)]

VEC = {}
for _name, _width in (("dt_b", LAYERS * CN), ("conv_w", LAYERS * CN * TAPS), ("conv_b", LAYERS * CN), ("D", LAYERS * CN),
                      ("A_log", LAYERS * CN * NS), ("lam1", H), ("lam2", H), ("fc1_b", FC), ("proj_b", DM),
                      ("fc2_b", DM), ("enc_b", 1), ("b1", EC), ("rank", EX)):
    VEC[_name] = (sum(w for _, w in VEC.values()), _width)
VEC_W = sum(w for _, w in VEC.values())
MVEC = {n: KN * i for i, n in enumerate(("norm0", "norm1", "ln1_w", "ln1_b", "rms_w", "ln2_w", "ln2_b"))}

WEIGHTS = {
    "w_in": (0, KC, LAYERS * KN * 2 * DI), "w_x": (0, P, LAYERS * CN * XROWS), "w_dt": (DT0, RANK, LAYERS * DI),
    "w_out": (0, P, LAYERS * CN * DM), "w_qk": (0, KC, KN * 3 * 3 * P), "w_v": (0, KC, KN * DM),
    "w_proj": (0, KC, KN * DM), "w_fc1": (0, KC, KN * 4 * DM), "w_fc2": (0, P, FC * DM), "w_enc": (0, KC, KN * ER),
    "w_sw": (0, ER + 1, EX), "w_1": (0, KC, KN * EX * ER), "w_2": (0, P, EC * DM), "b_2": (0, P, DM),
    "ident": (0, P, P), "vec": (0, P, VEC_W), "mvec": (0, KC, KN * len(MVEC)),
}
SELECTORS = {"sel_bc": (0, 3 * BCR, BCR * P), "sel_ex": (0, P, EC * P)}


def build(nc, ids, emb_rows, weights, out):
    with ExitStack() as ctx:
        def sb(name, shape, dt=F32):
            return ctx.enter_context(nc.sbuf_tensor(name, shape, dt))

        def sem(name):
            return ctx.enter_context(nc.semaphore(name))

        w = {}
        for name, (p0, rows, cols) in {**WEIGHTS, **SELECTORS}.items():
            w[name] = sb(name, [P if p0 else rows, cols], BF16 if name in SELECTORS else F32)
        w_in = w["w_in"][:, :].rearrange("p (l k n) -> p l k n", l=LAYERS, k=KN)
        w_x = w["w_x"][:, :].rearrange("p (l c n) -> p l c n", l=LAYERS, c=CN)
        w_dt = w["w_dt"][:, :].rearrange("p (l n) -> p l n", l=LAYERS)
        w_out = w["w_out"][:, :].rearrange("p (l c n) -> p l c n", l=LAYERS, c=CN)
        w_qk = w["w_qk"][:, :].rearrange("p (k j n) -> p k j n", k=KN, j=9)
        w_v = w["w_v"][:, :].rearrange("p (k n) -> p k n", k=KN)
        w_proj = w["w_proj"][:, :].rearrange("p (k n) -> p k n", k=KN)
        w_fc1 = w["w_fc1"][:, :].rearrange("p (k n) -> p k n", k=KN)
        w_fc2 = w["w_fc2"][:, :].rearrange("p (j n) -> p j n", j=FC)
        w_enc = w["w_enc"][:, :].rearrange("p (k n) -> p k n", k=KN)
        w_1 = w["w_1"][:, :].rearrange("p (k n) -> p k n", k=KN)
        w_2 = w["w_2"][:, :].rearrange("p (j n) -> p j n", j=EC)
        sel_bc = w["sel_bc"][:, :].rearrange("p (n m) -> p n m", n=BCR)
        sel_ex = w["sel_ex"][:, :].rearrange("p (j m) -> p j m", j=EC)
        ident = w["ident"][:, :]

        def vec(name, i=0, n=1):
            at = VEC[name][0] + i
            return w["vec"][:, at:at + n]

        def mvec(name, k):
            at = MVEC[name] + k
            return w["mvec"][:, at:at + 1]

        diag_d = sb("diag_d", [P, LAYERS, CN, P])
        decay_rate = sb("decay_rate", [P, LAYERS * CN * NS])
        neg_lam = sb("neg_lam", [P, H])
        eps5 = sb("eps5", [P, 1])
        eps6 = sb("eps6", [P, 1])

        spare = sb("spare", [P, 2])

        ids_raw = sb("ids_raw", [P, SEQS], I32)
        ids_neg = sb("ids_neg", [P, SEQS], I32)
        ids_ok = sb("ids_ok", [P, SEQS], I32)
        ids_now = sb("ids_now", [P, G], I32)

        emb = sb("emb", [P, G, DM])
        mid = sb("mid", [P, G, DM])
        mamba_out = sb("mamba_out", [P, G, DM])
        square = sb("square", [P, DM])
        ssq = sb("ssq", [P, G])
        lnv = sb("lnv", [P, G])
        rstd = sb("rstd", [P, G])
        xn = sb("xn", [P, G, DM])
        xnT = sb("xnT", [KC, KN, T])
        xr_pad = sb("xr_pad", [P, CN, G, PAD + L])
        xs = sb("xs", [P, CN, T])
        gate = sb("gate", [P, CN, T])
        dt_in = sb("dt_in", [P, T])
        bc_rest = dt_in[0:3 * BCR, :]
        bc_parts = sb("bc_parts", [3 * BCR, T], BF16)
        bc_mid = sb("bc_mid", [3 * BCR, T], BF16)
        delta = sb("delta", [P, CN, T])
        delta_x = sb("delta_x", [P, CN, T])
        decay = sb("decay", [P, 2, CN, T])
        state = sb("state", [P, RING, CN, T])
        z_abs, z_pos, z_exp, z_log = state[:, 0], state[:, 1], state[:, 2], state[:, 0]

        stats = sb("stats", [P, G, 6])
        mv = sb("mv", [P, G, 2])
        a_ln = sb("a_ln", [P, G])
        a_rstd = sb("a_rstd", [P, G])
        a_ssq = sb("a_ssq", [P, G])
        x_a = sb("x_a", [P, G, DM])
        x_2 = sb("x_2", [P, G, DM])
        h_3 = sb("h_3", [P, G, DM])
        normed = sb("normed", [P, G, DM])
        hT = sb("hT", [KC, KN, T])
        q_sb = sb("q_sb", [P, 3, T])
        k_sb = sb("k_sb", [P, 3, G, 2, L])
        v_sb = sb("v_sb", [P, G, H, OW])
        top = sb("top", [P, 2, 4])
        probs = sb("probs", [P, 2, 4 * L])
        probsT = sb("probsT", [P, 2, 4 * L])
        o_scale = sb("o_scale", [P, 2 * BATCH, 2])
        o_parts = sb("o_parts", [P, 2 * BATCH, 2, HD])
        o_sb = sb("o_sb", [P, G, H, HD])
        a_sq = sb("a_sq", [P, DM])
        hidden = k_sb[:, :, :, :, :].rearrange("p j s t m -> p (j s t m)").rearrange("p (j t) -> p j t", t=T)
        enc = sb("enc", [ER + 1, T])
        gmax = sb("gmax", [P, G])
        gsub = sb("gsub", [P, G, EX])
        gexp = sb("gexp", [P, G, EX])
        gsum = sb("gsum", [P, G])
        gprob = sb("gprob", [P, G])
        gmask = sb("gmask", [P, G, EX])
        gcand = sb("gcand", [P, G, EX])
        gbest = sb("gbest", [P, G])
        onehot = sb("onehot", [P, G, P])
        onehotT = q_sb[:, 0, :]
        onehotTb = q_sb[:, 1, 0:T // 2].bitcast(BF16)
        result = o_sb[:, :, :, :].rearrange("p s h d -> p s (h d)")

        mb = ctx.enter_context(nc.psum_tensor("mb", [P, 5, BANK], F32))
        ab = ctx.enter_context(nc.psum_tensor("ab", [P, 3, BANK], F32))
        BANK_B, BANK_C = 3, 4

        loaded = sem("loaded")
        ids_loaded = sem("ids_loaded")
        ids_steps = sem("ids_steps")
        constants = sem("constants")
        zeroed = sem("zeroed")
        eps_set = sem("eps_set")
        rate_held = sem("rate_held")
        rate_exp = sem("rate_exp")
        ids_picked = sem("ids_picked")
        embedded = sem("embedded")
        ssq_done = sem("ssq_done")
        rms_log = sem("rms_log")
        rms_done = sem("rms_done")
        xn_ready = sem("xn_ready")
        xnT_ready = sem("xnT_ready")
        xnT_in = sem("xnT_in")
        xr_ready = sem("xr_ready")
        xr_padded = sem("xr_padded")
        tap_last = sem("tap_last")
        taps_done = sem("taps_done")
        res_ready = sem("res_ready")
        gate_ready = sem("gate_ready")
        xs_ready = sem("xs_ready")
        xdbl_ready = sem("xdbl_ready")
        bc_high = sem("bc_high")
        dt_ready = sem("dt_ready")
        bc_steps = sem("bc_steps")
        z_ready = sem("z_ready")
        z_taken = sem("z_taken")
        z_exped = sem("z_exped")
        z_logged = sem("z_logged")
        delta_steps = sem("delta_steps")
        b_ready = sem("b_ready")
        c_ready = sem("c_ready")
        y_added = sem("y_added")
        decayed = sem("decayed")
        driven = sem("driven")
        scanned = sem("scanned")
        read_out = sem("read_out")
        gated = sem("gated")
        mixed = sem("mixed")
        layer_done = sem("layer_done")

        stats_done = sem("stats_done")
        stats_part = sem("stats_part")
        var_log = sem("var_log")
        var_done = sem("var_done")
        x_ready = sem("x_ready")
        ln_ready = sem("ln_ready")
        hT_ready = sem("hT_ready")
        hT_in = sem("hT_in")
        bias_added = sem("bias_added")
        qk_ready = sem("qk_ready")
        qk_in = sem("qk_in")
        v_ready = sem("v_ready")
        v_in = sem("v_in")
        scored = sem("scored")
        top_found = sem("top_found")
        shifted = sem("shifted")
        exped = sem("exped")
        turned = sem("turned")
        turned_in = sem("turned_in")
        weighted = sem("weighted")
        o_steps = sem("o_steps")
        o_ssq = sem("o_ssq")
        o_log = sem("o_log")
        o_rstd = sem("o_rstd")
        o_normed = sem("o_normed")
        proj_ready = sem("proj_ready")
        x2_ready = sem("x2_ready")
        res_steps = sem("res_steps")
        fc1_ready = sem("fc1_ready")
        gelu_done = sem("gelu_done")
        fc2_ready = sem("fc2_ready")
        h3_ready = sem("h3_ready")
        enc_ready = sem("enc_ready")
        enc_in = sem("enc_in")
        logits_ready = sem("logits_ready")
        gate_shift = sem("gate_shift")
        gate_exp = sem("gate_exp")
        route_steps = sem("route_steps")
        onehot_ready = sem("onehot_ready")
        turned_hot = sem("turned_hot")
        hot_in = sem("hot_in")
        ex_ready = sem("ex_ready")
        ex_gelu = sem("ex_gelu")
        ex_masked = sem("ex_masked")
        out_ready = sem("out_ready")
        result_ready = sem("result_ready")
        stored = sem("stored")

        NW = 16 * (len(WEIGHTS) + len(SELECTORS))

        def norm_src(layer):
            return emb if layer == 0 else mid

        block = ctx.enter_context(nc.Block())

        @block.sync
        def _(sp):
            sp.dma_start(ids_raw[:, :], ids).then_inc(ids_loaded, 16)
            for name, (p0, rows, _cols) in {**WEIGHTS, **SELECTORS}.items():
                sp.dma_start(w[name][p0:p0 + rows, :], weights[name]).then_inc(loaded, 16)

            with sp.Fori(0, GROUPS, 1) as g:
                sp.wait_ge(result_ready, g + 1)
                sp.dma_start(out[bass.ds(g, 1)].rearrange("a p s d -> p (a s) d"), result[:, :, :]).then_inc(stored, 16)
            sp.wait_ge(stored, 16 * GROUPS)

        @block.gpsimd
        def _(pool):
            nc.gpsimd.memset(xr_pad[:, :, :, 0:PAD], 0.0)
            for i in range(2):
                nc.gpsimd.memset(decay[:, i].rearrange("p c (s t) -> p (c s) t", s=G)[:, :, 0:1], 0.0)
            nc.gpsimd.memset(v_sb[:, :, :, HD:OW], 1.0)
            nc.gpsimd.memset(onehot[:, :, :], 0.0).then_inc(zeroed, 1)

            def gather(g):
                pool.wait_ge(ids_steps, 4)
                if isinstance(g, int):
                    nc.gpsimd.tensor_copy(ids_now[:, :], ids_ok[:, G * g:G * g + G]).then_inc(ids_picked, 1)
                else:
                    nc.gpsimd.tensor_copy(ids_now[:, :], ids_ok[:, bass.ds(G * g, G)]).then_inc(ids_picked, 1)
                pool.wait_ge(ids_picked, g + 1)
                nc.gpsimd.tensor_tensor(spare[:, 1:2], eps5[:, :], eps5[:, :], ALU.add)
                for s in range(G):
                    nc.gpsimd.indirect_dma_start(
                        out=emb[:, s, :], out_offset=None, in_=emb_rows,
                        in_offset=bass.IndirectOffsetOnAxis(ap=ids_now[:, s:s + 1], axis=0),
                    ).then_inc(embedded, 16)

            def attention(a, step):
                if step == STEP_NORM:
                    pool.wait_ge(x_ready, a + 1)
                    bias = vec("proj_b", 0, DM).unsqueeze(1).to_broadcast([P, G, DM])
                    nc.gpsimd.tensor_tensor(x_2[:, :, :], x_a[:, :, :], bias, ALU.add).then_inc(bias_added, 1)
                if step == STEP_LN2:
                    pool.wait_ge(x2_ready, a + 1)
                    nc.gpsimd.tensor_tensor(h_3[:, :, :], x_2[:, :, :], mamba_out[:, :, :], ALU.add).then_inc(res_steps, 1)
                    pool.wait_ge(res_steps, 2 * a + 1)
                    bias = vec("fc2_b", 0, DM).unsqueeze(1).to_broadcast([P, G, DM])
                    nc.gpsimd.tensor_tensor(h_3[:, :, :], h_3[:, :, :], bias, ALU.add).then_inc(res_steps, 1)

            pool.wait_ge(loaded, NW)
            pool.wait_ge(eps_set, 1)
            gather(0)
            pool.wait_ge(layer_done, 1)
            gather(1)
            with pool.Fori(1, GROUPS - 1, 1) as g:
                for slot in range(NS):
                    for step in STEPS_OF_SLOT[slot]:
                        attention(g - 1, step)
                pool.wait_ge(layer_done, 2 * g + 1)
                gather(g + 1)
                for slot in range(NS, SLOTS):
                    for step in STEPS_OF_SLOT[slot]:
                        attention(g - 1, step)
            for a in (GROUPS - 2, GROUPS - 1):
                for step in range(STEPS):
                    attention(a, step)

        @block.tensor
        def _(pe):
            pe.wait_ge(loaded, NW)

            def mamba_front(g, l):
                n = 2 * g + l
                src = xn
                pe.wait_ge(xn_ready, n + 1)
                for k in range(KN):
                    for s in range(G):
                        ins = nc.tensor.transpose(mb[0:KC, BANK_B + k, s * L:(s + 1) * L],
                                                  src[:, s, k * KC:(k + 1) * KC], ident)
                    ins.then_inc(xnT_ready, 1)
                pe.wait_ge(xnT_in, KN * n + KN)
                for c in range(CN):
                    for k in range(KN):
                        ins = nc.tensor.matmul(mb[:, c, :], w_in[:, l, k, c * P:(c + 1) * P], xnT[:, k, :],
                                               start=(k == 0), stop=(k == KN - 1))
                    ins.then_inc(xr_ready, 1)
                for c, bank in enumerate((BANK_B, BANK_C, 0)):
                    if bank == 0:
                        pe.wait_ge(tap_last, CN * n + 1)
                    for k in range(KN):
                        ins = nc.tensor.matmul(mb[:, bank, :], w_in[:, l, k, DI + c * P:DI + (c + 1) * P], xnT[:, k, :],
                                               start=(k == 0), stop=(k == KN - 1))
                    ins.then_inc(res_ready, 1)
                pe.wait_ge(tap_last, CN * n + 2)
                for c in range(CN):
                    pe.wait_ge(xs_ready, CN * n + c + 1)
                    ins = nc.tensor.matmul(mb[0:XROWS, 1, :], w_x[:, l, c, :], xs[:, c, :], start=(c == 0), stop=(c == CN - 1))
                ins.then_inc(xdbl_ready, 1)
                pe.wait_ge(dt_ready, n + 1)
                pe.wait_ge(gate_ready, CN * n + CN)
                pe.wait_ge(bc_steps, 5 * n + 1)
                for c, bank in enumerate((2, 0, 1)):
                    ins = nc.tensor.matmul(mb[:, bank, :], w_dt[DT0:DT0 + RANK, l, c * P:(c + 1) * P],
                                           dt_in[DT0:DT0 + RANK, :], start=True, stop=True)
                    ins.then_inc(z_ready, 1)

            def send_b(g, l, i):
                n = 2 * g + l
                if i:
                    pe.wait_ge(driven, NS * n + i)
                nc.tensor.matmul(mb[:, BANK_B, :], sel_bc[:, i, :], bc_parts[:, :], start=True, stop=True).then_inc(b_ready, 1)

            def send_c(g, l, i):
                n = 2 * g + l
                if i:
                    pe.wait_ge(read_out, NS * n + i)
                nc.tensor.matmul(mb[:, BANK_C, :], sel_bc[:, NS + i, :], bc_parts[:, :], start=True, stop=True).then_inc(c_ready, 1)

            def add_y(g, l, i):
                n = 2 * g + l
                pe.wait_ge(read_out, NS * n + i + 1)
                for c in range(CN):
                    ins = nc.tensor.matmul(mb[:, c, :], ident, state[:, i % RING, c, :], start=False, stop=(i == NS - 1))
                ins.then_inc(y_added, 1)

            def mamba(g, l, aside):
                n = 2 * g + l
                mamba_front(g, l)
                pe.wait_ge(bc_steps, 5 * n + 5)
                send_b(g, l, 0)
                send_c(g, l, 0)
                pe.wait_ge(z_taken, CN * n + CN)
                for c in range(CN):
                    nc.tensor.matmul(mb[:, c, :], diag_d[:, l, c, :], xs[:, c, :], start=True, stop=False)
                for i in range(NS):
                    if i + 1 < NS:
                        send_b(g, l, i + 1)
                    aside(l * NS + i)
                    add_y(g, l, i)
                    if i + 1 < NS:
                        send_c(g, l, i + 1)
                pe.wait_ge(gated, n + 1)
                for s in range(G):
                    for c in range(CN):
                        ins = nc.tensor.matmul(mb[:, BANK_B + s // 2, (s % 2) * DM:(s % 2 + 1) * DM],
                                               gate[:, c, s * L:(s + 1) * L], w_out[:, l, c, :],
                                               start=(c == 0), stop=(c == CN - 1))
                ins.then_inc(mixed, 1)

            def turn(src, count):
                for k in range(KN):
                    for s in range(G):
                        ins = nc.tensor.transpose(ab[0:KC, k, s * L:(s + 1) * L], src[:, s, k * KC:(k + 1) * KC], ident)
                    ins.then_inc(hT_ready, 1)

            def attention(a, step):
                if step == STEP_LN1:
                    pe.wait_ge(ln_ready, 3 * a + 1)
                    if not isinstance(a, int) or a:
                        pe.wait_ge(result_ready, a)
                    turn(normed, 0)
                for j in range(9):
                    if step == STEP_QK + j // 3:
                        if j == 0:
                            pe.wait_ge(hT_in, 4 * KN * a + KN)
                        if j >= 3:
                            pe.wait_ge(qk_in, 9 * a + j - 2)
                        for k in range(KN):
                            ins = nc.tensor.matmul(ab[:, (j + 2) % 3, :], w_qk[:, k, j, :], hT[:, k, :],
                                                   start=(k == 0), stop=(k == KN - 1))
                        ins.then_inc(qk_ready, 1)
                if step == STEP_V:
                    pe.wait_ge(qk_in, 9 * a + 9)
                    for s in range(G):
                        for k in range(KN):
                            ins = nc.tensor.matmul(ab[:, 1 + s // 2, (s % 2) * DM:(s % 2 + 1) * DM],
                                                   hT[:, k, s * L:(s + 1) * L], w_v[:, k, :], start=(k == 0), stop=(k == KN - 1))
                    ins.then_inc(v_ready, 1)
                slot = step - STEP_HEADS
                if 0 <= slot < HEAD_SLOTS:
                    h, u = slot // 2, slot % 2
                    j, r = h // 4, 32 * (h % 4)
                    if slot == 0:
                        pe.wait_ge(v_in, a + 1)
                    else:
                        pe.wait_ge(shifted, HEAD_SLOTS * a + slot)
                    for i in range(2):
                        s = 2 * u + i
                        ins = nc.tensor.matmul(ab[:, 0, i * 2 * L:(i + 1) * 2 * L], q_sb[r:r + 32, j, s * L:(s + 1) * L],
                                               k_sb[r:r + 32, j, s, :, :].rearrange("p t m -> p (t m)"), start=True, stop=True)
                    ins.then_inc(scored, 1)
                if 0 <= slot - 1 < HEAD_SLOTS:
                    t = slot - 1
                    pe.wait_ge(exped, HEAD_SLOTS * a + t + 1)
                    if t:
                        pe.wait_ge(turned_in, HEAD_SLOTS * a + t)
                    for q in range(4):
                        ins = nc.tensor.transpose(ab[:, 1, q * L:(q + 1) * L], probs[:, t % 2, q * L:(q + 1) * L], ident)
                    ins.then_inc(turned, 1)
                if 0 <= slot - 2 < HEAD_SLOTS:
                    t = slot - 2
                    h, u = t // 2, t % 2
                    pe.wait_ge(turned_in, HEAD_SLOTS * a + t + 1)
                    if t % BATCH == 0 and t:
                        pe.wait_ge(o_steps, 16 * a + 4 * (t // BATCH) - 1)
                    for q in range(4):
                        at = ((t % BATCH) * 4 + q) * OW
                        ins = nc.tensor.matmul(ab[:, 2, at:at + OW], probsT[:, t % 2, q * L:(q + 1) * L],
                                               v_sb[:, 2 * u + q // 2, h, :], start=True, stop=True)
                    ins.then_inc(weighted, 1)
                if step == STEP_OT:
                    pe.wait_ge(o_normed, a + 1)
                    turn(normed, 1)
                if step == STEP_PROJ:
                    pe.wait_ge(hT_in, 4 * KN * a + 2 * KN)
                    for s in range(G):
                        for k in range(KN):
                            ins = nc.tensor.matmul(ab[:, 1 + s // 2, (s % 2) * DM:(s % 2 + 1) * DM],
                                                   hT[:, k, s * L:(s + 1) * L], w_proj[:, k, :], start=(k == 0), stop=(k == KN - 1))
                    ins.then_inc(proj_ready, 1)
                if step == STEP_LN2:
                    pe.wait_ge(ln_ready, 3 * a + 2)
                    turn(normed, 2)
                for j in range(FC):
                    if step == STEP_FC1 + j // 2:
                        if j == 0:
                            pe.wait_ge(hT_in, 4 * KN * a + 3 * KN)
                        if j >= 3:
                            pe.wait_ge(gelu_done, FC * a + j - 2)
                        for k in range(KN):
                            ins = nc.tensor.matmul(ab[:, (j + 2) % 3, :], w_fc1[:, k, j * P:(j + 1) * P], hT[:, k, :],
                                                   start=(k == 0), stop=(k == KN - 1))
                        ins.then_inc(fc1_ready, 1)
                if step == STEP_FC2:
                    pe.wait_ge(gelu_done, FC * a + FC)
                    for s in range(G):
                        for j in range(FC):
                            ins = nc.tensor.matmul(ab[:, 1 + s // 2, (s % 2) * DM:(s % 2 + 1) * DM],
                                                   hidden[:, j, s * L:(s + 1) * L], w_fc2[:, j, :], start=(j == 0), stop=(j == FC - 1))
                    ins.then_inc(fc2_ready, 1)
                if step == STEP_XT:
                    pe.wait_ge(ln_ready, 3 * a + 3)
                    turn(normed, 3)
                if step == STEP_ENC:
                    pe.wait_ge(hT_in, 4 * KN * a + 4 * KN)
                    for k in range(KN):
                        ins = nc.tensor.matmul(ab[0:ER, 2, :], w_enc[:, k, :], hT[:, k, :], start=(k == 0), stop=(k == KN - 1))
                    ins.then_inc(enc_ready, 1)
                if step == STEP_LOGITS:
                    pe.wait_ge(enc_in, a + 1)
                    for s in range(G):
                        ins = nc.tensor.matmul(ab[:, 0, s * EX:(s + 1) * EX], enc[:, s * L:(s + 1) * L], w["w_sw"][:, :],
                                               start=True, stop=True)
                    ins.then_inc(logits_ready, 1)
                if step == STEP_ROUTE:
                    pe.wait_ge(onehot_ready, a + 1)
                    for s in range(G):
                        ins = nc.tensor.transpose(ab[:, 1, s * L:(s + 1) * L], onehot[:, s, :], ident)
                    ins.then_inc(turned_hot, 1)
                if 0 <= step - STEP_EXPERTS < EC:
                    j = step - STEP_EXPERTS
                    pe.wait_ge(hot_in, 2 * a + 2)
                    if j:
                        pe.wait_ge(ex_masked, EC * a + j)
                    for k in range(KN):
                        nc.tensor.matmul(ab[:, 0, :], w_1[:, k, j * P:(j + 1) * P], hT[:, k, :], start=(k == 0), stop=(k == KN - 1))
                    nc.tensor.matmul(ab[:, 1, :], sel_ex[:, j, :], onehotTb, start=True, stop=True).then_inc(ex_ready, 1)
                if step == STEP_OUT:
                    pe.wait_ge(ex_masked, EC * a + EC)
                    for s in range(G):
                        for j in range(EC):
                            nc.tensor.matmul(ab[:, 1 + s // 2, (s % 2) * DM:(s % 2 + 1) * DM],
                                             hidden[:, j, s * L:(s + 1) * L], w_2[:, j, :], start=(j == 0), stop=False)
                        ins = nc.tensor.matmul(ab[:, 1 + s // 2, (s % 2) * DM:(s % 2 + 1) * DM],
                                               onehotT[:, s * L:(s + 1) * L], w["b_2"][:, :], start=False, stop=True)
                    ins.then_inc(out_ready, 1)

            pe.wait_ge(constants, 1)
            for l in range(LAYERS):
                mamba(0, l, lambda slot: None)
            with pe.Fori(1, GROUPS, 1) as g:
                def aside(slot):
                    for step in STEPS_OF_SLOT[slot]:
                        attention(g - 1, step)
                for l in range(LAYERS):
                    mamba(g, l, aside)
            for step in range(STEPS):
                attention(GROUPS - 1, step)

        @block.scalar
        def _(act):
            act.wait_ge(loaded, NW)
            act.wait_ge(zeroed, 1)
            act.wait_ge(eps_set, 1)
            act.wait_ge(rate_held, 1)
            nc.scalar.activation(decay_rate[:, :], decay_rate[:, :], ACT.Exp).then_inc(rate_exp, 1)
            act.wait_ge(constants, 1)

            def mamba_front(g, l):
                n = 2 * g + l
                src = norm_src(l)
                if l == 0:
                    act.wait_ge(embedded, 64 * g + 64)
                else:
                    act.wait_ge(layer_done, n)
                for s in range(G):
                    if s:
                        act.wait_ge(ssq_done, G * n + s)
                    elif not isinstance(n, int) or n:
                        act.wait_ge(ssq_done, G * n)
                    nc.scalar.activation(square[:, :], src[:, s, :], ACT.Square, accum_out=ssq[:, s:s + 1]).then_inc(ssq_done, 1)
                act.wait_ge(ssq_done, G * n + G)
                nc.scalar.activation(lnv[:, :], ssq[:, :], ACT.Ln, scale=1.0 / DM, bias=eps5[:, 0:1]).then_inc(rms_log, 1)
                act.wait_ge(rms_log, n + 1)
                nc.scalar.activation(rstd[:, :], lnv[:, :], ACT.Exp, scale=-0.5).then_inc(rms_done, 1)
                for k in range(KN):
                    act.wait_ge(xnT_ready, KN * n + k + 1)
                    nc.scalar.activation(xnT[:, k, :], mb[0:KC, BANK_B + k, :], ACT.Copy,
                                         scale=mvec(f"norm{l}", k)).then_inc(xnT_in, 1)
                for c in range(CN):
                    act.wait_ge(xr_ready, CN * n + c + 1)
                    nc.scalar.activation(xr_pad[:, c, :, PAD:], mb[:, c, :].rearrange("p (s t) -> p s t", s=G),
                                         ACT.Copy).then_inc(xr_padded, 1)
                    i = l * CN + c
                    nc.scalar.activation(xs[:, c, :], mb[:, c, :], ACT.Identity, scale=vec("conv_w", i * TAPS + PAD),
                                         bias=vec("conv_b", i)).then_inc(tap_last, 1)
                for c, bank in enumerate((BANK_B, BANK_C, 0)):
                    act.wait_ge(res_ready, CN * n + c + 1)
                    nc.scalar.activation(gate[:, c, :], mb[:, bank, :], ACT.Silu).then_inc(gate_ready, 1)
                for c in range(CN):
                    act.wait_ge(taps_done, CN * PAD * n + CN * (PAD - 1) + c + 1)
                    nc.scalar.activation(xs[:, c, :], xs[:, c, :], ACT.Silu).then_inc(xs_ready, 1)
                act.wait_ge(xdbl_ready, n + 1)
                nc.scalar.activation(dt_in[DT0:DT0 + RANK, :], mb[DT0:DT0 + RANK, 1, :], ACT.Copy).then_inc(dt_ready, 1)
                nc.scalar.activation(bc_parts[:, :], mb[0:3 * BCR, 1, :], ACT.Copy).then_inc(bc_high, 1)
                for c, bank in enumerate((2, 0, 1)):
                    act.wait_ge(z_ready, CN * n + c + 1)
                    nc.scalar.activation(z_abs[:, c, :], mb[:, bank, :], ACT.Abs, bias=vec("dt_b", l * CN + c))
                    nc.scalar.activation(z_pos[:, c, :], mb[:, bank, :], ACT.Relu, bias=vec("dt_b", l * CN + c)).then_inc(z_taken, 1)
                act.wait_ge(z_taken, CN * n + CN)
                nc.scalar.activation(z_exp, z_abs, ACT.Exp, scale=-1.0).then_inc(z_exped, 1)
                act.wait_ge(z_exped, n + 1)
                nc.scalar.activation(z_log, z_exp, ACT.Ln, bias=1.0).then_inc(z_logged, 1)

            def decay_step(g, l, i):
                n = 2 * g + l
                if i == 0:
                    act.wait_ge(delta_steps, 5 * n + 4)
                if i >= 2:
                    act.wait_ge(scanned, NS * n + i - 1)
                for c in range(CN):
                    at = (l * CN + c) * NS + i
                    ins = nc.scalar.activation(decay[:, i % 2, c, :].rearrange("p (s t) -> p s t", s=G)[:, :, 1:],
                                               delta[:, c, :].rearrange("p (s t) -> p s t", s=G)[:, :, 1:],
                                               ACT.Exp, scale=decay_rate[:, at:at + 1])
                ins.then_inc(decayed, 1)

            def mamba(g, l, aside):
                mamba_front(g, l)
                decay_step(g, l, 0)
                for i in range(NS):
                    if i + 1 < NS:
                        decay_step(g, l, i + 1)
                    aside(l * NS + i)

            def inv_std(a, i):
                act.wait_ge(stats_done, 4 * a + i + 1)
                nc.scalar.activation(a_ln[:, :], mv[:, :, 1], ACT.Ln, bias=eps5[:, 0:1]).then_inc(var_log, 1)
                act.wait_ge(var_log, 4 * a + i + 1)
                nc.scalar.activation(a_rstd[:, :], a_ln[:, :], ACT.Exp, scale=-0.5).then_inc(var_done, 1)

            def take_turned(a, i, weight, bias):
                for k in range(KN):
                    act.wait_ge(hT_ready, 4 * KN * a + KN * i + k + 1)
                    if bias:
                        ins = nc.scalar.activation(hT[:, k, :], ab[0:KC, k, :], ACT.Identity, scale=mvec(weight, k), bias=mvec(bias, k))
                    elif weight:
                        ins = nc.scalar.activation(hT[:, k, :], ab[0:KC, k, :], ACT.Copy, scale=mvec(weight, k))
                    else:
                        ins = nc.scalar.activation(hT[:, k, :], ab[0:KC, k, :], ACT.Copy)
                    ins.then_inc(hT_in, 1)

            def attention(a, step):
                if step == STEP_STATS:
                    inv_std(a, 0)
                if step == STEP_NORM:
                    inv_std(a, 1)
                if step == STEP_LN1:
                    take_turned(a, 0, "ln1_w", "ln1_b")
                for j in range(9):
                    if step == STEP_QK + j // 3:
                        act.wait_ge(qk_ready, 9 * a + j + 1)
                        bank = ab[:, (j + 2) % 3, :]
                        if j < 3:
                            ins = nc.scalar.activation(q_sb[:, j, :], bank, ACT.Copy)
                        else:
                            ins = nc.scalar.activation(k_sb[:, j % 3, :, j // 3 - 1, :], bank.rearrange("p (s m) -> p s m", s=G), ACT.Copy)
                        ins.then_inc(qk_in, 1)
                if step == STEP_V:
                    act.wait_ge(v_ready, a + 1)
                    for i in range(2):
                        ins = nc.scalar.activation(v_sb[:, 2 * i:2 * i + 2, :, 0:HD],
                                                   ab[:, 1 + i, 0:2 * DM].rearrange("p (s h d) -> p s h d", s=2, h=H), ACT.Copy)
                    ins.then_inc(v_in, 1)
                slot = step - STEP_HEADS
                if 0 <= slot - 1 < HEAD_SLOTS:
                    t = slot - 1
                    act.wait_ge(turned, HEAD_SLOTS * a + t + 1)
                    if t >= 2:
                        act.wait_ge(weighted, HEAD_SLOTS * a + t - 1)
                    nc.scalar.activation(probsT[:, t % 2, :], ab[:, 1, :], ACT.Copy).then_inc(turned_in, 1)
                if 0 <= slot < HEAD_SLOTS:
                    act.wait_ge(shifted, HEAD_SLOTS * a + slot + 1)
                    nc.scalar.activation(probs[:, slot % 2, :], probs[:, slot % 2, :], ACT.Exp,
                                         scale=float(HD) ** -0.5).then_inc(exped, 1)
                if step == STEP_RMS:
                    act.wait_ge(o_steps, 16 * a + 16)
                    for s in range(G):
                        if s:
                            act.wait_ge(o_ssq, G * a + s)
                        elif not isinstance(a, int) or a:
                            act.wait_ge(o_ssq, G * a)
                        nc.scalar.activation(a_sq[:, :], o_sb[:, s, :, :].rearrange("p h d -> p (h d)"), ACT.Square,
                                             accum_out=a_ssq[:, s:s + 1]).then_inc(o_ssq, 1)
                    act.wait_ge(o_ssq, G * a + G)
                    nc.scalar.activation(a_ln[:, :], a_ssq[:, :], ACT.Ln, scale=1.0 / DM, bias=eps6[:, 0:1]).then_inc(o_log, 1)
                    act.wait_ge(o_log, a + 1)
                    nc.scalar.activation(a_rstd[:, :], a_ln[:, :], ACT.Exp, scale=-0.5).then_inc(o_rstd, 1)
                if step == STEP_OT:
                    take_turned(a, 1, "rms_w", None)
                if step == STEP_PROJ:
                    inv_std(a, 2)
                if step == STEP_LN2:
                    take_turned(a, 2, "ln2_w", "ln2_b")
                for j in range(FC):
                    if step == STEP_FC1 + j // 2:
                        act.wait_ge(fc1_ready, FC * a + j + 1)
                        nc.scalar.activation(hidden[:, j, :], ab[:, (j + 2) % 3, :], ACT.Gelu, bias=vec("fc1_b", j)).then_inc(gelu_done, 1)
                if step == STEP_FC2:
                    inv_std(a, 3)
                if step == STEP_XT:
                    take_turned(a, 3, None, None)
                if step == STEP_ENC:
                    act.wait_ge(enc_ready, a + 1)
                    nc.scalar.activation(enc[0:ER, :], ab[0:ER, 2, :], ACT.Identity, bias=vec("enc_b")[0:ER, :]).then_inc(enc_in, 1)
                if step == STEP_LOGITS:
                    act.wait_ge(gate_shift, a + 1)
                    nc.scalar.activation(gexp[:, :, :], gsub[:, :, :], ACT.Exp).then_inc(gate_exp, 1)
                if step == STEP_ROUTE:
                    act.wait_ge(turned_hot, a + 1)
                    nc.scalar.activation(onehotT, ab[:, 1, :], ACT.Copy).then_inc(hot_in, 1)
                    nc.scalar.activation(onehotTb, ab[:, 1, :], ACT.Copy).then_inc(hot_in, 1)
                if 0 <= step - STEP_EXPERTS < EC:
                    j = step - STEP_EXPERTS
                    act.wait_ge(ex_ready, EC * a + j + 1)
                    nc.scalar.activation(hidden[:, j, :], ab[:, 0, :], ACT.Gelu, bias=vec("b1", j)).then_inc(ex_gelu, 1)

            for l in range(LAYERS):
                mamba(0, l, lambda slot: None)
            with act.Fori(1, GROUPS, 1) as g:
                def aside(slot):
                    for step in STEPS_OF_SLOT[slot]:
                        attention(g - 1, step)
                for l in range(LAYERS):
                    mamba(g, l, aside)
            for step in range(STEPS):
                attention(GROUPS - 1, step)

        @block.vector
        def _(dve):
            nc.vector.memset(eps5[:, :], 1e-5)
            nc.vector.memset(enc[ER:ER + 1, :], 1.0)
            nc.vector.memset(eps6[:, :], 1e-6).then_inc(eps_set, 1)
            dve.wait_ge(ids_loaded, 16)
            nc.vector.tensor_scalar(ids_neg[:, :], ids_raw[:, :], 0, V, ALU.is_lt, ALU.mult).then_inc(ids_steps, 1)
            dve.wait_ge(ids_steps, 1)
            nc.vector.tensor_tensor(ids_ok[:, :], ids_raw[:, :], ids_neg[:, :], ALU.add).then_inc(ids_steps, 1)
            dve.wait_ge(ids_steps, 2)
            nc.vector.tensor_scalar(ids_ok[:, :], ids_ok[:, :], 0, V - 1, ALU.max, ALU.min).then_inc(ids_steps, 2)
            dve.wait_ge(loaded, NW)
            nc.vector.tensor_scalar(decay_rate[:, :], vec("A_log", 0, LAYERS * CN * NS), LOG_MAX, None, ALU.min).then_inc(rate_held, 1)
            dve.wait_ge(rate_exp, 1)
            nc.vector.tensor_scalar(decay_rate[:, :], decay_rate[:, :], -1.0, None, ALU.mult)
            nc.vector.tensor_tensor(neg_lam[:, :], vec("lam2", 0, H), vec("lam1", 0, H), ALU.subtract)
            for i in range(LAYERS * CN):
                nc.vector.tensor_scalar(diag_d[:, i // CN, i % CN, :], ident, vec("D", i), None, ALU.mult)
            dve.wait_ge(zeroed, 1)
            nc.vector.memset(gbest[:, :], 0.0).then_inc(constants, 1)
            dve.wait_ge(constants, 1)
            nc.vector.tensor_scalar(neg_lam[:, :], neg_lam[:, :], 0.1, None, ALU.subtract).then_inc(constants, 1)

            def mamba_front(g, l):
                n = 2 * g + l
                src = norm_src(l)
                dve.wait_ge(rms_done, n + 1)
                if l:
                    dve.wait_ge(layer_done, n)
                for s in range(G):
                    ins = nc.vector.tensor_scalar(xn[:, s, :], src[:, s, :], rstd[:, s:s + 1], None, ALU.mult)
                ins.then_inc(xn_ready, 1)
                for k in range(PAD):
                    for c in range(CN):
                        if k == 0:
                            dve.wait_ge(tap_last, CN * n + c + 1)
                        else:
                            dve.wait_ge(taps_done, CN * PAD * n + CN * (k - 1) + c + 1)
                        tile = xs[:, c, :].rearrange("p (s t) -> p s t", s=G)
                        nc.vector.scalar_tensor_tensor(tile, xr_pad[:, c, :, k:k + L], vec("conv_w", (l * CN + c) * TAPS + k),
                                                       tile, ALU.mult, ALU.add).then_inc(taps_done, 1)
                dve.wait_ge(bc_high, n + 1)
                nc.vector.tensor_tensor(bc_rest, mb[0:3 * BCR, 1, :], bc_parts[:, :], ALU.subtract).then_inc(bc_steps, 1)
                dve.wait_ge(bc_steps, 5 * n + 1)
                nc.vector.tensor_copy(bc_mid[:, :], bc_rest).then_inc(bc_steps, 1)
                dve.wait_ge(bc_steps, 5 * n + 2)
                nc.vector.tensor_tensor(bc_rest, bc_rest, bc_mid[:, :], ALU.subtract).then_inc(bc_steps, 1)
                nc.vector.tensor_copy(bc_parts[BCR:2 * BCR, :], bc_mid[BCR:2 * BCR, :]).then_inc(bc_steps, 1)
                dve.wait_ge(bc_steps, 5 * n + 3)
                nc.vector.tensor_copy(bc_parts[2 * BCR:3 * BCR, :], bc_rest[2 * BCR:3 * BCR, :]).then_inc(bc_steps, 1)
                dve.wait_ge(z_exped, n + 1)
                nc.vector.tensor_scalar(delta[:, :, :], z_exp, 1.0, 1.0, ALU.add, ALU.subtract).then_inc(delta_steps, 1)
                dve.wait_ge(delta_steps, 5 * n + 1)
                nc.vector.tensor_tensor(delta_x[:, :, :], z_exp, delta[:, :, :], ALU.subtract).then_inc(delta_steps, 1)
                dve.wait_ge(z_logged, n + 1)
                dve.wait_ge(delta_steps, 5 * n + 2)
                nc.vector.scalar_tensor_tensor(delta[:, :, :], z_log, DELTA_MIN, z_pos, ALU.max, ALU.add).then_inc(delta_steps, 1)
                dve.wait_ge(delta_steps, 5 * n + 3)
                nc.vector.tensor_tensor(delta[:, :, :], delta[:, :, :], delta_x[:, :, :], ALU.add).then_inc(delta_steps, 1)
                dve.wait_ge(delta_steps, 5 * n + 4)
                nc.vector.tensor_tensor(delta_x[:, :, :], delta[:, :, :], xs[:, :, :], ALU.mult).then_inc(delta_steps, 1)

            def drive_step(g, l, i):
                n = 2 * g + l
                dve.wait_ge(b_ready, NS * n + i + 1)
                if i == 0:
                    dve.wait_ge(delta_steps, 5 * n + 5)
                if i >= RING:
                    dve.wait_ge(y_added, NS * n + i - RING + 1)
                b = mb[:, BANK_B, :].unsqueeze(1).to_broadcast([P, CN, T])
                nc.vector.tensor_tensor(state[:, i % RING], delta_x[:, :, :], b, ALU.mult).then_inc(driven, 1)

            def mamba(g, l, aside):
                n = 2 * g + l
                mamba_front(g, l)
                drive_step(g, l, 0)
                for i in range(NS):
                    dve.wait_ge(decayed, NS * n + i + 1)
                    dve.wait_ge(driven, NS * n + i + 1)
                    nc.vector.tensor_tensor_scan(state[:, i % RING].rearrange("p c t -> p (c t)"),
                                                 decay[:, i % 2].rearrange("p c t -> p (c t)"),
                                                 state[:, i % RING].rearrange("p c t -> p (c t)"),
                                                 0.0, ALU.mult, ALU.add).then_inc(scanned, 1)
                    if i + 1 < NS:
                        drive_step(g, l, i + 1)
                    dve.wait_ge(scanned, NS * n + i + 1)
                    dve.wait_ge(c_ready, NS * n + i + 1)
                    cc = mb[:, BANK_C, :].unsqueeze(1).to_broadcast([P, CN, T])
                    nc.vector.tensor_tensor(state[:, i % RING], state[:, i % RING], cc, ALU.mult).then_inc(read_out, 1)
                    aside(l * NS + i)
                dve.wait_ge(y_added, NS * n + NS)
                nc.vector.tensor_tensor(gate[:, :, :], mb[:, 0:CN, :], gate[:, :, :], ALU.mult).then_inc(gated, 1)
                dve.wait_ge(mixed, n + 1)
                if l == LAYERS - 1 and (not isinstance(g, int) or g):
                    dve.wait_ge(res_steps, 2 * g)
                dst = (mid if l == 0 else mamba_out)[:, :, :].rearrange("p (b s) d -> p b (s d)", b=2)
                nc.vector.tensor_tensor(dst, norm_src(l)[:, :, :].rearrange("p (b s) d -> p b (s d)", b=2),
                                        mb[:, BANK_B:BANK_C + 1, 0:2 * DM], ALU.add).then_inc(layer_done, 1)

            def measure(a, i, src):
                for s in range(G):
                    ins = nc.vector.bn_stats(stats[:, s, :], src[:, s, :])
                ins.then_inc(stats_part, 1)
                dve.wait_ge(stats_part, 4 * a + i + 1)
                nc.vector.memset(spare[:, 0:1], 0.0)
                for s in range(G):
                    ins = nc.vector.bn_aggr(mv[:, s, :], stats[:, s, :])
                ins.then_inc(stats_done, 1)

            def normalize(a, i, dst, src, done):
                dve.wait_ge(var_done, 4 * a + i + 1)
                for s in range(G):
                    ins = nc.vector.tensor_scalar(dst[:, s, :], src[:, s, :], mv[:, s, 0:1], a_rstd[:, s:s + 1],
                                                  ALU.subtract, ALU.mult)
                ins.then_inc(done, 1)

            def attention(a, step):
                if step == STEP_STATS:
                    dve.wait_ge(layer_done, 2 * a + 2)
                    measure(a, 0, mamba_out)
                if step == STEP_NORM:
                    normalize(a, 0, x_a, mamba_out, x_ready)
                    dve.wait_ge(x_ready, a + 1)
                    measure(a, 1, x_a)
                if step == STEP_LN1:
                    normalize(a, 1, normed, x_a, ln_ready)
                slot = step - STEP_HEADS
                if 0 <= slot < HEAD_SLOTS:
                    dve.wait_ge(scored, HEAD_SLOTS * a + slot + 1)
                    s4 = ab[:, 0, :].rearrange("p (q m) -> p q m", q=4)
                    nc.vector.tensor_reduce(top[:, slot % 2, :], s4, AX.X, ALU.max).then_inc(top_found, 1)
                    dve.wait_ge(top_found, HEAD_SLOTS * a + slot + 1)
                    if slot >= 2:
                        dve.wait_ge(turned, HEAD_SLOTS * a + slot - 1)
                    nc.vector.tensor_tensor(probs[:, slot % 2, :].rearrange("p (q m) -> p q m", q=4), s4,
                                            top[:, slot % 2, :].unsqueeze(2).to_broadcast([P, 4, L]), ALU.subtract).then_inc(shifted, 1)
                t = slot - 3
                if 0 <= t < HEAD_SLOTS and t % BATCH == BATCH - 1:
                    b = t // BATCH
                    hb = BATCH // 2
                    dve.wait_ge(weighted, HEAD_SLOTS * a + t + 1)
                    if b or not isinstance(a, int) or a:
                        dve.wait_ge(o_steps, 16 * a + 4 * b)
                    o = ab[:, 2, 0:4 * BATCH * OW].rearrange("p (n w) -> p n w", w=OW)
                    nc.vector.reciprocal(o_scale[:, :, :].rearrange("p n t -> p (n t)"), o[:, :, HD]).then_inc(o_steps, 1)
                    dve.wait_ge(o_steps, 16 * a + 4 * b + 1)
                    second = o_scale[:, :, 1].rearrange("p (h s) -> p h s", h=hb)
                    nc.vector.tensor_tensor(second, second, neg_lam[:, hb * b:hb * b + hb].unsqueeze(2).to_broadcast([P, hb, G]),
                                            ALU.mult).then_inc(o_steps, 1)
                    dve.wait_ge(o_steps, 16 * a + 4 * b + 2)
                    nc.vector.tensor_tensor(o_parts[:, :, :, :].rearrange("p n t d -> p (n t) d"), o[:, :, 0:HD],
                                            o_scale[:, :, :].rearrange("p n t -> p (n t)").unsqueeze(2).to_broadcast([P, 4 * BATCH, HD]),
                                            ALU.mult).then_inc(o_steps, 1)
                    dve.wait_ge(o_steps, 16 * a + 4 * b + 3)
                    if b == 0 and (not isinstance(a, int) or a):
                        dve.wait_ge(stored, 16 * a)
                    nc.vector.tensor_tensor(o_sb[:, :, hb * b:hb * b + hb, :].rearrange("p s h d -> p h s d"),
                                            o_parts[:, :, 0, :].rearrange("p (h s) d -> p h s d", h=hb),
                                            o_parts[:, :, 1, :].rearrange("p (h s) d -> p h s d", h=hb), ALU.add).then_inc(o_steps, 1)
                if step == STEP_RMS:
                    dve.wait_ge(o_rstd, a + 1)
                    dve.wait_ge(o_steps, 16 * a + 16)
                    for s in range(G):
                        ins = nc.vector.tensor_scalar(normed[:, s, :], o_sb[:, s, :, :].rearrange("p h d -> p (h d)"),
                                                      a_rstd[:, s:s + 1], None, ALU.mult)
                    ins.then_inc(o_normed, 1)
                pair = ab[:, 1:3, 0:2 * DM]
                if step == STEP_PROJ:
                    dve.wait_ge(proj_ready, a + 1)
                    dve.wait_ge(bias_added, a + 1)
                    nc.vector.tensor_tensor(x_2[:, :, :].rearrange("p (b s) d -> p b (s d)", b=2), pair,
                                            x_2[:, :, :].rearrange("p (b s) d -> p b (s d)", b=2), ALU.add).then_inc(x2_ready, 1)
                    dve.wait_ge(x2_ready, a + 1)
                    measure(a, 2, x_2)
                if step == STEP_LN2:
                    normalize(a, 2, normed, x_2, ln_ready)
                if step == STEP_FC2:
                    dve.wait_ge(fc2_ready, a + 1)
                    dve.wait_ge(res_steps, 2 * a + 2)
                    nc.vector.tensor_tensor(h_3[:, :, :].rearrange("p (b s) d -> p b (s d)", b=2), pair,
                                            h_3[:, :, :].rearrange("p (b s) d -> p b (s d)", b=2), ALU.add).then_inc(h3_ready, 1)
                    dve.wait_ge(h3_ready, a + 1)
                    measure(a, 3, h_3)
                if step == STEP_XT:
                    normalize(a, 3, normed, h_3, ln_ready)
                if step == STEP_LOGITS:
                    dve.wait_ge(logits_ready, a + 1)
                    lg = ab[:, 0, 0:G * EX].rearrange("p (s e) -> p s e", s=G)
                    nc.vector.tensor_reduce(gmax[:, :], lg, AX.X, ALU.max).then_inc(route_steps, 1)
                    dve.wait_ge(route_steps, 6 * a + 1)
                    nc.vector.tensor_tensor(gsub[:, :, :], lg, gmax[:, :].unsqueeze(2).to_broadcast([P, G, EX]), ALU.subtract).then_inc(gate_shift, 1)
                    dve.wait_ge(gate_shift, a + 1)
                    rank = vec("rank", 0, EX).unsqueeze(1).to_broadcast([P, G, EX])
                    nc.vector.tensor_scalar(gmask[:, :, :], gsub[:, :, :], 0.0, None, ALU.is_ge).then_inc(route_steps, 1)
                    dve.wait_ge(route_steps, 6 * a + 2)
                    nc.vector.tensor_tensor(gcand[:, :, :], gmask[:, :, :], rank, ALU.mult).then_inc(route_steps, 1)
                    dve.wait_ge(route_steps, 6 * a + 3)
                    nc.vector.tensor_reduce(gbest[:, :], gcand[:, :, :], AX.X, ALU.max).then_inc(route_steps, 1)
                    dve.wait_ge(route_steps, 6 * a + 4)
                    nc.vector.tensor_tensor(onehot[:, :, 0:EX], gcand[:, :, :], gbest[:, :].unsqueeze(2).to_broadcast([P, G, EX]),
                                            ALU.is_equal).then_inc(onehot_ready, 1)
                    dve.wait_ge(gate_exp, a + 1)
                    nc.vector.tensor_reduce(gsum[:, :], gexp[:, :, :], AX.X, ALU.add).then_inc(route_steps, 1)
                    dve.wait_ge(route_steps, 6 * a + 5)
                    nc.vector.reciprocal(gprob[:, :], gsum[:, :]).then_inc(route_steps, 1)
                if 0 <= step - STEP_EXPERTS < EC:
                    j = step - STEP_EXPERTS
                    dve.wait_ge(ex_gelu, EC * a + j + 1)
                    nc.vector.tensor_tensor(hidden[:, j, :], ab[:, 1, :], hidden[:, j, :], ALU.mult).then_inc(ex_masked, 1)
                if step == STEP_OUT:
                    dve.wait_ge(out_ready, a + 1)
                    dve.wait_ge(route_steps, 6 * a + 6)
                    for s in range(G):
                        ins = nc.vector.scalar_tensor_tensor(result[:, s, :], ab[:, 1 + s // 2, (s % 2) * DM:(s % 2 + 1) * DM],
                                                             gprob[:, s:s + 1], h_3[:, s, :], ALU.mult, ALU.add)
                    ins.then_inc(result_ready, 1)

            for l in range(LAYERS):
                mamba(0, l, lambda slot: None)
            with dve.Fori(1, GROUPS, 1) as g:
                def aside(slot):
                    for step in STEPS_OF_SLOT[slot]:
                        attention(g - 1, step)
                for l in range(LAYERS):
                    mamba(g, l, aside)
            for step in range(STEPS):
                attention(GROUPS - 1, step)


def kernel(**inputs):
    import concourse.bacc as bacc
    import ml_dtypes
    import numpy as np
    from concourse.bass_utils import run_bass_kernel_spmd

    x = {k.replace("L0_", ""): np.asarray(v) for k, v in inputs.items()}

    def chunks(a, rows):
        a = a.reshape(a.shape[:-2] + (a.shape[-2] // rows, rows, a.shape[-1]))
        return np.moveaxis(a, -2, 0).reshape(rows, -1)

    def per_channel(a, rows):
        return np.moveaxis(a.reshape(a.shape[:-1] + (a.shape[-1] // rows, rows)), -1, 0).reshape(rows, -1)

    xp = x["tok_x_proj_w"]
    bc = xp[:, :, RANK:]
    q1, k1, v1 = x["attn_qkv1_w"].reshape(3, 3, 4, HD, DM)
    q2, k2, _ = x["attn_qkv2_w"].reshape(3, 3, 4, HD, DM)
    qk = np.zeros((3, 3, 4, 2, HD, DM), np.float32)
    qk[0, :, :, 0], qk[0, :, :, 1] = q1, q2
    qk[1, :, :, 0] = k1
    qk[2, :, :, 1] = k2
    sw = np.concatenate([x["ffn_sw_w"], x["ffn_sw_b"][None]], 0)
    b_2 = np.zeros((P, DM), np.float32)
    b_2[:EX] = x["ffn_b2"]
    enc_b = np.zeros((P, 1), np.float32)
    enc_b[:ER, 0] = x["ffn_enc_b"]
    vectors = {
        "dt_b": per_channel(x["tok_dt_proj_b"], P),
        "conv_w": np.moveaxis(x["tok_conv_w"].reshape(LAYERS, CN, P, TAPS), 2, 0).reshape(P, -1),
        "conv_b": per_channel(x["tok_conv_b"], P), "D": per_channel(x["tok_D"], P),
        "A_log": np.moveaxis(x["tok_A_log"].reshape(LAYERS, CN, P, NS), 2, 0).reshape(P, -1),
        "lam1": np.broadcast_to(x["attn_lam1"].reshape(1, H), (P, H)),
        "lam2": np.broadcast_to(x["attn_lam2"].reshape(1, H), (P, H)),
        "fc1_b": per_channel(x["attn_fc1_b"], P), "proj_b": np.broadcast_to(x["attn_proj_b"], (P, DM)),
        "fc2_b": np.broadcast_to(x["attn_fc2_b"], (P, DM)), "enc_b": enc_b,
        "b1": per_channel(x["ffn_b1"].reshape(-1), P),
        "rank": np.broadcast_to(np.arange(EX, 0, -1, dtype=np.float32), (P, EX)),
    }
    mvectors = {"norm0": x["tok_norm_w"][0], "norm1": x["tok_norm_w"][1], "ln1_w": x["attn_ln1_w"], "ln1_b": x["attn_ln1_b"],
                "rms_w": x["attn_rms_w"], "ln2_w": x["attn_ln2_w"], "ln2_b": x["attn_ln2_b"]}
    sel_bc = np.zeros((3, BCR, BCR, P), ml_dtypes.bfloat16)
    for n in range(BCR):
        sel_bc[:, n, n] = 1
    sel_ex = np.zeros((P, EC, P // ER, ER), ml_dtypes.bfloat16)
    for e in range(EX):
        sel_ex[e, e // (P // ER), e % (P // ER)] = 1
    arrays = {
        "w_in": chunks(x["tok_in_proj_w"], KC), "w_x": chunks(np.concatenate([bc, bc, bc, xp[:, :, :RANK]], -1), P),
        "w_dt": np.moveaxis(x["tok_dt_proj_w"], 1, 0).reshape(RANK, -1), "w_out": chunks(x["tok_out_proj_w"], P),
        "w_qk": chunks(qk.reshape(9 * P, DM).T, KC), "w_v": chunks(v1.reshape(DM, DM).T, KC),
        "w_proj": chunks(x["attn_proj_w"].T, KC), "w_fc1": chunks(x["attn_fc1_w"].T, KC),
        "w_fc2": chunks(x["attn_fc2_w"].T, P), "w_enc": chunks(x["ffn_enc_w"], KC), "w_sw": sw,
        "w_1": chunks(np.moveaxis(x["ffn_w1"], 0, 1).reshape(DM, EX * ER), KC),
        "w_2": chunks(x["ffn_w2"].reshape(EX * ER, DM), P), "b_2": b_2, "ident": np.eye(P, dtype=np.float32),
        "vec": np.concatenate([vectors[n] for n in VEC], 1), "mvec": np.concatenate([per_channel(mvectors[n], KC) for n in MVEC], 1),
        "sel_bc": sel_bc.reshape(3 * BCR, -1), "sel_ex": sel_ex.reshape(P, -1),
    }
    arrays["ids"] = x["x"].T
    arrays["emb_rows"] = x["tok_emb"]
    arrays = {k: np.ascontiguousarray(v) for k, v in arrays.items()}
    nc = bacc.Bacc("TRN2", target_bir_lowering=False, num_devices=1)
    drams = {k: nc.dram_tensor(k + "_dram", v.shape, mybir.dt.from_np(v.dtype), kind="ExternalInput").ap() for k, v in arrays.items()}
    out = nc.dram_tensor("out_dram", (SEQS, L, DM), F32, kind="ExternalOutput").ap()
    build(nc, drams["ids"], drams["emb_rows"], drams, out.rearrange("(g s) p d -> g p s d", s=G))
    r = run_bass_kernel_spmd(nc, [{k + "_dram": v for k, v in arrays.items()}], core_ids=[0])
    return r.results[0]["out_dram"]
```

```python
from contextlib import ExitStack

import concourse.bass as bass
from concourse import mybir

F32 = mybir.dt.float32
BF16 = mybir.dt.bfloat16
I32 = mybir.dt.int32
ACT = mybir.ActivationFunctionType
ALU = mybir.AluOpType
AX = mybir.AxisListType

P = 128
SEQS, L = 128, 128
G = 4
GROUPS = SEQS // G
T = G * L
V, DM, DI, NS, RANK = 8000, 192, 384, 16, 12
LAYERS, TAPS = 2, 4
KC, KN = 96, 2
CN = DI // P
PAD = TAPS - 1
BCR = 2 * NS
XROWS = 3 * BCR + RANK
DT0 = 3 * BCR
H, HD = 12, 16
FC = 4 * DM // P
EX, ER = 8, 64
EC = EX * ER // P
BANK = 512
HEAD_SLOTS = H * 2
BATCH = 6
OW = HD + 1
RING = 3
LOG_MAX = 78.0
DELTA_MIN = 1.2e-32

FRONT_UNITS = 8
SLOT_UNITS = 3
LAYER_UNITS = FRONT_UNITS + SLOT_UNITS * NS
UNITS = LAYERS * LAYER_UNITS
AT_STATS, AT_STD, AT_NORM = (0, 2, 77, 91), (1, 3, 78, 92), (2, 4, 79, 93)
AT_TURN, AT_TAKE = (5, 74, 80, 94), (6, 75, 81, 95)
AT_QK, AT_V = 7, 17
AT_HEADS = 19
HEAD_TURN, HEAD_TAKE, HEAD_OUT, HEAD_SUM = 3, 4, 5, 6
AT_RMS, AT_RMS_NORM = 72, 73
AT_PROJ = 76
AT_FC1, AT_FC2 = 82, 89
AT_ENC, AT_LOGITS = 96, 98
AT_ROUTE_TURN, AT_ROUTE_TAKE, AT_ROUTE_SUM = 100, 101, 101
AT_EXPERTS = 102
AT_OUT = 110

VEC = {}
for _name, _width in (("dt_b", LAYERS * CN), ("conv_w", LAYERS * CN * TAPS), ("conv_b", LAYERS * CN), ("D", LAYERS * CN),
                      ("A_log", LAYERS * CN * NS), ("lam1", H), ("lam2", H), ("fc1_b", FC), ("proj_b", DM),
                      ("fc2_b", DM), ("enc_b", 1), ("b1", EC), ("rank", EX)):
    VEC[_name] = (sum(w for _, w in VEC.values()), _width)
VEC_W = sum(w for _, w in VEC.values())
MVEC = {n: KN * i for i, n in enumerate(("norm0", "norm1", "ln1_w", "ln1_b", "rms_w", "ln2_w", "ln2_b"))}

WEIGHTS = {
    "w_in": (0, KC, LAYERS * KN * 2 * DI), "w_x": (0, P, LAYERS * CN * XROWS), "w_dt": (DT0, RANK, LAYERS * DI),
    "w_out": (0, P, LAYERS * CN * DM), "w_qk": (0, KC, KN * 3 * 3 * P), "w_v": (0, KC, KN * DM),
    "w_proj": (0, KC, KN * DM), "w_fc1": (0, KC, KN * 4 * DM), "w_fc2": (0, P, FC * DM), "w_enc": (0, KC, KN * ER),
    "w_sw": (0, ER + 1, EX), "w_1": (0, KC, KN * EX * ER), "w_2": (0, P, EC * DM), "b_2": (0, P, DM),
    "ident": (0, P, P), "vec": (0, P, VEC_W), "mvec": (0, KC, KN * len(MVEC)),
}
SELECTORS = {"sel_bc": (0, 3 * BCR, BCR * P), "sel_ex": (0, P, EC * P)}


def build(nc, ids, emb_rows, weights, out):
    with ExitStack() as ctx:
        def sb(name, shape, dt=F32):
            return ctx.enter_context(nc.sbuf_tensor(name, shape, dt))

        def sem(name):
            return ctx.enter_context(nc.semaphore(name))

        w = {}
        for name, (p0, rows, cols) in {**WEIGHTS, **SELECTORS}.items():
            w[name] = sb(name, [P if p0 else rows, cols], BF16 if name in SELECTORS else F32)
        w_in = w["w_in"][:, :].rearrange("p (l k n) -> p l k n", l=LAYERS, k=KN)
        w_x = w["w_x"][:, :].rearrange("p (l c n) -> p l c n", l=LAYERS, c=CN)
        w_dt = w["w_dt"][:, :].rearrange("p (l n) -> p l n", l=LAYERS)
        w_out = w["w_out"][:, :].rearrange("p (l c n) -> p l c n", l=LAYERS, c=CN)
        w_qk = w["w_qk"][:, :].rearrange("p (k j n) -> p k j n", k=KN, j=9)
        w_v = w["w_v"][:, :].rearrange("p (k n) -> p k n", k=KN)
        w_proj = w["w_proj"][:, :].rearrange("p (k n) -> p k n", k=KN)
        w_fc1 = w["w_fc1"][:, :].rearrange("p (k n) -> p k n", k=KN)
        w_fc2 = w["w_fc2"][:, :].rearrange("p (j n) -> p j n", j=FC)
        w_enc = w["w_enc"][:, :].rearrange("p (k n) -> p k n", k=KN)
        w_1 = w["w_1"][:, :].rearrange("p (k n) -> p k n", k=KN)
        w_2 = w["w_2"][:, :].rearrange("p (j n) -> p j n", j=EC)
        sel_bc = w["sel_bc"][:, :].rearrange("p (n m) -> p n m", n=BCR)
        sel_ex = w["sel_ex"][:, :].rearrange("p (j m) -> p j m", j=EC)
        ident = w["ident"][:, :]

        def vec(name, i=0, n=1):
            at = VEC[name][0] + i
            return w["vec"][:, at:at + n]

        def mvec(name, k):
            at = MVEC[name] + k
            return w["mvec"][:, at:at + 1]

        diag_d = sb("diag_d", [P, LAYERS, CN, P])
        decay_rate = sb("decay_rate", [P, LAYERS * CN * NS])
        neg_lam = sb("neg_lam", [P, H])
        eps5 = sb("eps5", [P, 1])
        eps6 = sb("eps6", [P, 1])

        spare = sb("spare", [P, 2])

        ids_raw = sb("ids_raw", [P, SEQS], I32)
        ids_neg = sb("ids_neg", [P, SEQS], I32)
        ids_ok = sb("ids_ok", [P, SEQS], I32)
        ids_now = sb("ids_now", [P, G], I32)

        emb = sb("emb", [P, G, DM])
        mid = sb("mid", [P, G, DM])
        mamba_out = sb("mamba_out", [P, G, DM])
        square = sb("square", [P, DM])
        ssq = sb("ssq", [P, G])
        lnv = sb("lnv", [P, G])
        rstd = sb("rstd", [P, G])
        xn = sb("xn", [P, G, DM])
        xnT = sb("xnT", [KC, KN, T])
        xr_pad = sb("xr_pad", [P, CN, G, PAD + L])
        xs = sb("xs", [P, CN, T])
        gate = sb("gate", [P, CN, T])
        dt_in = sb("dt_in", [P, T])
        bc_rest = dt_in[0:3 * BCR, :]
        bc_parts = sb("bc_parts", [3 * BCR, T], BF16)
        bc_mid = sb("bc_mid", [3 * BCR, T], BF16)
        delta = sb("delta", [P, CN, T])
        delta_x = sb("delta_x", [P, CN, T])
        decay = sb("decay", [P, 2, CN, T])
        state = sb("state", [P, RING, CN, T])
        z_abs, z_pos, z_exp, z_log = state[:, 0], state[:, 1], state[:, 2], state[:, 0]

        stats = sb("stats", [P, G, 6])
        mv = sb("mv", [P, G, 2])
        a_ln = sb("a_ln", [P, G])
        a_rstd = sb("a_rstd", [P, G])
        a_ssq = sb("a_ssq", [P, G])
        x_a = sb("x_a", [P, G, DM])
        x_2 = sb("x_2", [P, G, DM])
        h_3 = sb("h_3", [P, G, DM])
        normed = sb("normed", [P, G, DM])
        hT = sb("hT", [KC, KN, T])
        q_sb = sb("q_sb", [P, 3, T])
        k_sb = sb("k_sb", [P, 3, G, 2, L])
        v_sb = sb("v_sb", [P, G, H, OW])
        top = sb("top", [P, 2, 4])
        probs = sb("probs", [P, 2, 4 * L])
        probsT = sb("probsT", [P, 2, 4 * L])
        o_scale = sb("o_scale", [P, 2 * BATCH, 2])
        o_parts = sb("o_parts", [P, 2 * BATCH, 2, HD])
        o_sb = sb("o_sb", [P, G, H, HD])
        a_sq = sb("a_sq", [P, DM])
        hidden = k_sb[:, :, :, :, :].rearrange("p j s t m -> p (j s t m)").rearrange("p (j t) -> p j t", t=T)
        enc = sb("enc", [ER + 1, T])
        gmax = sb("gmax", [P, G])
        gsub = sb("gsub", [P, G, EX])
        gexp = sb("gexp", [P, G, EX])
        gsum = sb("gsum", [P, G])
        gprob = sb("gprob", [P, G])
        gmask = sb("gmask", [P, G, EX])
        gcand = sb("gcand", [P, G, EX])
        gbest = sb("gbest", [P, G])
        onehot = sb("onehot", [P, G, P])
        onehotT = q_sb[:, 0, :]
        onehotTb = q_sb[:, 1, 0:T // 2].bitcast(BF16)
        result = o_sb[:, :, :, :].rearrange("p s h d -> p s (h d)")

        mb = ctx.enter_context(nc.psum_tensor("mb", [P, 5, BANK], F32))
        ab = ctx.enter_context(nc.psum_tensor("ab", [P, 3, BANK], F32))
        BANK_B, BANK_C = 3, 4

        loaded = sem("loaded")
        ids_loaded = sem("ids_loaded")
        ids_steps = sem("ids_steps")
        constants = sem("constants")
        zeroed = sem("zeroed")
        eps_set = sem("eps_set")
        rate_held = sem("rate_held")
        rate_exp = sem("rate_exp")
        ids_picked = sem("ids_picked")
        embedded = sem("embedded")
        ssq_done = sem("ssq_done")
        rms_log = sem("rms_log")
        rms_done = sem("rms_done")
        xn_ready = sem("xn_ready")
        xnT_ready = sem("xnT_ready")
        xnT_in = sem("xnT_in")
        xr_ready = sem("xr_ready")
        xr_padded = sem("xr_padded")
        tap_last = sem("tap_last")
        taps_done = sem("taps_done")
        res_ready = sem("res_ready")
        gate_ready = sem("gate_ready")
        xs_ready = sem("xs_ready")
        xdbl_ready = sem("xdbl_ready")
        bc_high = sem("bc_high")
        dt_ready = sem("dt_ready")
        bc_steps = sem("bc_steps")
        z_ready = sem("z_ready")
        z_taken = sem("z_taken")
        z_exped = sem("z_exped")
        z_logged = sem("z_logged")
        delta_steps = sem("delta_steps")
        b_ready = sem("b_ready")
        c_ready = sem("c_ready")
        y_added = sem("y_added")
        decayed = sem("decayed")
        driven = sem("driven")
        scanned = sem("scanned")
        read_out = sem("read_out")
        gated = sem("gated")
        mixed = sem("mixed")
        layer_done = sem("layer_done")

        stats_done = sem("stats_done")
        stats_part = sem("stats_part")
        var_log = sem("var_log")
        var_done = sem("var_done")
        x_ready = sem("x_ready")
        ln_ready = sem("ln_ready")
        hT_ready = sem("hT_ready")
        hT_in = sem("hT_in")
        bias_added = sem("bias_added")
        qk_ready = sem("qk_ready")
        qk_in = sem("qk_in")
        v_ready = sem("v_ready")
        v_in = sem("v_in")
        scored = sem("scored")
        top_found = sem("top_found")
        exped = sem("exped")
        turned = sem("turned")
        turned_in = sem("turned_in")
        weighted = sem("weighted")
        o_steps = sem("o_steps")
        o_ssq = sem("o_ssq")
        o_log = sem("o_log")
        o_rstd = sem("o_rstd")
        o_normed = sem("o_normed")
        proj_ready = sem("proj_ready")
        x2_ready = sem("x2_ready")
        res_steps = sem("res_steps")
        fc1_ready = sem("fc1_ready")
        gelu_done = sem("gelu_done")
        fc2_ready = sem("fc2_ready")
        h3_ready = sem("h3_ready")
        enc_ready = sem("enc_ready")
        enc_in = sem("enc_in")
        logits_ready = sem("logits_ready")
        gate_shift = sem("gate_shift")
        gate_exp = sem("gate_exp")
        route_steps = sem("route_steps")
        onehot_ready = sem("onehot_ready")
        turned_hot = sem("turned_hot")
        hot_in = sem("hot_in")
        ex_ready = sem("ex_ready")
        ex_gelu = sem("ex_gelu")
        ex_masked = sem("ex_masked")
        out_ready = sem("out_ready")
        result_ready = sem("result_ready")
        stored = sem("stored")

        NW = 16 * (len(WEIGHTS) + len(SELECTORS))

        def norm_src(layer):
            return emb if layer == 0 else mid

        block = ctx.enter_context(nc.Block())

        @block.sync
        def _(sp):
            sp.dma_start(ids_raw[:, :], ids).then_inc(ids_loaded, 16)
            for name, (p0, rows, _cols) in {**WEIGHTS, **SELECTORS}.items():
                sp.dma_start(w[name][p0:p0 + rows, :], weights[name]).then_inc(loaded, 16)

            with sp.Fori(0, GROUPS, 1) as g:
                sp.wait_ge(result_ready, g + 1)
                sp.dma_start(out[bass.ds(g, 1)].rearrange("a p s d -> p (a s) d"), result[:, :, :]).then_inc(stored, 16)
            sp.wait_ge(stored, 16 * GROUPS)

        @block.gpsimd
        def _(pool):
            nc.gpsimd.memset(xr_pad[:, :, :, 0:PAD], 0.0)
            for i in range(2):
                nc.gpsimd.memset(decay[:, i].rearrange("p c (s t) -> p (c s) t", s=G)[:, :, 0:1], 0.0)
            nc.gpsimd.memset(v_sb[:, :, :, HD:OW], 1.0)
            nc.gpsimd.memset(onehot[:, :, :], 0.0).then_inc(zeroed, 1)

            def gather(g):
                pool.wait_ge(ids_steps, 4)
                if isinstance(g, int):
                    nc.gpsimd.tensor_copy(ids_now[:, :], ids_ok[:, G * g:G * g + G]).then_inc(ids_picked, 1)
                else:
                    nc.gpsimd.tensor_copy(ids_now[:, :], ids_ok[:, bass.ds(G * g, G)]).then_inc(ids_picked, 1)
                pool.wait_ge(ids_picked, g + 1)
                nc.gpsimd.tensor_tensor(spare[:, 1:2], eps5[:, :], eps5[:, :], ALU.add)
                for s in range(G):
                    nc.gpsimd.indirect_dma_start(
                        out=emb[:, s, :], out_offset=None, in_=emb_rows,
                        in_offset=bass.IndirectOffsetOnAxis(ap=ids_now[:, s:s + 1], axis=0),
                    ).then_inc(embedded, 16)

            def attention(a, unit):
                if unit == AT_NORM[0] + 1:
                    pool.wait_ge(x_ready, a + 1)
                    bias = vec("proj_b", 0, DM).unsqueeze(1).to_broadcast([P, G, DM])
                    nc.gpsimd.tensor_tensor(x_2[:, :, :], x_a[:, :, :], bias, ALU.add).then_inc(bias_added, 1)
                if unit == AT_STATS[2] + 1:
                    pool.wait_ge(x2_ready, a + 1)
                    nc.gpsimd.tensor_tensor(h_3[:, :, :], x_2[:, :, :], mamba_out[:, :, :], ALU.add).then_inc(res_steps, 1)
                    pool.wait_ge(res_steps, 2 * a + 1)
                    bias = vec("fc2_b", 0, DM).unsqueeze(1).to_broadcast([P, G, DM])
                    nc.gpsimd.tensor_tensor(h_3[:, :, :], h_3[:, :, :], bias, ALU.add).then_inc(res_steps, 1)

            pool.wait_ge(loaded, NW)
            pool.wait_ge(eps_set, 1)
            gather(0)
            pool.wait_ge(layer_done, 1)
            gather(1)
            with pool.Fori(1, GROUPS - 1, 1) as g:
                for unit in range(LAYER_UNITS):
                    attention(g - 1, unit)
                pool.wait_ge(layer_done, 2 * g + 1)
                gather(g + 1)
                for unit in range(LAYER_UNITS, UNITS):
                    attention(g - 1, unit)
            for a in (GROUPS - 2, GROUPS - 1):
                for unit in range(UNITS):
                    attention(a, unit)

        @block.tensor
        def _(pe):
            pe.wait_ge(loaded, NW)

            def mamba_front(g, l, aside):
                n = 2 * g + l
                src = xn
                at = l * LAYER_UNITS
                pe.wait_ge(xn_ready, n + 1)
                for k in range(KN):
                    for s in range(G):
                        ins = nc.tensor.transpose(mb[0:KC, BANK_B + k, s * L:(s + 1) * L],
                                                  src[:, s, k * KC:(k + 1) * KC], ident)
                    ins.then_inc(xnT_ready, 1)
                aside(at)
                pe.wait_ge(xnT_in, KN * n + KN)
                for c in range(CN):
                    for k in range(KN):
                        ins = nc.tensor.matmul(mb[:, c, :], w_in[:, l, k, c * P:(c + 1) * P], xnT[:, k, :],
                                               start=(k == 0), stop=(k == KN - 1))
                    ins.then_inc(xr_ready, 1)
                    aside(at + 1 + c)
                for c, bank in enumerate((BANK_B, BANK_C, 0)):
                    if bank == 0:
                        pe.wait_ge(tap_last, CN * n + 1)
                    for k in range(KN):
                        ins = nc.tensor.matmul(mb[:, bank, :], w_in[:, l, k, DI + c * P:DI + (c + 1) * P], xnT[:, k, :],
                                               start=(k == 0), stop=(k == KN - 1))
                    ins.then_inc(res_ready, 1)
                    aside(at + 4 + c)
                pe.wait_ge(tap_last, CN * n + 2)
                for c in range(CN):
                    pe.wait_ge(xs_ready, CN * n + c + 1)
                    ins = nc.tensor.matmul(mb[0:XROWS, 1, :], w_x[:, l, c, :], xs[:, c, :], start=(c == 0), stop=(c == CN - 1))
                ins.then_inc(xdbl_ready, 1)
                aside(at + 7)
                pe.wait_ge(dt_ready, n + 1)
                pe.wait_ge(gate_ready, CN * n + CN)
                pe.wait_ge(bc_steps, 5 * n + 1)
                for c, bank in enumerate((2, 0, 1)):
                    ins = nc.tensor.matmul(mb[:, bank, :], w_dt[DT0:DT0 + RANK, l, c * P:(c + 1) * P],
                                           dt_in[DT0:DT0 + RANK, :], start=True, stop=True)
                    ins.then_inc(z_ready, 1)

            def send_b(g, l, i):
                n = 2 * g + l
                if i:
                    pe.wait_ge(driven, NS * n + i)
                nc.tensor.matmul(mb[:, BANK_B, :], sel_bc[:, i, :], bc_parts[:, :], start=True, stop=True).then_inc(b_ready, 1)

            def send_c(g, l, i):
                n = 2 * g + l
                if i:
                    pe.wait_ge(read_out, NS * n + i)
                nc.tensor.matmul(mb[:, BANK_C, :], sel_bc[:, NS + i, :], bc_parts[:, :], start=True, stop=True).then_inc(c_ready, 1)

            def add_y(g, l, i):
                n = 2 * g + l
                pe.wait_ge(read_out, NS * n + i + 1)
                for c in range(CN):
                    ins = nc.tensor.matmul(mb[:, c, :], ident, state[:, i % RING, c, :], start=False, stop=(i == NS - 1))
                ins.then_inc(y_added, 1)

            def mamba(g, l, aside):
                n = 2 * g + l
                mamba_front(g, l, aside)
                pe.wait_ge(bc_steps, 5 * n + 5)
                send_b(g, l, 0)
                send_c(g, l, 0)
                pe.wait_ge(z_taken, CN * n + CN)
                for c in range(CN):
                    nc.tensor.matmul(mb[:, c, :], diag_d[:, l, c, :], xs[:, c, :], start=True, stop=False)
                for i in range(NS):
                    at = l * LAYER_UNITS + FRONT_UNITS + SLOT_UNITS * i
                    if i + 1 < NS:
                        send_b(g, l, i + 1)
                    if i:
                        add_y(g, l, i - 1)
                        send_c(g, l, i)
                    for unit in range(at, at + SLOT_UNITS):
                        aside(unit)
                add_y(g, l, NS - 1)
                pe.wait_ge(gated, n + 1)
                for s in range(G):
                    for c in range(CN):
                        ins = nc.tensor.matmul(mb[:, BANK_B + s // 2, (s % 2) * DM:(s % 2 + 1) * DM],
                                               gate[:, c, s * L:(s + 1) * L], w_out[:, l, c, :],
                                               start=(c == 0), stop=(c == CN - 1))
                ins.then_inc(mixed, 1)

            def turn(src, count):
                for k in range(KN):
                    for s in range(G):
                        ins = nc.tensor.transpose(ab[0:KC, k, s * L:(s + 1) * L], src[:, s, k * KC:(k + 1) * KC], ident)
                    ins.then_inc(hT_ready, 1)

            def attention(a, unit):
                if unit == AT_TURN[0]:
                    pe.wait_ge(ln_ready, 3 * a + 1)
                    if not isinstance(a, int) or a:
                        pe.wait_ge(result_ready, a)
                    turn(normed, 0)
                for j in range(9):
                    if unit == AT_QK + j:
                        if j == 0:
                            pe.wait_ge(hT_in, 4 * KN * a + KN)
                        if j >= 3:
                            pe.wait_ge(qk_in, 9 * a + j - 2)
                        for k in range(KN):
                            ins = nc.tensor.matmul(ab[:, (j + 2) % 3, :], w_qk[:, k, j, :], hT[:, k, :],
                                                   start=(k == 0), stop=(k == KN - 1))
                        ins.then_inc(qk_ready, 1)
                if unit == AT_V:
                    pe.wait_ge(qk_in, 9 * a + 9)
                    for s in range(G):
                        for k in range(KN):
                            ins = nc.tensor.matmul(ab[:, 1 + s // 2, (s % 2) * DM:(s % 2 + 1) * DM],
                                                   hT[:, k, s * L:(s + 1) * L], w_v[:, k, :], start=(k == 0), stop=(k == KN - 1))
                    ins.then_inc(v_ready, 1)
                slot, odd = divmod(unit - AT_HEADS, 2)
                if not odd and 0 <= slot < HEAD_SLOTS:
                    h, u = slot // 2, slot % 2
                    j, r = h // 4, 32 * (h % 4)
                    if slot == 0:
                        pe.wait_ge(v_in, a + 1)
                    else:
                        pe.wait_ge(exped, HEAD_SLOTS * a + slot)
                    for i in range(2):
                        s = 2 * u + i
                        ins = nc.tensor.matmul(ab[:, 0, i * 2 * L:(i + 1) * 2 * L], q_sb[r:r + 32, j, s * L:(s + 1) * L],
                                               k_sb[r:r + 32, j, s, :, :].rearrange("p t m -> p (t m)"), start=True, stop=True)
                    ins.then_inc(scored, 1)
                t, odd = divmod(unit - AT_HEADS - HEAD_TURN, 2)
                if not odd and 0 <= t < HEAD_SLOTS:
                    pe.wait_ge(exped, HEAD_SLOTS * a + t + 1)
                    if t:
                        pe.wait_ge(turned_in, HEAD_SLOTS * a + t)
                    for q in range(4):
                        ins = nc.tensor.transpose(ab[:, 1, q * L:(q + 1) * L], probs[:, t % 2, q * L:(q + 1) * L], ident)
                    ins.then_inc(turned, 1)
                t, odd = divmod(unit - AT_HEADS - HEAD_OUT, 2)
                if not odd and 0 <= t < HEAD_SLOTS:
                    h, u = t // 2, t % 2
                    pe.wait_ge(turned_in, HEAD_SLOTS * a + t + 1)
                    if t % BATCH == 0 and t:
                        pe.wait_ge(o_steps, 16 * a + 4 * (t // BATCH) - 1)
                    for q in range(4):
                        at = ((t % BATCH) * 4 + q) * OW
                        ins = nc.tensor.matmul(ab[:, 2, at:at + OW], probsT[:, t % 2, q * L:(q + 1) * L],
                                               v_sb[:, 2 * u + q // 2, h, :], start=True, stop=True)
                    ins.then_inc(weighted, 1)
                if unit == AT_TURN[1]:
                    pe.wait_ge(o_normed, a + 1)
                    turn(normed, 1)
                if unit == AT_PROJ:
                    pe.wait_ge(hT_in, 4 * KN * a + 2 * KN)
                    for s in range(G):
                        for k in range(KN):
                            ins = nc.tensor.matmul(ab[:, 1 + s // 2, (s % 2) * DM:(s % 2 + 1) * DM],
                                                   hT[:, k, s * L:(s + 1) * L], w_proj[:, k, :], start=(k == 0), stop=(k == KN - 1))
                    ins.then_inc(proj_ready, 1)
                if unit == AT_TURN[2]:
                    pe.wait_ge(ln_ready, 3 * a + 2)
                    turn(normed, 2)
                for j in range(FC):
                    if unit == AT_FC1 + j:
                        if j == 0:
                            pe.wait_ge(hT_in, 4 * KN * a + 3 * KN)
                        if j >= 3:
                            pe.wait_ge(gelu_done, FC * a + j - 2)
                        for k in range(KN):
                            ins = nc.tensor.matmul(ab[:, (j + 2) % 3, :], w_fc1[:, k, j * P:(j + 1) * P], hT[:, k, :],
                                                   start=(k == 0), stop=(k == KN - 1))
                        ins.then_inc(fc1_ready, 1)
                if unit in (AT_FC2, AT_FC2 + 1):
                    pe.wait_ge(gelu_done, FC * a + FC)
                    half = unit - AT_FC2
                    for s in (2 * half, 2 * half + 1):
                        for j in range(FC):
                            ins = nc.tensor.matmul(ab[:, 1 + s // 2, (s % 2) * DM:(s % 2 + 1) * DM],
                                                   hidden[:, j, s * L:(s + 1) * L], w_fc2[:, j, :], start=(j == 0), stop=(j == FC - 1))
                    ins.then_inc(fc2_ready, 1)
                if unit == AT_TURN[3]:
                    pe.wait_ge(ln_ready, 3 * a + 3)
                    turn(normed, 3)
                if unit == AT_ENC:
                    pe.wait_ge(hT_in, 4 * KN * a + 4 * KN)
                    for k in range(KN):
                        ins = nc.tensor.matmul(ab[0:ER, 2, :], w_enc[:, k, :], hT[:, k, :], start=(k == 0), stop=(k == KN - 1))
                    ins.then_inc(enc_ready, 1)
                if unit == AT_LOGITS:
                    pe.wait_ge(enc_in, a + 1)
                    for s in range(G):
                        ins = nc.tensor.matmul(ab[:, 0, s * EX:(s + 1) * EX], enc[:, s * L:(s + 1) * L], w["w_sw"][:, :],
                                               start=True, stop=True)
                    ins.then_inc(logits_ready, 1)
                if unit == AT_ROUTE_TURN:
                    pe.wait_ge(onehot_ready, a + 1)
                    for s in range(G):
                        ins = nc.tensor.transpose(ab[:, 1, s * L:(s + 1) * L], onehot[:, s, :], ident)
                    ins.then_inc(turned_hot, 1)
                j, odd = divmod(unit - AT_EXPERTS, 2)
                if not odd and 0 <= j < EC:
                    pe.wait_ge(hot_in, 2 * a + 2)
                    if j:
                        pe.wait_ge(ex_masked, EC * a + j)
                    for k in range(KN):
                        nc.tensor.matmul(ab[:, 0, :], w_1[:, k, j * P:(j + 1) * P], hT[:, k, :], start=(k == 0), stop=(k == KN - 1))
                    nc.tensor.matmul(ab[:, 1, :], sel_ex[:, j, :], onehotTb, start=True, stop=True).then_inc(ex_ready, 1)
                if unit in (AT_OUT, AT_OUT + 1):
                    pe.wait_ge(ex_masked, EC * a + EC)
                    half = unit - AT_OUT
                    for s in (2 * half, 2 * half + 1):
                        for j in range(EC):
                            nc.tensor.matmul(ab[:, 1 + s // 2, (s % 2) * DM:(s % 2 + 1) * DM],
                                             hidden[:, j, s * L:(s + 1) * L], w_2[:, j, :], start=(j == 0), stop=False)
                        ins = nc.tensor.matmul(ab[:, 1 + s // 2, (s % 2) * DM:(s % 2 + 1) * DM],
                                               onehotT[:, s * L:(s + 1) * L], w["b_2"][:, :], start=False, stop=True)
                    ins.then_inc(out_ready, 1)

            pe.wait_ge(constants, 1)
            for l in range(LAYERS):
                mamba(0, l, lambda unit: None)
            with pe.Fori(1, GROUPS, 1) as g:
                def aside(unit):
                    attention(g - 1, unit)

                for l in range(LAYERS):
                    mamba(g, l, aside)
            for unit in range(UNITS):
                attention(GROUPS - 1, unit)

        @block.scalar
        def _(act):
            act.wait_ge(loaded, NW)
            act.wait_ge(zeroed, 1)
            act.wait_ge(eps_set, 1)
            act.wait_ge(rate_held, 1)
            nc.scalar.activation(decay_rate[:, :], decay_rate[:, :], ACT.Exp).then_inc(rate_exp, 1)
            act.wait_ge(constants, 1)

            def mamba_front(g, l, aside):
                n = 2 * g + l
                src = norm_src(l)
                at = l * LAYER_UNITS
                if l == 0:
                    act.wait_ge(embedded, 64 * g + 64)
                else:
                    act.wait_ge(layer_done, n)
                for s in range(G):
                    if s:
                        act.wait_ge(ssq_done, G * n + s)
                    elif not isinstance(n, int) or n:
                        act.wait_ge(ssq_done, G * n)
                    nc.scalar.activation(square[:, :], src[:, s, :], ACT.Square, accum_out=ssq[:, s:s + 1]).then_inc(ssq_done, 1)
                act.wait_ge(ssq_done, G * n + G)
                nc.scalar.activation(lnv[:, :], ssq[:, :], ACT.Ln, scale=1.0 / DM, bias=eps5[:, 0:1]).then_inc(rms_log, 1)
                act.wait_ge(rms_log, n + 1)
                nc.scalar.activation(rstd[:, :], lnv[:, :], ACT.Exp, scale=-0.5).then_inc(rms_done, 1)
                for k in range(KN):
                    act.wait_ge(xnT_ready, KN * n + k + 1)
                    nc.scalar.activation(xnT[:, k, :], mb[0:KC, BANK_B + k, :], ACT.Copy,
                                         scale=mvec(f"norm{l}", k)).then_inc(xnT_in, 1)
                aside(at)
                for c in range(CN):
                    act.wait_ge(xr_ready, CN * n + c + 1)
                    nc.scalar.activation(xr_pad[:, c, :, PAD:], mb[:, c, :].rearrange("p (s t) -> p s t", s=G),
                                         ACT.Copy).then_inc(xr_padded, 1)
                    i = l * CN + c
                    nc.scalar.activation(xs[:, c, :], mb[:, c, :], ACT.Identity, scale=vec("conv_w", i * TAPS + PAD),
                                         bias=vec("conv_b", i)).then_inc(tap_last, 1)
                    aside(at + 1 + c)
                for c, bank in enumerate((BANK_B, BANK_C, 0)):
                    act.wait_ge(res_ready, CN * n + c + 1)
                    nc.scalar.activation(gate[:, c, :], mb[:, bank, :], ACT.Silu).then_inc(gate_ready, 1)
                    if c < CN - 1:
                        aside(at + 4 + c)
                for c in range(CN):
                    act.wait_ge(taps_done, CN * PAD * n + CN * (PAD - 1) + c + 1)
                    nc.scalar.activation(xs[:, c, :], xs[:, c, :], ACT.Silu).then_inc(xs_ready, 1)
                aside(at + 6)
                act.wait_ge(xdbl_ready, n + 1)
                nc.scalar.activation(dt_in[DT0:DT0 + RANK, :], mb[DT0:DT0 + RANK, 1, :], ACT.Copy).then_inc(dt_ready, 1)
                nc.scalar.activation(bc_parts[:, :], mb[0:3 * BCR, 1, :], ACT.Copy).then_inc(bc_high, 1)
                aside(at + 7)
                for c, bank in enumerate((2, 0, 1)):
                    act.wait_ge(z_ready, CN * n + c + 1)
                    nc.scalar.activation(z_abs[:, c, :], mb[:, bank, :], ACT.Abs, bias=vec("dt_b", l * CN + c))
                    nc.scalar.activation(z_pos[:, c, :], mb[:, bank, :], ACT.Relu, bias=vec("dt_b", l * CN + c)).then_inc(z_taken, 1)
                act.wait_ge(z_taken, CN * n + CN)
                nc.scalar.activation(z_exp, z_abs, ACT.Exp, scale=-1.0).then_inc(z_exped, 1)
                act.wait_ge(z_exped, n + 1)
                nc.scalar.activation(z_log, z_exp, ACT.Ln, bias=1.0).then_inc(z_logged, 1)

            def decay_step(g, l, i):
                n = 2 * g + l
                if i == 0:
                    act.wait_ge(delta_steps, 5 * n + 4)
                if i >= 2:
                    act.wait_ge(scanned, NS * n + i - 1)
                for c in range(CN):
                    at = (l * CN + c) * NS + i
                    ins = nc.scalar.activation(decay[:, i % 2, c, :].rearrange("p (s t) -> p s t", s=G)[:, :, 1:],
                                               delta[:, c, :].rearrange("p (s t) -> p s t", s=G)[:, :, 1:],
                                               ACT.Exp, scale=decay_rate[:, at:at + 1])
                ins.then_inc(decayed, 1)

            def mamba(g, l, aside):
                mamba_front(g, l, aside)
                decay_step(g, l, 0)
                for i in range(NS):
                    at = l * LAYER_UNITS + FRONT_UNITS + SLOT_UNITS * i
                    if i + 1 < NS:
                        decay_step(g, l, i + 1)
                    for unit in range(at, at + SLOT_UNITS):
                        aside(unit)

            def inv_std(a, i):
                act.wait_ge(stats_done, 4 * a + i + 1)
                nc.scalar.activation(a_ln[:, :], mv[:, :, 1], ACT.Ln, bias=eps5[:, 0:1]).then_inc(var_log, 1)
                act.wait_ge(var_log, 4 * a + i + 1)
                nc.scalar.activation(a_rstd[:, :], a_ln[:, :], ACT.Exp, scale=-0.5).then_inc(var_done, 1)

            def take_turned(a, i, weight, bias):
                for k in range(KN):
                    act.wait_ge(hT_ready, 4 * KN * a + KN * i + k + 1)
                    if bias:
                        ins = nc.scalar.activation(hT[:, k, :], ab[0:KC, k, :], ACT.Identity, scale=mvec(weight, k), bias=mvec(bias, k))
                    elif weight:
                        ins = nc.scalar.activation(hT[:, k, :], ab[0:KC, k, :], ACT.Copy, scale=mvec(weight, k))
                    else:
                        ins = nc.scalar.activation(hT[:, k, :], ab[0:KC, k, :], ACT.Copy)
                    ins.then_inc(hT_in, 1)

            def attention(a, unit):
                if unit in AT_STD:
                    inv_std(a, AT_STD.index(unit))
                if unit in AT_TAKE:
                    i = AT_TAKE.index(unit)
                    take_turned(a, i, ("ln1_w", "rms_w", "ln2_w", None)[i], ("ln1_b", None, "ln2_b", None)[i])
                for j in range(9):
                    if unit == AT_QK + j + 1:
                        act.wait_ge(qk_ready, 9 * a + j + 1)
                        bank = ab[:, (j + 2) % 3, :]
                        if j < 3:
                            ins = nc.scalar.activation(q_sb[:, j, :], bank, ACT.Copy, scale=float(HD) ** -0.5)
                        else:
                            ins = nc.scalar.activation(k_sb[:, j % 3, :, j // 3 - 1, :], bank.rearrange("p (s m) -> p s m", s=G), ACT.Copy)
                        ins.then_inc(qk_in, 1)
                if unit == AT_V + 1:
                    act.wait_ge(v_ready, a + 1)
                    for i in range(2):
                        ins = nc.scalar.activation(v_sb[:, 2 * i:2 * i + 2, :, 0:HD],
                                                   ab[:, 1 + i, 0:2 * DM].rearrange("p (s h d) -> p s h d", s=2, h=H), ACT.Copy)
                    ins.then_inc(v_in, 1)
                t, odd = divmod(unit - AT_HEADS - HEAD_TAKE, 2)
                if not odd and 0 <= t < HEAD_SLOTS:
                    act.wait_ge(turned, HEAD_SLOTS * a + t + 1)
                    if t >= 2:
                        act.wait_ge(weighted, HEAD_SLOTS * a + t - 1)
                    nc.scalar.activation(probsT[:, t % 2, :], ab[:, 1, :], ACT.Copy).then_inc(turned_in, 1)
                slot, odd = divmod(unit - AT_HEADS - 1, 2)
                if not odd and 0 <= slot < HEAD_SLOTS:
                    act.wait_ge(top_found, HEAD_SLOTS * a + slot + 1)
                    if slot >= 2:
                        act.wait_ge(turned, HEAD_SLOTS * a + slot - 1)
                    for q in range(4):
                        ins = nc.scalar.activation(probs[:, slot % 2, q * L:(q + 1) * L], ab[:, 0, q * L:(q + 1) * L], ACT.Exp,
                                                   bias=top[:, slot % 2, q:q + 1])
                    ins.then_inc(exped, 1)
                if unit == AT_RMS:
                    act.wait_ge(o_steps, 16 * a + 16)
                    for s in range(G):
                        if s:
                            act.wait_ge(o_ssq, G * a + s)
                        elif not isinstance(a, int) or a:
                            act.wait_ge(o_ssq, G * a)
                        nc.scalar.activation(a_sq[:, :], o_sb[:, s, :, :].rearrange("p h d -> p (h d)"), ACT.Square,
                                             accum_out=a_ssq[:, s:s + 1]).then_inc(o_ssq, 1)
                    act.wait_ge(o_ssq, G * a + G)
                    nc.scalar.activation(a_ln[:, :], a_ssq[:, :], ACT.Ln, scale=1.0 / DM, bias=eps6[:, 0:1]).then_inc(o_log, 1)
                    act.wait_ge(o_log, a + 1)
                    nc.scalar.activation(a_rstd[:, :], a_ln[:, :], ACT.Exp, scale=-0.5).then_inc(o_rstd, 1)
                for j in range(FC):
                    if unit == AT_FC1 + j + 1:
                        act.wait_ge(fc1_ready, FC * a + j + 1)
                        nc.scalar.activation(hidden[:, j, :], ab[:, (j + 2) % 3, :], ACT.Gelu, bias=vec("fc1_b", j)).then_inc(gelu_done, 1)
                if unit == AT_ENC + 1:
                    act.wait_ge(enc_ready, a + 1)
                    nc.scalar.activation(enc[0:ER, :], ab[0:ER, 2, :], ACT.Identity, bias=vec("enc_b")[0:ER, :]).then_inc(enc_in, 1)
                if unit == AT_LOGITS + 2:
                    act.wait_ge(gate_shift, a + 1)
                    nc.scalar.activation(gexp[:, :, :], gsub[:, :, :], ACT.Exp).then_inc(gate_exp, 1)
                if unit == AT_ROUTE_TAKE:
                    act.wait_ge(turned_hot, a + 1)
                    nc.scalar.activation(onehotT, ab[:, 1, :], ACT.Copy).then_inc(hot_in, 1)
                    nc.scalar.activation(onehotTb, ab[:, 1, :], ACT.Copy).then_inc(hot_in, 1)
                j, odd = divmod(unit - AT_EXPERTS - 1, 2)
                if not odd and 0 <= j < EC:
                    act.wait_ge(ex_ready, EC * a + j + 1)
                    nc.scalar.activation(hidden[:, j, :], ab[:, 0, :], ACT.Gelu, bias=vec("b1", j)).then_inc(ex_gelu, 1)

            for l in range(LAYERS):
                mamba(0, l, lambda unit: None)
            with act.Fori(1, GROUPS, 1) as g:
                def aside(unit):
                    attention(g - 1, unit)

                for l in range(LAYERS):
                    mamba(g, l, aside)
            for unit in range(UNITS):
                attention(GROUPS - 1, unit)

        @block.vector
        def _(dve):
            nc.vector.memset(eps5[:, :], 1e-5)
            nc.vector.memset(enc[ER:ER + 1, :], 1.0)
            nc.vector.memset(eps6[:, :], 1e-6).then_inc(eps_set, 1)
            dve.wait_ge(ids_loaded, 16)
            nc.vector.tensor_scalar(ids_neg[:, :], ids_raw[:, :], 0, V, ALU.is_lt, ALU.mult).then_inc(ids_steps, 1)
            dve.wait_ge(ids_steps, 1)
            nc.vector.tensor_tensor(ids_ok[:, :], ids_raw[:, :], ids_neg[:, :], ALU.add).then_inc(ids_steps, 1)
            dve.wait_ge(ids_steps, 2)
            nc.vector.tensor_scalar(ids_ok[:, :], ids_ok[:, :], 0, V - 1, ALU.max, ALU.min).then_inc(ids_steps, 2)
            dve.wait_ge(loaded, NW)
            nc.vector.tensor_scalar(decay_rate[:, :], vec("A_log", 0, LAYERS * CN * NS), LOG_MAX, None, ALU.min).then_inc(rate_held, 1)
            dve.wait_ge(rate_exp, 1)
            nc.vector.tensor_scalar(decay_rate[:, :], decay_rate[:, :], -1.0, None, ALU.mult)
            nc.vector.tensor_tensor(neg_lam[:, :], vec("lam2", 0, H), vec("lam1", 0, H), ALU.subtract)
            for i in range(LAYERS * CN):
                nc.vector.tensor_scalar(diag_d[:, i // CN, i % CN, :], ident, vec("D", i), None, ALU.mult)
            dve.wait_ge(zeroed, 1)
            nc.vector.memset(gbest[:, :], 0.0).then_inc(constants, 1)
            dve.wait_ge(constants, 1)
            nc.vector.tensor_scalar(neg_lam[:, :], neg_lam[:, :], 0.1, None, ALU.subtract).then_inc(constants, 1)

            def mamba_front(g, l, aside):
                n = 2 * g + l
                src = norm_src(l)
                at = l * LAYER_UNITS
                dve.wait_ge(rms_done, n + 1)
                if l:
                    dve.wait_ge(layer_done, n)
                for s in range(G):
                    ins = nc.vector.tensor_scalar(xn[:, s, :], src[:, s, :], rstd[:, s:s + 1], None, ALU.mult)
                ins.then_inc(xn_ready, 1)
                aside(at)
                aside(at + 1)
                for k in range(PAD):
                    for c in range(CN):
                        if k == 0:
                            dve.wait_ge(tap_last, CN * n + c + 1)
                        else:
                            dve.wait_ge(taps_done, CN * PAD * n + CN * (k - 1) + c + 1)
                        tile = xs[:, c, :].rearrange("p (s t) -> p s t", s=G)
                        nc.vector.scalar_tensor_tensor(tile, xr_pad[:, c, :, k:k + L], vec("conv_w", (l * CN + c) * TAPS + k),
                                                       tile, ALU.mult, ALU.add).then_inc(taps_done, 1)
                        if k == 0 and c < CN - 1:
                            aside(at + 2 + c)
                for unit in range(at + 4, at + 7):
                    aside(unit)
                dve.wait_ge(bc_high, n + 1)
                nc.vector.tensor_tensor(bc_rest, mb[0:3 * BCR, 1, :], bc_parts[:, :], ALU.subtract).then_inc(bc_steps, 1)
                dve.wait_ge(bc_steps, 5 * n + 1)
                nc.vector.tensor_copy(bc_mid[:, :], bc_rest).then_inc(bc_steps, 1)
                dve.wait_ge(bc_steps, 5 * n + 2)
                nc.vector.tensor_tensor(bc_rest, bc_rest, bc_mid[:, :], ALU.subtract).then_inc(bc_steps, 1)
                nc.vector.tensor_copy(bc_parts[BCR:2 * BCR, :], bc_mid[BCR:2 * BCR, :]).then_inc(bc_steps, 1)
                dve.wait_ge(bc_steps, 5 * n + 3)
                nc.vector.tensor_copy(bc_parts[2 * BCR:3 * BCR, :], bc_rest[2 * BCR:3 * BCR, :]).then_inc(bc_steps, 1)
                aside(at + 7)
                dve.wait_ge(z_exped, n + 1)
                nc.vector.tensor_scalar(delta[:, :, :], z_exp, 1.0, 1.0, ALU.add, ALU.subtract).then_inc(delta_steps, 1)
                dve.wait_ge(delta_steps, 5 * n + 1)
                nc.vector.tensor_tensor(delta_x[:, :, :], z_exp, delta[:, :, :], ALU.subtract).then_inc(delta_steps, 1)
                dve.wait_ge(z_logged, n + 1)
                dve.wait_ge(delta_steps, 5 * n + 2)
                nc.vector.scalar_tensor_tensor(delta[:, :, :], z_log, DELTA_MIN, z_pos, ALU.max, ALU.add).then_inc(delta_steps, 1)
                dve.wait_ge(delta_steps, 5 * n + 3)
                nc.vector.tensor_tensor(delta[:, :, :], delta[:, :, :], delta_x[:, :, :], ALU.add).then_inc(delta_steps, 1)
                dve.wait_ge(delta_steps, 5 * n + 4)
                nc.vector.tensor_tensor(delta_x[:, :, :], delta[:, :, :], xs[:, :, :], ALU.mult).then_inc(delta_steps, 1)

            def drive_step(g, l, i):
                n = 2 * g + l
                dve.wait_ge(b_ready, NS * n + i + 1)
                if i == 0:
                    dve.wait_ge(delta_steps, 5 * n + 5)
                if i >= RING:
                    dve.wait_ge(y_added, NS * n + i - RING + 1)
                b = mb[:, BANK_B, :].unsqueeze(1).to_broadcast([P, CN, T])
                nc.vector.tensor_tensor(state[:, i % RING], delta_x[:, :, :], b, ALU.mult).then_inc(driven, 1)

            def mamba(g, l, aside):
                n = 2 * g + l
                mamba_front(g, l, aside)
                drive_step(g, l, 0)
                for i in range(NS):
                    at = l * LAYER_UNITS + FRONT_UNITS + SLOT_UNITS * i
                    dve.wait_ge(decayed, NS * n + i + 1)
                    dve.wait_ge(driven, NS * n + i + 1)
                    nc.vector.tensor_tensor_scan(state[:, i % RING].rearrange("p c t -> p (c t)"),
                                                 decay[:, i % 2].rearrange("p c t -> p (c t)"),
                                                 state[:, i % RING].rearrange("p c t -> p (c t)"),
                                                 0.0, ALU.mult, ALU.add).then_inc(scanned, 1)
                    aside(at)
                    if i + 1 < NS:
                        drive_step(g, l, i + 1)
                    aside(at + 1)
                    dve.wait_ge(scanned, NS * n + i + 1)
                    dve.wait_ge(c_ready, NS * n + i + 1)
                    cc = mb[:, BANK_C, :].unsqueeze(1).to_broadcast([P, CN, T])
                    nc.vector.tensor_tensor(state[:, i % RING], state[:, i % RING], cc, ALU.mult).then_inc(read_out, 1)
                    aside(at + 2)
                dve.wait_ge(y_added, NS * n + NS)
                nc.vector.tensor_tensor(gate[:, :, :], mb[:, 0:CN, :], gate[:, :, :], ALU.mult).then_inc(gated, 1)
                dve.wait_ge(mixed, n + 1)
                if l == LAYERS - 1 and (not isinstance(g, int) or g):
                    dve.wait_ge(res_steps, 2 * g)
                dst = (mid if l == 0 else mamba_out)[:, :, :].rearrange("p (b s) d -> p b (s d)", b=2)
                nc.vector.tensor_tensor(dst, norm_src(l)[:, :, :].rearrange("p (b s) d -> p b (s d)", b=2),
                                        mb[:, BANK_B:BANK_C + 1, 0:2 * DM], ALU.add).then_inc(layer_done, 1)

            def measure(a, i, src):
                for s in range(G):
                    ins = nc.vector.bn_stats(stats[:, s, :], src[:, s, :])
                ins.then_inc(stats_part, 1)
                dve.wait_ge(stats_part, 4 * a + i + 1)
                nc.vector.memset(spare[:, 0:1], 0.0)
                for s in range(G):
                    ins = nc.vector.bn_aggr(mv[:, s, :], stats[:, s, :])
                ins.then_inc(stats_done, 1)

            def normalize(a, i, dst, src, done):
                dve.wait_ge(var_done, 4 * a + i + 1)
                for s in range(G):
                    ins = nc.vector.tensor_scalar(dst[:, s, :], src[:, s, :], mv[:, s, 0:1], a_rstd[:, s:s + 1],
                                                  ALU.subtract, ALU.mult)
                ins.then_inc(done, 1)

            def attention(a, unit):
                if unit == AT_STATS[0]:
                    dve.wait_ge(layer_done, 2 * a + 2)
                    measure(a, 0, mamba_out)
                if unit == AT_NORM[0]:
                    normalize(a, 0, x_a, mamba_out, x_ready)
                    dve.wait_ge(x_ready, a + 1)
                    measure(a, 1, x_a)
                if unit == AT_NORM[1]:
                    normalize(a, 1, normed, x_a, ln_ready)
                slot, odd = divmod(unit - AT_HEADS - 1, 2)
                if not odd and 0 <= slot < HEAD_SLOTS:
                    dve.wait_ge(scored, HEAD_SLOTS * a + slot + 1)
                    if slot >= 2:
                        dve.wait_ge(exped, HEAD_SLOTS * a + slot - 1)
                    nc.vector.tensor_reduce(top[:, slot % 2, :], ab[:, 0, :].rearrange("p (q m) -> p q m", q=4), AX.X,
                                            ALU.max, negate=True).then_inc(top_found, 1)
                t, odd = divmod(unit - AT_HEADS - HEAD_SUM, 2)
                if not odd and 0 <= t < HEAD_SLOTS and t % BATCH == BATCH - 1:
                    b = t // BATCH
                    hb = BATCH // 2
                    dve.wait_ge(weighted, HEAD_SLOTS * a + t + 1)
                    if b or not isinstance(a, int) or a:
                        dve.wait_ge(o_steps, 16 * a + 4 * b)
                    o = ab[:, 2, 0:4 * BATCH * OW].rearrange("p (n w) -> p n w", w=OW)
                    nc.vector.reciprocal(o_scale[:, :, :].rearrange("p n t -> p (n t)"), o[:, :, HD]).then_inc(o_steps, 1)
                    dve.wait_ge(o_steps, 16 * a + 4 * b + 1)
                    second = o_scale[:, :, 1].rearrange("p (h s) -> p h s", h=hb)
                    nc.vector.tensor_tensor(second, second, neg_lam[:, hb * b:hb * b + hb].unsqueeze(2).to_broadcast([P, hb, G]),
                                            ALU.mult).then_inc(o_steps, 1)
                    dve.wait_ge(o_steps, 16 * a + 4 * b + 2)
                    nc.vector.tensor_tensor(o_parts[:, :, :, :].rearrange("p n t d -> p (n t) d"), o[:, :, 0:HD],
                                            o_scale[:, :, :].rearrange("p n t -> p (n t)").unsqueeze(2).to_broadcast([P, 4 * BATCH, HD]),
                                            ALU.mult).then_inc(o_steps, 1)
                    dve.wait_ge(o_steps, 16 * a + 4 * b + 3)
                    if b == 0 and (not isinstance(a, int) or a):
                        dve.wait_ge(stored, 16 * a)
                    nc.vector.tensor_tensor(o_sb[:, :, hb * b:hb * b + hb, :].rearrange("p s h d -> p h s d"),
                                            o_parts[:, :, 0, :].rearrange("p (h s) d -> p h s d", h=hb),
                                            o_parts[:, :, 1, :].rearrange("p (h s) d -> p h s d", h=hb), ALU.add).then_inc(o_steps, 1)
                if unit == AT_RMS_NORM:
                    dve.wait_ge(o_rstd, a + 1)
                    dve.wait_ge(o_steps, 16 * a + 16)
                    for s in range(G):
                        ins = nc.vector.tensor_scalar(normed[:, s, :], o_sb[:, s, :, :].rearrange("p h d -> p (h d)"),
                                                      a_rstd[:, s:s + 1], None, ALU.mult)
                    ins.then_inc(o_normed, 1)
                pair = ab[:, 1:3, 0:2 * DM]
                if unit == AT_STATS[2]:
                    dve.wait_ge(proj_ready, a + 1)
                    dve.wait_ge(bias_added, a + 1)
                    nc.vector.tensor_tensor(x_2[:, :, :].rearrange("p (b s) d -> p b (s d)", b=2), pair,
                                            x_2[:, :, :].rearrange("p (b s) d -> p b (s d)", b=2), ALU.add).then_inc(x2_ready, 1)
                    dve.wait_ge(x2_ready, a + 1)
                    measure(a, 2, x_2)
                if unit == AT_NORM[2]:
                    normalize(a, 2, normed, x_2, ln_ready)
                if unit == AT_STATS[3]:
                    dve.wait_ge(fc2_ready, 2 * a + 2)
                    dve.wait_ge(res_steps, 2 * a + 2)
                    nc.vector.tensor_tensor(h_3[:, :, :].rearrange("p (b s) d -> p b (s d)", b=2), pair,
                                            h_3[:, :, :].rearrange("p (b s) d -> p b (s d)", b=2), ALU.add).then_inc(h3_ready, 1)
                    dve.wait_ge(h3_ready, a + 1)
                    measure(a, 3, h_3)
                if unit == AT_NORM[3]:
                    normalize(a, 3, normed, h_3, ln_ready)
                if unit == AT_LOGITS + 1:
                    dve.wait_ge(logits_ready, a + 1)
                    lg = ab[:, 0, 0:G * EX].rearrange("p (s e) -> p s e", s=G)
                    nc.vector.tensor_reduce(gmax[:, :], lg, AX.X, ALU.max).then_inc(route_steps, 1)
                    dve.wait_ge(route_steps, 6 * a + 1)
                    nc.vector.tensor_tensor(gsub[:, :, :], lg, gmax[:, :].unsqueeze(2).to_broadcast([P, G, EX]), ALU.subtract).then_inc(gate_shift, 1)
                    dve.wait_ge(gate_shift, a + 1)
                    rank = vec("rank", 0, EX).unsqueeze(1).to_broadcast([P, G, EX])
                    nc.vector.tensor_scalar(gmask[:, :, :], gsub[:, :, :], 0.0, None, ALU.is_ge).then_inc(route_steps, 1)
                    dve.wait_ge(route_steps, 6 * a + 2)
                    nc.vector.tensor_tensor(gcand[:, :, :], gmask[:, :, :], rank, ALU.mult).then_inc(route_steps, 1)
                    dve.wait_ge(route_steps, 6 * a + 3)
                    nc.vector.tensor_reduce(gbest[:, :], gcand[:, :, :], AX.X, ALU.max).then_inc(route_steps, 1)
                    dve.wait_ge(route_steps, 6 * a + 4)
                    nc.vector.tensor_tensor(onehot[:, :, 0:EX], gcand[:, :, :], gbest[:, :].unsqueeze(2).to_broadcast([P, G, EX]),
                                            ALU.is_equal).then_inc(onehot_ready, 1)
                if unit == AT_ROUTE_SUM:
                    dve.wait_ge(gate_exp, a + 1)
                    nc.vector.tensor_reduce(gsum[:, :], gexp[:, :, :], AX.X, ALU.add).then_inc(route_steps, 1)
                    dve.wait_ge(route_steps, 6 * a + 5)
                    nc.vector.reciprocal(gprob[:, :], gsum[:, :]).then_inc(route_steps, 1)
                j, odd = divmod(unit - AT_EXPERTS - 1, 2)
                if not odd and 0 <= j < EC:
                    dve.wait_ge(ex_gelu, EC * a + j + 1)
                    nc.vector.tensor_tensor(hidden[:, j, :], ab[:, 1, :], hidden[:, j, :], ALU.mult).then_inc(ex_masked, 1)
                if unit == AT_OUT + 1:
                    dve.wait_ge(out_ready, 2 * a + 2)
                    dve.wait_ge(route_steps, 6 * a + 6)
                    for s in range(G):
                        ins = nc.vector.scalar_tensor_tensor(result[:, s, :], ab[:, 1 + s // 2, (s % 2) * DM:(s % 2 + 1) * DM],
                                                             gprob[:, s:s + 1], h_3[:, s, :], ALU.mult, ALU.add)
                    ins.then_inc(result_ready, 1)

            for l in range(LAYERS):
                mamba(0, l, lambda unit: None)
            with dve.Fori(1, GROUPS, 1) as g:
                def aside(unit):
                    attention(g - 1, unit)

                for l in range(LAYERS):
                    mamba(g, l, aside)
            for unit in range(UNITS):
                attention(GROUPS - 1, unit)


def kernel(**inputs):
    import concourse.bacc as bacc
    import ml_dtypes
    import numpy as np
    from concourse.bass_utils import run_bass_kernel_spmd

    x = {k.replace("L0_", ""): np.asarray(v) for k, v in inputs.items()}

    def chunks(a, rows):
        a = a.reshape(a.shape[:-2] + (a.shape[-2] // rows, rows, a.shape[-1]))
        return np.moveaxis(a, -2, 0).reshape(rows, -1)

    def per_channel(a, rows):
        return np.moveaxis(a.reshape(a.shape[:-1] + (a.shape[-1] // rows, rows)), -1, 0).reshape(rows, -1)

    xp = x["tok_x_proj_w"]
    bc = xp[:, :, RANK:]
    q1, k1, v1 = x["attn_qkv1_w"].reshape(3, 3, 4, HD, DM)
    q2, k2, _ = x["attn_qkv2_w"].reshape(3, 3, 4, HD, DM)
    qk = np.zeros((3, 3, 4, 2, HD, DM), np.float32)
    qk[0, :, :, 0], qk[0, :, :, 1] = q1, q2
    qk[1, :, :, 0] = k1
    qk[2, :, :, 1] = k2
    sw = np.concatenate([x["ffn_sw_w"], x["ffn_sw_b"][None]], 0)
    b_2 = np.zeros((P, DM), np.float32)
    b_2[:EX] = x["ffn_b2"]
    enc_b = np.zeros((P, 1), np.float32)
    enc_b[:ER, 0] = x["ffn_enc_b"]
    vectors = {
        "dt_b": per_channel(x["tok_dt_proj_b"], P),
        "conv_w": np.moveaxis(x["tok_conv_w"].reshape(LAYERS, CN, P, TAPS), 2, 0).reshape(P, -1),
        "conv_b": per_channel(x["tok_conv_b"], P), "D": per_channel(x["tok_D"], P),
        "A_log": np.moveaxis(x["tok_A_log"].reshape(LAYERS, CN, P, NS), 2, 0).reshape(P, -1),
        "lam1": np.broadcast_to(x["attn_lam1"].reshape(1, H), (P, H)),
        "lam2": np.broadcast_to(x["attn_lam2"].reshape(1, H), (P, H)),
        "fc1_b": per_channel(x["attn_fc1_b"], P), "proj_b": np.broadcast_to(x["attn_proj_b"], (P, DM)),
        "fc2_b": np.broadcast_to(x["attn_fc2_b"], (P, DM)), "enc_b": enc_b,
        "b1": per_channel(x["ffn_b1"].reshape(-1), P),
        "rank": np.broadcast_to(np.arange(EX, 0, -1, dtype=np.float32), (P, EX)),
    }
    mvectors = {"norm0": x["tok_norm_w"][0], "norm1": x["tok_norm_w"][1], "ln1_w": x["attn_ln1_w"], "ln1_b": x["attn_ln1_b"],
                "rms_w": x["attn_rms_w"], "ln2_w": x["attn_ln2_w"], "ln2_b": x["attn_ln2_b"]}
    sel_bc = np.zeros((3, BCR, BCR, P), ml_dtypes.bfloat16)
    for n in range(BCR):
        sel_bc[:, n, n] = 1
    sel_ex = np.zeros((P, EC, P // ER, ER), ml_dtypes.bfloat16)
    for e in range(EX):
        sel_ex[e, e // (P // ER), e % (P // ER)] = 1
    arrays = {
        "w_in": chunks(x["tok_in_proj_w"], KC), "w_x": chunks(np.concatenate([bc, bc, bc, xp[:, :, :RANK]], -1), P),
        "w_dt": np.moveaxis(x["tok_dt_proj_w"], 1, 0).reshape(RANK, -1), "w_out": chunks(x["tok_out_proj_w"], P),
        "w_qk": chunks(qk.reshape(9 * P, DM).T, KC), "w_v": chunks(v1.reshape(DM, DM).T, KC),
        "w_proj": chunks(x["attn_proj_w"].T, KC), "w_fc1": chunks(x["attn_fc1_w"].T, KC),
        "w_fc2": chunks(x["attn_fc2_w"].T, P), "w_enc": chunks(x["ffn_enc_w"], KC), "w_sw": sw,
        "w_1": chunks(np.moveaxis(x["ffn_w1"], 0, 1).reshape(DM, EX * ER), KC),
        "w_2": chunks(x["ffn_w2"].reshape(EX * ER, DM), P), "b_2": b_2, "ident": np.eye(P, dtype=np.float32),
        "vec": np.concatenate([vectors[n] for n in VEC], 1), "mvec": np.concatenate([per_channel(mvectors[n], KC) for n in MVEC], 1),
        "sel_bc": sel_bc.reshape(3 * BCR, -1), "sel_ex": sel_ex.reshape(P, -1),
    }
    arrays["ids"] = x["x"].T
    arrays["emb_rows"] = x["tok_emb"]
    arrays = {k: np.ascontiguousarray(v) for k, v in arrays.items()}
    nc = bacc.Bacc("TRN2", target_bir_lowering=False, num_devices=1)
    drams = {k: nc.dram_tensor(k + "_dram", v.shape, mybir.dt.from_np(v.dtype), kind="ExternalInput").ap() for k, v in arrays.items()}
    out = nc.dram_tensor("out_dram", (SEQS, L, DM), F32, kind="ExternalOutput").ap()
    build(nc, drams["ids"], drams["emb_rows"], drams, out.rearrange("(g s) p d -> g p s d", s=G))
    r = run_bass_kernel_spmd(nc, [{k + "_dram": v for k, v in arrays.items()}], core_ids=[0])
    return r.results[0]["out_dram"]
```

```python
from contextlib import ExitStack

import concourse.bass as bass
from concourse import mybir

F32 = mybir.dt.float32
BF16 = mybir.dt.bfloat16
I32 = mybir.dt.int32
ACT = mybir.ActivationFunctionType
ALU = mybir.AluOpType
AX = mybir.AxisListType

P = 128
SEQS, L = 128, 128
G = 4
GROUPS = SEQS // G
T = G * L
V, DM, DI, NS, RANK = 8000, 192, 384, 16, 12
LAYERS, TAPS = 2, 4
KC, KN = 96, 2
CN = DI // P
PAD = TAPS - 1
BCR = 2 * NS
XROWS = 3 * BCR + RANK
DT0 = 3 * BCR
H, HD = 12, 16
FC = 4 * DM // P
EX, ER = 8, 64
EC = EX * ER // P
BANK = 512
EXP_LOG = "natural_log_exp_and_others"
HEAD_SLOTS = G * H
PAIRS = HEAD_SLOTS // 2
BATCH = 6
BATCHES = HEAD_SLOTS // BATCH
OW = HD + 1
RING = 4
LOG_MAX = 78.0
DELTA_MIN = 1.2e-32

PLACES = 3 * NS
ODD, EVEN = 0, 1
AT_OUT_PROJ = 1
F_AT = (16, 7)
F_STAT, F_NORM, F_TURN = 0, 1, 2
F_XR, F_RES = (4, 6, 8), (9, 11, 13)
F_SILU = 15
F_XPROJ = 16
F_Z = 19
F_SPLIT, F_LOG, F_DELTA = 21, 22, 23
AT_STATS, AT_STD, AT_NORM = (4, 6, 73, 83), (5, 7, 74, 84), (6, 8, 75, 85)
AT_TURN = (9, 71, 76, 86)
AT_QK, AT_V = (10, 11, 12, 13, 14, 15), 16
AT_HEADS = 17
AT_HEADS_TURN, AT_HEADS_OUT = 19, 20
AT_HEADS_SUM = 21
AT_RMS, AT_RMS_NORM = 69, 70
AT_PROJ = 72
AT_FC1 = (77, 78, 79)
AT_FC2 = 81
AT_ENC, AT_LOGITS = 87, 88
AT_ROUTE_TURN, AT_ROUTE_SUM = 89, 90
AT_EXPERTS = (90, 91)
AT_MASKS = (92, 93)
AT_OUT = 94


def head_slot(unit, first):
    slot = unit - first
    return slot if 0 <= slot < HEAD_SLOTS else None


def head_pair(unit, first):
    pair, rest = divmod(unit - first, 2)
    return (pair, pair % H, pair // H * 2) if not rest and 0 <= pair < PAIRS else (None, 0, 0)


VEC = {}
for _name, _width in (("dt_b", LAYERS * CN), ("conv_w", LAYERS * CN * TAPS), ("conv_b", LAYERS * CN), ("D", LAYERS * CN),
                      ("A_log", LAYERS * CN * NS), ("lam1", H), ("lam2", H), ("fc1_b", FC), ("proj_b", DM),
                      ("fc2_b", DM), ("enc_b", 1), ("b1", EC), ("rank", EX), ("set", 2)):
    VEC[_name] = (sum(w for _, w in VEC.values()), _width)
VEC_W = sum(w for _, w in VEC.values())
MVEC = {n: KN * i for i, n in enumerate(("norm0", "norm1", "ln1_w", "ln1_b", "rms_w", "ln2_w", "ln2_b"))}

WEIGHTS = {
    "w_in": (0, KC, LAYERS * KN * 2 * DI), "w_x": (0, P, LAYERS * CN * XROWS), "w_dt": (DT0, RANK, LAYERS * DI),
    "w_out": (0, P, LAYERS * CN * DM), "w_qk": (0, KC, KN * 2 * 3 * P), "w_v": (0, KC, KN * DM),
    "w_proj": (0, KC, KN * DM), "w_fc1": (0, KC, KN * 4 * DM), "w_fc2": (0, P, FC * DM), "w_enc": (0, KC, KN * ER),
    "w_sw": (0, ER + 1, EX), "w_1": (0, KC, KN * EX * ER), "w_2": (0, P, EC * DM), "b_2": (0, EX, DM),
    "ident": (0, P, P), "vec": (0, P, VEC_W), "mvec": (0, KC, KN * len(MVEC)),
}
SELECTORS = {"sel_bc": (0, 3 * BCR, BCR), "sel_ex": (0, EX, EC * P)}


def build(nc, ids, emb_rows, weights, out):
    with ExitStack() as ctx:
        def sb(name, shape, dt=F32):
            return ctx.enter_context(nc.sbuf_tensor(name, shape, dt))

        def sem(name):
            return ctx.enter_context(nc.semaphore(name))

        w = {}
        for name, (p0, rows, cols) in {**WEIGHTS, **SELECTORS}.items():
            w[name] = sb(name, [P if p0 else rows, cols], BF16 if name in SELECTORS else F32)
        w_in = w["w_in"][:, :].rearrange("p (l k n) -> p l k n", l=LAYERS, k=KN)
        w_x = w["w_x"][:, :].rearrange("p (l c n) -> p l c n", l=LAYERS, c=CN)
        w_dt = w["w_dt"][:, :].rearrange("p (l n) -> p l n", l=LAYERS)
        w_out = w["w_out"][:, :].rearrange("p (l c n) -> p l c n", l=LAYERS, c=CN)
        w_qk = w["w_qk"][:, :].rearrange("p (k j n) -> p k j n", k=KN, j=6)
        w_v = w["w_v"][:, :].rearrange("p (k n) -> p k n", k=KN)
        w_proj = w["w_proj"][:, :].rearrange("p (k n) -> p k n", k=KN)
        w_fc1 = w["w_fc1"][:, :].rearrange("p (k n) -> p k n", k=KN)
        w_fc2 = w["w_fc2"][:, :].rearrange("p (j n) -> p j n", j=FC)
        w_enc = w["w_enc"][:, :].rearrange("p (k n) -> p k n", k=KN)
        w_1 = w["w_1"][:, :].rearrange("p (k n) -> p k n", k=KN)
        w_2 = w["w_2"][:, :].rearrange("p (j n) -> p j n", j=EC)
        sel_bc = w["sel_bc"][:, :].unsqueeze(2).to_broadcast([3 * BCR, BCR, P])
        sel_ex = w["sel_ex"][:, :].rearrange("p (j m) -> p j m", j=EC)
        ident = w["ident"][:, :]

        def vec(name, i=0, n=1):
            at = VEC[name][0] + i
            return w["vec"][:, at:at + n]

        def mvec(name, k):
            at = MVEC[name] + k
            return w["mvec"][:, at:at + 1]

        diag_d = sb("diag_d", [P, LAYERS, CN, P])
        decay_rate = sb("decay_rate", [P, LAYERS * CN * NS])
        neg_lam = sb("neg_lam", [P, H])
        eps5 = sb("eps5", [P, 1])
        eps6 = sb("eps6", [P, 1])

        spare = sb("spare", [P, 3])

        ids_raw = sb("ids_raw", [P, SEQS], I32)
        ids_ok = sb("ids_ok", [P, SEQS], I32)
        ids_now = sb("ids_now", [P, G], I32)

        emb = sb("emb", [P, G, DM])
        mid = sb("mid", [P, G, DM])
        mamba_out = sb("mamba_out", [P, G, DM])
        kept = sb("kept", [P, G, DM])
        ssq = sb("ssq", [P, G])
        lnv = sb("lnv", [P, G])
        rstd = sb("rstd", [P, G])
        xnT_dt = sb("xnT_dt", [P, KN, T])
        xnT = xnT_dt[0:KC]
        dt_in = xnT_dt[:, 0, :]
        bc_rest = xnT_dt[0:3 * BCR, 0, :]
        bc_mid = xnT_dt[0:3 * BCR, 1, 0:T // 2].bitcast(BF16)
        xr_pad = sb("xr_pad", [P, CN, G, PAD + L])
        xs = sb("xs", [P, CN, T])
        xn = xs[:, :, :].rearrange("p c t -> p (c t)")[:, 0:G * DM].rearrange("p (s d) -> p s d", s=G)
        gate_2 = sb("gate_2", [P, 2, CN, T])
        bc_parts_2 = sb("bc_parts_2", [3 * BCR, 2, T], BF16)
        delta_2 = sb("delta_2", [P, 2, CN, T])
        delta_x_2 = sb("delta_x_2", [P, 2, CN, T])
        decay = sb("decay", [P, 2, CN, T])
        state = sb("state", [P, RING, CN, T])
        z_tmp = xr_pad[:, :, :, PAD:]

        stats = sb("stats", [P, G, 6])
        mv = sb("mv", [P, G, 2])
        a_ln = sb("a_ln", [P, G])
        a_rstd = sb("a_rstd", [P, G])
        a_ssq = sb("a_ssq", [P, G])
        x_2 = sb("x_2", [P, G, DM])
        x_a = x_2
        h_3 = mamba_out
        normed = sb("normed", [P, G, DM])
        hT = sb("hT", [KC, KN, T])
        q_sb = sb("q_sb", [P, 3, T])
        k_sb = sb("k_sb", [P, 3, G, 2, L])
        v_sb = sb("v_sb", [P, G, H, OW])
        top = sb("top", [P, 2, 4])
        probs = sb("probs", [P, 2, 4 * L])
        probsT = sb("probsT", [P, 2, 2 * L])
        o_raw = sb("o_raw", [P, BATCH, 2, OW])
        o_scale = sb("o_scale", [P, BATCH, 2])
        o_parts = normed[:, 0, :].rearrange("p (n t d) -> p n t d", n=BATCH, t=2)
        o_sb = sb("o_sb", [P, G, H, HD])
        hidden = k_sb[:, :, :, :, :].rearrange("p j s t m -> p (j s t m)").rearrange("p (j t) -> p j t", t=T)
        enc = probs[0:ER + 1, 0, :]
        gmax = sb("gmax", [P, G])
        gsub = sb("gsub", [P, G, EX])
        gexp = sb("gexp", [P, G, EX])
        gsum = sb("gsum", [P, G])
        gprob = sb("gprob", [P, G])
        gmask = sb("gmask", [P, G, EX])
        gcand = sb("gcand", [P, G, EX])
        gbest = sb("gbest", [P, G])
        onehot = sb("onehot", [P, G, EX])
        onehotT = q_sb[0:EX, 0, :]
        onehotTb = q_sb[0:EX, 1, 0:T // 2].bitcast(BF16)
        result = o_sb[:, :, :, :].rearrange("p s h d -> p s (h d)")

        mb = ctx.enter_context(nc.psum_tensor("mb", [P, 5, BANK], F32))
        ab = ctx.enter_context(nc.psum_tensor("ab", [P, 3, BANK], F32))
        BANK_B, BANK_C = 3, 4

        loaded = sem("loaded")
        ids_loaded = sem("ids_loaded")
        ids_steps = sem("ids_steps")
        constants = sem("constants")
        zeroed = sem("zeroed")
        eps_set = sem("eps_set")
        rate_held = sem("rate_held")
        rate_exp = sem("rate_exp")
        ids_picked = sem("ids_picked")
        embedded = sem("embedded")
        ssq_done = sem("ssq_done")
        rms_log = sem("rms_log")
        rms_done = sem("rms_done")
        xn_ready = sem("xn_ready")
        xnT_ready = sem("xnT_ready")
        xnT_in = sem("xnT_in")
        xr_ready = sem("xr_ready")
        skip_added = sem("skip_added")
        z_abs_done = sem("z_abs_done")
        tap_last = sem("tap_last")
        taps_done = sem("taps_done")
        res_ready = sem("res_ready")
        res_in = sem("res_in")
        gate_ready = sem("gate_ready")
        xs_ready = sem("xs_ready")
        xdbl_ready = sem("xdbl_ready")
        bc_high = sem("bc_high")
        dt_ready = sem("dt_ready")
        bc_steps = sem("bc_steps")
        z_ready = sem("z_ready")
        z_split = sem("z_split")
        z_taken = sem("z_taken")
        z_exped = sem("z_exped")
        z_logged = sem("z_logged")
        delta_steps = sem("delta_steps")
        b_ready = sem("b_ready")
        c_ready = sem("c_ready")
        y_added = sem("y_added")
        decayed = sem("decayed")
        driven = sem("driven")
        scanned = sem("scanned")
        read_out = sem("read_out")
        gated = sem("gated")
        mixed = sem("mixed")
        half_added = sem("half_added")
        layer_done = sem("layer_done")
        input_kept = sem("input_kept")

        stats_done = sem("stats_done")
        stats_part = sem("stats_part")
        var_log = sem("var_log")
        var_done = sem("var_done")
        x_ready = sem("x_ready")
        ln_ready = sem("ln_ready")
        hT_ready = sem("hT_ready")
        hT_in = sem("hT_in")
        bias_added = sem("bias_added")
        qk_ready = sem("qk_ready")
        qk_in = sem("qk_in")
        v_ready = sem("v_ready")
        v_in = sem("v_in")
        scored = sem("scored")
        top_found = sem("top_found")
        exped = sem("exped")
        turned = sem("turned")
        turned_in = sem("turned_in")
        weighted = sem("weighted")
        o_taken = sem("o_taken")
        o_steps = sem("o_steps")
        o_ssq = sem("o_ssq")
        o_log = sem("o_log")
        o_rstd = sem("o_rstd")
        o_normed = sem("o_normed")
        proj_ready = sem("proj_ready")
        x2_ready = sem("x2_ready")
        res_steps = sem("res_steps")
        fc1_ready = sem("fc1_ready")
        gelu_done = sem("gelu_done")
        fc2_ready = sem("fc2_ready")
        h3_ready = sem("h3_ready")
        enc_ready = sem("enc_ready")
        ones_set = sem("ones_set")
        enc_in = sem("enc_in")
        logits_ready = sem("logits_ready")
        gate_shift = sem("gate_shift")
        gate_exp = sem("gate_exp")
        route_steps = sem("route_steps")
        onehot_ready = sem("onehot_ready")
        turned_hot = sem("turned_hot")
        hot_in = sem("hot_in")
        ex_ready = sem("ex_ready")
        ex_gelu = sem("ex_gelu")
        masks_ready = sem("masks_ready")
        ex_masked = sem("ex_masked")
        out_ready = sem("out_ready")
        result_ready = sem("result_ready")
        stored = sem("stored")

        NW = 16 * (len(WEIGHTS) + len(SELECTORS))

        def sets(odd):
            i = 0 if odd else 1
            return gate_2[:, i], bc_parts_2[:, i], delta_2[:, i], delta_x_2[:, i]

        def later(n):
            return not isinstance(n, int) or n > 0

        def phases(run, loop):
            last = 2 * GROUPS - 1

            def both(g):
                run(ODD, (2 * g - 1, 0, True), (2 * g, 1, False, 2 * g - 2), (2 * g - 2, 1, kept, g, False), g - 2)
                run(EVEN, (2 * g, 1, False), (2 * g + 1, 0, True, 64 * g + 128), (2 * g - 1, 0, emb, g + 1, True), g - 2)

            run(EVEN, None, (0, 0, False, 64), None, None)
            run(EVEN, (0, 0, False), (1, 0, True, 128), None, None)
            run(ODD, None, None, (0, 0, kept, 1, False), None)
            run(ODD, (1, 0, True), (2, 1, False, 1), None, None)
            run(EVEN, (2, 1, False), (3, 0, True, 192), (1, 0, emb, 2, True), None)
            both(2)
            with loop(3, GROUPS - 1, 1) as g:
                both(g)
            run(ODD, (last - 2, 0, True), (last - 1, 1, False, last - 3), (last - 3, 1, kept, GROUPS - 1, False), GROUPS - 3)
            run(EVEN, (last - 1, 1, False), (last, 1, True, last - 1), (last - 2, 0, emb, GROUPS, True), GROUPS - 3)
            run(ODD, (last, 1, True), None, (last - 1, 1, kept, GROUPS, False), GROUPS - 2)
            run(EVEN, None, None, None, GROUPS - 2)
            run(ODD, None, None, (last, 1, mid, GROUPS, True), GROUPS - 1)
            run(EVEN, None, None, None, GROUPS - 1)

        block = ctx.enter_context(nc.Block())

        @block.sync
        def _(sp):
            sp.dma_start(ids_raw[:, :], ids).then_inc(ids_loaded, 16)
            for name, (p0, rows, _cols) in {**WEIGHTS, **SELECTORS}.items():
                sp.dma_start(w[name][p0:p0 + rows, :], weights[name]).then_inc(loaded, 16)

            with sp.Fori(0, GROUPS, 1) as g:
                sp.wait_ge(result_ready, g + 1)
                sp.dma_start(out[bass.ds(g, 1)].rearrange("a p s d -> p (a s) d"), result[:, :, :]).then_inc(stored, 16)
            sp.wait_ge(stored, 16 * GROUPS)

        @block.gpsimd
        def _(pool):
            nc.gpsimd.memset(xr_pad[:, :, :, 0:PAD], 0.0)
            for i in range(2):
                nc.gpsimd.memset(decay[:, i].rearrange("p c (s t) -> p (c s) t", s=G)[:, :, 0:1], 0.0)
            nc.gpsimd.memset(v_sb[:, :, :, HD:OW], 1.0).then_inc(zeroed, 1)

            def gather(g):
                pool.wait_ge(ids_steps, 4)
                if isinstance(g, int):
                    nc.gpsimd.tensor_copy(ids_now[:, :], ids_ok[:, G * g:G * g + G]).then_inc(ids_picked, 1)
                else:
                    nc.gpsimd.tensor_copy(ids_now[:, :], ids_ok[:, bass.ds(G * g, G)]).then_inc(ids_picked, 1)
                pool.wait_ge(ids_picked, g + 1)
                nc.gpsimd.tensor_tensor(spare[:, 1:2], eps5[:, :], eps5[:, :], ALU.add)
                for s in range(G):
                    nc.gpsimd.indirect_dma_start(
                        out=emb[:, s, :], out_offset=None, in_=emb_rows,
                        in_offset=bass.IndirectOffsetOnAxis(ap=ids_now[:, s:s + 1], axis=0),
                    ).then_inc(embedded, 16)

            def attention(a, unit):
                if unit == AT_NORM[1] + 1:
                    pool.wait_ge(ln_ready, 3 * a + 1)
                    bias = vec("proj_b", 0, DM).unsqueeze(1).to_broadcast([P, G, DM])
                    nc.gpsimd.tensor_tensor(x_2[:, :, :], x_a[:, :, :], bias, ALU.add).then_inc(bias_added, 1)
                if unit == AT_STATS[2] + 1:
                    pool.wait_ge(x2_ready, a + 1)
                    nc.gpsimd.tensor_tensor(h_3[:, :, :], x_2[:, :, :], mamba_out[:, :, :], ALU.add).then_inc(res_steps, 1)
                    pool.wait_ge(res_steps, 2 * a + 1)
                    bias = vec("fc2_b", 0, DM).unsqueeze(1).to_broadcast([P, G, DM])
                    nc.gpsimd.tensor_tensor(h_3[:, :, :], h_3[:, :, :], bias, ALU.add).then_inc(res_steps, 1)

            pool.wait_ge(loaded, NW)
            pool.wait_ge(eps_set, 1)
            gather(0)
            pool.wait_ge(embedded, 64)
            nc.gpsimd.tensor_copy(kept[:, :, :], emb[:, :, :]).then_inc(input_kept, 1)
            pool.wait_ge(input_kept, 1)
            pool.wait_ge(xn_ready, 1)
            gather(1)

            def both(g, gathers):
                pool.wait_ge(layer_done, 2 * g - 1)
                nc.gpsimd.tensor_tensor(spare[:, 2:3], eps5[:, :], eps5[:, :], ALU.add)
                nc.gpsimd.tensor_copy(kept[:, :, :], mid[:, :, :]).then_inc(input_kept, 1)
                for unit in range(PLACES):
                    attention(g - 2, unit)
                if gathers:
                    pool.wait_ge(layer_done, 2 * g)
                    gather(g + 1)
                for unit in range(PLACES, 2 * PLACES):
                    attention(g - 2, unit)

            pool.wait_ge(layer_done, 1)
            nc.gpsimd.tensor_copy(kept[:, :, :], mid[:, :, :]).then_inc(input_kept, 1)
            pool.wait_ge(layer_done, 2)
            gather(2)
            both(2, True)
            with pool.Fori(3, GROUPS - 1, 1) as g:
                both(g, True)
            both(GROUPS - 1, False)
            for a in (GROUPS - 2, GROUPS - 1):
                for unit in range(2 * PLACES):
                    attention(a, unit)

        @block.tensor
        def _(pe):
            pe.wait_ge(loaded, NW)

            def front(kind, layer, place):
                n, l, odd, _ = layer
                gate, bc_parts, delta, delta_x = sets(odd)
                step = place - F_AT[kind]
                for k in range(KN):
                    if step == F_TURN + k:
                        if k:
                            pe.wait_ge(xnT_in, KN * n + k)
                        else:
                            pe.wait_ge(xn_ready, n + 1)
                        for s in range(G):
                            ins = nc.tensor.transpose(ab[0:KC, 2, s * L:(s + 1) * L], xn[:, s, k * KC:(k + 1) * KC], ident)
                        ins.then_inc(xnT_ready, 1)
                for c in range(CN):
                    if step == F_XR[c]:
                        if c:
                            pe.wait_ge(tap_last, CN * n + c)
                        else:
                            pe.wait_ge(xnT_in, KN * n + KN)
                        for k in range(KN):
                            ins = nc.tensor.matmul(ab[:, 2, :], w_in[:, l, k, c * P:(c + 1) * P], xnT[:, k, :],
                                                   start=(k == 0), stop=(k == KN - 1))
                        ins.then_inc(xr_ready, 1)
                    if step == F_RES[c]:
                        if c:
                            pe.wait_ge(res_in, CN * n + c)
                        else:
                            pe.wait_ge(tap_last, CN * n + CN)
                        for k in range(KN):
                            ins = nc.tensor.matmul(ab[:, 2, :], w_in[:, l, k, DI + c * P:DI + (c + 1) * P], xnT[:, k, :],
                                                   start=(k == 0), stop=(k == KN - 1))
                        ins.then_inc(res_ready, 1)
                if step == F_XPROJ:
                    pe.wait_ge(res_in, CN * n + CN)
                    for c in range(CN):
                        pe.wait_ge(xs_ready, CN * n + c + 1)
                        ins = nc.tensor.matmul(ab[0:XROWS, 2, :], w_x[:, l, c, :], xs[:, c, :], start=(c == 0), stop=(c == CN - 1))
                    ins.then_inc(xdbl_ready, 1)
                for c in range(CN):
                    if step == F_Z + c:
                        if c == 0:
                            pe.wait_ge(dt_ready, n + 1)
                            pe.wait_ge(bc_steps, 5 * n + 5)
                        else:
                            pe.wait_ge(z_taken, CN * n + c)
                        nc.tensor.matmul(ab[:, 2, :], w_dt[DT0:DT0 + RANK, l, c * P:(c + 1) * P],
                                         dt_in[DT0:DT0 + RANK, :], start=True, stop=True).then_inc(z_ready, 1)

            def send_b(layer, i):
                n, l, odd = layer[:3]
                if i or later(n):
                    pe.wait_ge(driven, NS * n + i)
                if i == 0:
                    pe.wait_ge(bc_steps, 5 * n + 5)
                nc.tensor.matmul(mb[:, BANK_B, :], sel_bc[:, i, :], sets(odd)[1][:, :], start=True, stop=True).then_inc(b_ready, 1)

            def send_c(layer, i):
                n, l, odd = layer[:3]
                if i or later(n):
                    pe.wait_ge(read_out, NS * n + i)
                nc.tensor.matmul(mb[:, BANK_C, :], sel_bc[:, NS + i, :], sets(odd)[1][:, :], start=True, stop=True).then_inc(c_ready, 1)

            def add_y(n, i, c):
                if c == 0:
                    pe.wait_ge(read_out, NS * n + i + 1)
                ins = nc.tensor.matmul(mb[:, c, :], ident, state[:, i % RING, c, :], start=False, stop=(i == NS - 1))
                if c == CN - 1:
                    ins.then_inc(y_added, 1)

            def skip(layer):
                n, l, odd = layer
                if later(n):
                    pe.wait_ge(gated, n)
                for c in range(CN):
                    ins = nc.tensor.matmul(mb[:, c, :], diag_d[:, l, c, :], xs[:, c, :], start=True, stop=False)
                ins.then_inc(skip_added, 1)

            def out_proj(out, place):
                n, l = out[:2]
                half = place - AT_OUT_PROJ
                if half in (0, 1):
                    if half:
                        pe.wait_ge(half_added, n + 1)
                    else:
                        pe.wait_ge(gated, n + 1)
                        if not isinstance(n, int) or n < 2 * GROUPS - 1:
                            pe.wait_ge(z_taken, CN * n + 2 * CN)
                    gate = sets(out[4])[0]
                    for i, s in enumerate((2 * half, 2 * half + 1)):
                        for c in range(CN):
                            ins = nc.tensor.matmul(ab[:, 2, i * DM:(i + 1) * DM],
                                                   gate[:, c, s * L:(s + 1) * L], w_out[:, l, c, :],
                                                   start=(c == 0), stop=(c == CN - 1))
                    ins.then_inc(mixed, 1)

            def run(kind, scan, ahead, out, a):
                def aside(place):
                    if out:
                        out_proj(out, place)
                    if ahead:
                        front(kind, ahead, place)
                    if a is not None:
                        attention(a, kind * PLACES + place)

                for i in range(NS):
                    if scan:
                        send_c(scan, i)
                    if i == 0 and out:
                        for c in range(CN):
                            add_y(out[0], NS - 1, c)
                    for c in range(CN):
                        aside(3 * i + c)
                        if scan and i:
                            add_y(scan[0], i - 1, c)
                        elif scan and c == 1:
                            skip(scan)
                        if scan and c == CN - 1:
                            if i + 2 < NS:
                                send_b(scan, i + 2)
                            elif ahead:
                                send_b(ahead, i + 2 - NS)
                if ahead and not scan:
                    send_b(ahead, 0)
                    send_b(ahead, 1)

            def turn(src, count):
                for k in range(KN):
                    for s in range(G):
                        ins = nc.tensor.transpose(ab[0:KC, k, s * L:(s + 1) * L], src[:, s, k * KC:(k + 1) * KC], ident)
                    ins.then_inc(hT_ready, 1)

            def attention(a, unit):
                if unit == AT_TURN[0]:
                    pe.wait_ge(ln_ready, 3 * a + 1)
                    if not isinstance(a, int) or a:
                        pe.wait_ge(result_ready, a)
                    turn(normed, 0)
                for j in range(6):
                    if unit == AT_QK[j]:
                        if j == 0:
                            pe.wait_ge(hT_in, 4 * KN * a + KN)
                        if j >= 2:
                            pe.wait_ge(qk_in, 6 * a + j - 1)
                        for k in range(KN):
                            ins = nc.tensor.matmul(ab[:, j % 2, :], w_qk[:, k, j, :], hT[:, k, :],
                                                   start=(k == 0), stop=(k == KN - 1))
                        ins.then_inc(qk_ready, 1)
                if unit == AT_V:
                    pe.wait_ge(qk_in, 6 * a + 6)
                    for s in range(G):
                        for k in range(KN):
                            ins = nc.tensor.matmul(ab[:, s // 2, (s % 2) * DM:(s % 2 + 1) * DM],
                                                   hT[:, k, s * L:(s + 1) * L], w_v[:, k, :], start=(k == 0), stop=(k == KN - 1))
                    ins.then_inc(v_ready, 1)
                pair, h, s0 = head_pair(unit, AT_HEADS)
                if pair is not None:
                    j, r = h // 4, 32 * (h % 4)
                    if pair == 0:
                        pe.wait_ge(v_in, a + 1)
                    else:
                        pe.wait_ge(exped, PAIRS * a + pair)
                    for i in range(2):
                        s = s0 + i
                        ins = nc.tensor.matmul(ab[:, 0, i * 2 * L:(i + 1) * 2 * L], q_sb[r:r + 32, j, s * L:(s + 1) * L],
                                               k_sb[r:r + 32, j, s, :, :].rearrange("p t m -> p (t m)"), start=True, stop=True)
                    ins.then_inc(scored, 1)
                t = head_slot(unit, AT_HEADS_OUT)
                if t is not None:
                    s, h = t // 2 // H * 2 + t % 2, t // 2 % H
                    pe.wait_ge(turned_in, HEAD_SLOTS * a + t + 1)
                    for q in range(2):
                        at = 2 * L + ((t % BATCH) * 2 + q) * OW
                        ins = nc.tensor.matmul(ab[:, 1, at:at + OW], probsT[:, t % 2, q * L:(q + 1) * L],
                                               v_sb[:, s, h, :], start=True, stop=True)
                    ins.then_inc(weighted, 1)
                t = head_slot(unit, AT_HEADS_TURN)
                if t is not None:
                    pe.wait_ge(exped, PAIRS * a + t // 2 + 1)
                    if t:
                        pe.wait_ge(turned_in, HEAD_SLOTS * a + t)
                    for q in range(2):
                        at = (t % 2 * 2 + q) * L
                        ins = nc.tensor.transpose(ab[:, 1, q * L:(q + 1) * L], probs[:, t // 2 % 2, at:at + L], ident)
                    ins.then_inc(turned, 1)
                if unit == AT_TURN[1]:
                    pe.wait_ge(o_normed, a + 1)
                    turn(normed, 1)
                if unit == AT_PROJ:
                    pe.wait_ge(hT_in, 4 * KN * a + 2 * KN)
                    for s in range(G):
                        for k in range(KN):
                            ins = nc.tensor.matmul(ab[:, s // 2, (s % 2) * DM:(s % 2 + 1) * DM],
                                                   hT[:, k, s * L:(s + 1) * L], w_proj[:, k, :], start=(k == 0), stop=(k == KN - 1))
                    ins.then_inc(proj_ready, 1)
                if unit == AT_TURN[2]:
                    pe.wait_ge(ln_ready, 3 * a + 2)
                    turn(normed, 2)
                for j in range(FC):
                    if unit == AT_FC1[j // 2]:
                        if j == 0:
                            pe.wait_ge(hT_in, 4 * KN * a + 3 * KN)
                        if j >= 2:
                            pe.wait_ge(gelu_done, FC * a + j - 1)
                        for k in range(KN):
                            ins = nc.tensor.matmul(ab[:, j % 2, :], w_fc1[:, k, j * P:(j + 1) * P], hT[:, k, :],
                                                   start=(k == 0), stop=(k == KN - 1))
                        ins.then_inc(fc1_ready, 1)
                if unit in (AT_FC2, AT_FC2 + 1):
                    pe.wait_ge(gelu_done, FC * a + FC)
                    half = unit - AT_FC2
                    for s in (2 * half, 2 * half + 1):
                        for j in range(FC):
                            ins = nc.tensor.matmul(ab[:, s // 2, (s % 2) * DM:(s % 2 + 1) * DM],
                                                   hidden[:, j, s * L:(s + 1) * L], w_fc2[:, j, :], start=(j == 0), stop=(j == FC - 1))
                    ins.then_inc(fc2_ready, 1)
                if unit == AT_TURN[3]:
                    pe.wait_ge(ln_ready, 3 * a + 3)
                    turn(normed, 3)
                if unit == AT_ENC:
                    pe.wait_ge(hT_in, 4 * KN * a + 4 * KN)
                    for k in range(KN):
                        ins = nc.tensor.matmul(ab[0:ER, 0, :], w_enc[:, k, :], hT[:, k, :], start=(k == 0), stop=(k == KN - 1))
                    ins.then_inc(enc_ready, 1)
                if unit == AT_LOGITS:
                    pe.wait_ge(enc_in, a + 1)
                    pe.wait_ge(ones_set, a + 1)
                    for s in range(G):
                        ins = nc.tensor.matmul(ab[:, 1, s * EX:(s + 1) * EX], enc[:, s * L:(s + 1) * L], w["w_sw"][:, :],
                                               start=True, stop=True)
                    ins.then_inc(logits_ready, 1)
                if unit == AT_ROUTE_TURN:
                    pe.wait_ge(onehot_ready, a + 1)
                    for s in range(G):
                        ins = nc.tensor.transpose(ab[0:EX, 1, s * L:(s + 1) * L], onehot[:, s, :], ident)
                    ins.then_inc(turned_hot, 1)
                for j in range(EC):
                    if unit == AT_EXPERTS[j // 2]:
                        if j < 2:
                            pe.wait_ge(hot_in, 2 * a + 2)
                        else:
                            pe.wait_ge(ex_gelu, EC * a + j - 1)
                        for k in range(KN):
                            ins = nc.tensor.matmul(ab[:, j % 2, :], w_1[:, k, j * P:(j + 1) * P], hT[:, k, :],
                                                   start=(k == 0), stop=(k == KN - 1))
                        ins.then_inc(ex_ready, 1)
                    if unit == AT_MASKS[j // 2]:
                        if j < 2:
                            pe.wait_ge(ex_gelu, EC * a + EC)
                        else:
                            pe.wait_ge(ex_masked, EC * a + j - 1)
                        nc.tensor.matmul(ab[:, j % 2, :], sel_ex[:, j, :], onehotTb, start=True, stop=True).then_inc(masks_ready, 1)
                if unit in (AT_OUT, AT_OUT + 1):
                    pe.wait_ge(ex_masked, EC * a + EC)
                    half = unit - AT_OUT
                    for s in (2 * half, 2 * half + 1):
                        for j in range(EC):
                            nc.tensor.matmul(ab[:, s // 2, (s % 2) * DM:(s % 2 + 1) * DM],
                                             hidden[:, j, s * L:(s + 1) * L], w_2[:, j, :], start=(j == 0), stop=False)
                        ins = nc.tensor.matmul(ab[:, s // 2, (s % 2) * DM:(s % 2 + 1) * DM],
                                               onehotT[:, s * L:(s + 1) * L], w["b_2"][:, :], start=False, stop=True)
                    ins.then_inc(out_ready, 1)

            pe.wait_ge(constants, 1)
            phases(run, pe.Fori)

        @block.scalar
        def _(act):
            act.wait_ge(loaded, NW)
            act.wait_ge(zeroed, 1)
            act.wait_ge(eps_set, 1)
            act.wait_ge(rate_held, 1)
            nc.scalar.preload_act_table_set(EXP_LOG)
            nc.scalar.activation(decay_rate[:, :], decay_rate[:, :], ACT.Exp).then_inc(rate_exp, 1)
            act.wait_ge(constants, 1)

            def front(kind, layer, place):
                n, l, odd, inputs = layer
                gate, bc_parts, delta, delta_x = sets(odd)
                src = (emb, mid)[l]
                step = place - F_AT[kind]
                if step == F_STAT:
                    if l == 0:
                        act.wait_ge(embedded, inputs)
                    else:
                        act.wait_ge(layer_done, inputs)
                    if later(n):
                        act.wait_ge(skip_added, n)
                    for s in range(G):
                        ins = nc.scalar.activation(xn[:, s, :], src[:, s, :], ACT.Square, accum_out=ssq[:, s:s + 1])
                    ins.then_inc(ssq_done, 1)
                    act.wait_ge(ssq_done, n + 1)
                    nc.scalar.activation(lnv[:, :], ssq[:, :], ACT.Ln, scale=1.0 / DM, bias=eps5[:, 0:1]).then_inc(rms_log, 1)
                    act.wait_ge(rms_log, n + 1)
                    nc.scalar.activation(rstd[:, :], lnv[:, :], ACT.Exp, scale=-0.5).then_inc(rms_done, 1)
                for k in range(KN):
                    if step == F_TURN + k:
                        act.wait_ge(xnT_ready, KN * n + k + 1)
                        nc.scalar.activation(xnT[:, k, :], ab[0:KC, 2, :], ACT.Copy,
                                             scale=mvec(f"norm{l}", k)).then_inc(xnT_in, 1)
                for c in range(CN):
                    if step == F_XR[c]:
                        act.wait_ge(xr_ready, CN * n + c + 1)
                        bank = ab[:, 2, :]
                        nc.scalar.activation(xr_pad[:, c, :, PAD:], bank.rearrange("p (s t) -> p s t", s=G), ACT.Copy)
                        i = l * CN + c
                        nc.scalar.activation(xs[:, c, :], bank, ACT.Identity, scale=vec("conv_w", i * TAPS + PAD),
                                             bias=vec("conv_b", i)).then_inc(tap_last, 1)
                    if step == F_RES[c]:
                        act.wait_ge(res_ready, CN * n + c + 1)
                        if c == 0 and (not isinstance(n, int) or n >= 2):
                            act.wait_ge(mixed, 2 * n - 2)
                        nc.scalar.activation(gate[:, c, :], ab[:, 2, :], ACT.Copy).then_inc(res_in, 1)
                if step == F_SILU:
                    for c in range(CN):
                        act.wait_ge(taps_done, CN * PAD * n + PAD * c + PAD)
                        nc.scalar.activation(xs[:, c, :], xs[:, c, :], ACT.Silu).then_inc(xs_ready, 1)
                    for c in range(CN):
                        act.wait_ge(res_in, CN * n + c + 1)
                        nc.scalar.activation(gate[:, c, :], gate[:, c, :], ACT.Silu).then_inc(gate_ready, 1)
                    nc.scalar.preload_act_table_set(EXP_LOG)
                if step == F_XPROJ + 1:
                    act.wait_ge(xdbl_ready, n + 1)
                    nc.scalar.activation(dt_in[DT0:DT0 + RANK, :], ab[DT0:DT0 + RANK, 2, :], ACT.Copy).then_inc(dt_ready, 1)
                    nc.scalar.activation(bc_parts[:, :], ab[0:3 * BCR, 2, :], ACT.Copy).then_inc(bc_high, 1)
                for c in range(CN):
                    z = z_tmp[:, c]
                    if step == F_Z + c:
                        act.wait_ge(z_ready, CN * n + c + 1)
                        bank = ab[:, 2, :].rearrange("p (s t) -> p s t", s=G)
                        nc.scalar.activation(z, bank, ACT.Abs, bias=vec("dt_b", l * CN + c)).then_inc(z_abs_done, 1)
                        nc.scalar.activation(delta[:, c, :], ab[:, 2, :], ACT.Relu, bias=vec("dt_b", l * CN + c)).then_inc(z_taken, 1)
                        act.wait_ge(z_abs_done, CN * n + c + 1)
                        nc.scalar.activation(z, z, ACT.Exp, scale=-1.0).then_inc(z_exped, 1)
                    if step == F_LOG + c:
                        act.wait_ge(z_split, 2 * CN * n + 2 * c + 2)
                        nc.scalar.activation(z, z, ACT.Ln, bias=1.0).then_inc(z_logged, 1)

            def decay_step(layer, i, c):
                n, l, odd = layer[:3]
                delta = sets(odd)[2]
                if c == 0 and (i >= 2 or later(n)):
                    act.wait_ge(scanned, NS * n + i - 1)
                if i == 0 and c == 0:
                    act.wait_ge(delta_steps, 3 * CN * n + 3 * CN)
                at = (l * CN + c) * NS + i
                ins = nc.scalar.activation(decay[:, i % 2, c, :].rearrange("p (s t) -> p s t", s=G)[:, :, 1:],
                                           delta[:, c, :].rearrange("p (s t) -> p s t", s=G)[:, :, 1:],
                                           ACT.Exp, scale=decay_rate[:, at:at + 1])
                if c == CN - 1:
                    ins.then_inc(decayed, 1)

            def run(kind, scan, ahead, out, a):
                for i in range(NS):
                    for c in range(CN):
                        place = 3 * i + c
                        if scan and i + 1 < NS:
                            decay_step(scan, i + 1, c)
                        elif scan and ahead:
                            decay_step(ahead, 0, c)
                        if ahead:
                            front(kind, ahead, place)
                        if a is not None:
                            attention(a, kind * PLACES + place)
                if ahead and not scan:
                    for c in range(CN):
                        decay_step(ahead, 0, c)

            def inv_std(a, i):
                act.wait_ge(stats_done, 4 * a + i + 1)
                nc.scalar.activation(a_ln[:, :], mv[:, :, 1], ACT.Ln, bias=eps5[:, 0:1]).then_inc(var_log, 1)
                act.wait_ge(var_log, 4 * a + i + 1)
                nc.scalar.activation(a_rstd[:, :], a_ln[:, :], ACT.Exp, scale=-0.5).then_inc(var_done, 1)

            def take_outputs(batch):
                if later(batch):
                    act.wait_ge(o_steps, 4 * batch)
                nc.scalar.activation(o_raw[:, :, :, :].rearrange("p n t w -> p (n t w)"),
                                     ab[:, 1, 2 * L:2 * L + 2 * BATCH * OW], ACT.Copy).then_inc(o_taken, 1)

            def take_turned(a, i, weight, bias):
                for k in range(KN):
                    act.wait_ge(hT_ready, 4 * KN * a + KN * i + k + 1)
                    if bias:
                        ins = nc.scalar.activation(hT[:, k, :], ab[0:KC, k, :], ACT.Identity, scale=mvec(weight, k), bias=mvec(bias, k))
                    elif weight:
                        ins = nc.scalar.activation(hT[:, k, :], ab[0:KC, k, :], ACT.Copy, scale=mvec(weight, k))
                    else:
                        ins = nc.scalar.activation(hT[:, k, :], ab[0:KC, k, :], ACT.Copy)
                    ins.then_inc(hT_in, 1)

            def attention(a, unit):
                if unit in AT_STD:
                    inv_std(a, AT_STD.index(unit))
                if unit in AT_TURN:
                    i = AT_TURN.index(unit)
                    take_turned(a, i, ("ln1_w", "rms_w", "ln2_w", None)[i], ("ln1_b", None, "ln2_b", None)[i])
                for j in range(6):
                    if unit == AT_QK[j]:
                        act.wait_ge(qk_ready, 6 * a + j + 1)
                        bank = ab[:, j % 2, :]
                        if j < 3:
                            ins = nc.scalar.activation(q_sb[:, j, :], bank, ACT.Copy, scale=float(HD) ** -0.5)
                        else:
                            for i in range(2):
                                ins = nc.scalar.activation(k_sb[:, j % 3, :, i, :], bank.rearrange("p (s m) -> p s m", s=G), ACT.Copy,
                                                           scale=vec("set", i))
                        ins.then_inc(qk_in, 1)
                if unit == AT_V:
                    act.wait_ge(v_ready, a + 1)
                    for i in range(2):
                        ins = nc.scalar.activation(v_sb[:, 2 * i:2 * i + 2, :, 0:HD],
                                                   ab[:, i, 0:2 * DM].rearrange("p (s h d) -> p s h d", s=2, h=H), ACT.Copy)
                    ins.then_inc(v_in, 1)
                pair, _, _ = head_pair(unit, AT_HEADS + 1)
                if pair is not None:
                    act.wait_ge(top_found, PAIRS * a + pair + 1)
                    if pair >= 2:
                        act.wait_ge(turned, HEAD_SLOTS * a + 2 * pair - 2)
                    for q in range(4):
                        ins = nc.scalar.activation(probs[:, pair % 2, q * L:(q + 1) * L], ab[:, 0, q * L:(q + 1) * L], ACT.Exp,
                                                   bias=top[:, pair % 2, q:q + 1])
                    ins.then_inc(exped, 1)
                t = head_slot(unit, AT_HEADS_TURN)
                if t is not None:
                    act.wait_ge(turned, HEAD_SLOTS * a + t + 1)
                    if t and t % BATCH == 0:
                        take_outputs(BATCHES * a + t // BATCH - 1)
                    if t >= 2:
                        act.wait_ge(weighted, HEAD_SLOTS * a + t - 1)
                    nc.scalar.activation(probsT[:, t % 2, :], ab[:, 1, 0:2 * L], ACT.Copy).then_inc(turned_in, 1)
                if unit == AT_HEADS_OUT + HEAD_SLOTS - 1:
                    act.wait_ge(weighted, HEAD_SLOTS * a + HEAD_SLOTS)
                    take_outputs(BATCHES * a + BATCHES - 1)
                if unit == AT_RMS:
                    act.wait_ge(o_steps, 4 * BATCHES * (a + 1))
                    for s in range(G):
                        ins = nc.scalar.activation(normed[:, s, :], o_sb[:, s, :, :].rearrange("p h d -> p (h d)"), ACT.Square,
                                                   accum_out=a_ssq[:, s:s + 1])
                    ins.then_inc(o_ssq, 1)
                    act.wait_ge(o_ssq, a + 1)
                    nc.scalar.activation(a_ln[:, :], a_ssq[:, :], ACT.Ln, scale=1.0 / DM, bias=eps6[:, 0:1]).then_inc(o_log, 1)
                    act.wait_ge(o_log, a + 1)
                    nc.scalar.activation(a_rstd[:, :], a_ln[:, :], ACT.Exp, scale=-0.5).then_inc(o_rstd, 1)
                for j in range(FC):
                    if unit == AT_FC1[j // 2] + 1:
                        act.wait_ge(fc1_ready, FC * a + j + 1)
                        nc.scalar.activation(hidden[:, j, :], ab[:, j % 2, :], ACT.Gelu, bias=vec("fc1_b", j)).then_inc(gelu_done, 1)
                        if j % 2:
                            nc.scalar.preload_act_table_set(EXP_LOG)
                if unit == AT_ENC:
                    act.wait_ge(enc_ready, a + 1)
                    nc.scalar.activation(enc[0:ER, :], ab[0:ER, 0, :], ACT.Identity, bias=vec("enc_b")[0:ER, :]).then_inc(enc_in, 1)
                if unit == AT_LOGITS + 2:
                    act.wait_ge(gate_shift, a + 1)
                    nc.scalar.activation(gexp[:, :, :], gsub[:, :, :], ACT.Exp).then_inc(gate_exp, 1)
                if unit == AT_ROUTE_TURN:
                    act.wait_ge(turned_hot, a + 1)
                    nc.scalar.activation(onehotT, ab[0:EX, 1, :], ACT.Copy).then_inc(hot_in, 1)
                    nc.scalar.activation(onehotTb, ab[0:EX, 1, :], ACT.Copy).then_inc(hot_in, 1)
                for j in range(EC):
                    if unit == AT_EXPERTS[j // 2] + 1:
                        act.wait_ge(ex_ready, EC * a + j + 1)
                        nc.scalar.activation(hidden[:, j, :], ab[:, j % 2, :], ACT.Gelu, bias=vec("b1", j)).then_inc(ex_gelu, 1)
                        if j % 2:
                            nc.scalar.preload_act_table_set(EXP_LOG)

            phases(run, act.Fori)

        @block.vector
        def _(dve):
            nc.vector.memset(eps5[:, :], 1e-5)
            nc.vector.memset(eps6[:, :], 1e-6).then_inc(eps_set, 1)
            dve.wait_ge(ids_loaded, 16)
            nc.vector.tensor_scalar(ids_ok[:, :], ids_raw[:, :], 0, V, ALU.is_lt, ALU.mult).then_inc(ids_steps, 1)
            dve.wait_ge(ids_steps, 1)
            nc.vector.tensor_tensor(ids_ok[:, :], ids_raw[:, :], ids_ok[:, :], ALU.add).then_inc(ids_steps, 1)
            dve.wait_ge(ids_steps, 2)
            nc.vector.tensor_scalar(ids_ok[:, :], ids_ok[:, :], 0, V - 1, ALU.max, ALU.min).then_inc(ids_steps, 2)
            dve.wait_ge(loaded, NW)
            nc.vector.tensor_scalar(decay_rate[:, :], vec("A_log", 0, LAYERS * CN * NS), LOG_MAX, None, ALU.min).then_inc(rate_held, 1)
            dve.wait_ge(rate_exp, 1)
            nc.vector.tensor_scalar(decay_rate[:, :], decay_rate[:, :], -1.0, None, ALU.mult)
            nc.vector.tensor_tensor(neg_lam[:, :], vec("lam2", 0, H), vec("lam1", 0, H), ALU.subtract)
            for i in range(LAYERS * CN):
                nc.vector.tensor_scalar(diag_d[:, i // CN, i % CN, :], ident, vec("D", i), None, ALU.mult)
            dve.wait_ge(zeroed, 1)
            nc.vector.memset(gbest[:, :], 0.0).then_inc(constants, 1)
            dve.wait_ge(constants, 1)
            nc.vector.tensor_scalar(neg_lam[:, :], neg_lam[:, :], 0.1, None, ALU.subtract).then_inc(constants, 1)

            def front(kind, layer, place):
                n, l, odd, inputs = layer
                gate, bc_parts, delta, delta_x = sets(odd)
                src = (emb, mid)[l]
                step = place - F_AT[kind]
                if step == F_NORM:
                    dve.wait_ge(rms_done, n + 1)
                    if l:
                        dve.wait_ge(layer_done, inputs)
                    for s in range(G):
                        ins = nc.vector.tensor_scalar(xn[:, s, :], src[:, s, :], rstd[:, s:s + 1], None, ALU.mult)
                    ins.then_inc(xn_ready, 1)
                for c in range(CN):
                    if step == F_XR[c] + 2:
                        for k in range(PAD):
                            if k == 0:
                                dve.wait_ge(tap_last, CN * n + c + 1)
                            else:
                                dve.wait_ge(taps_done, CN * PAD * n + PAD * c + k)
                            tile = xs[:, c, :].rearrange("p (s t) -> p s t", s=G)
                            nc.vector.scalar_tensor_tensor(tile, xr_pad[:, c, :, k:k + L], vec("conv_w", (l * CN + c) * TAPS + k),
                                                           tile, ALU.mult, ALU.add).then_inc(taps_done, 1)
                if step == F_XPROJ + 1:
                    dve.wait_ge(bc_high, n + 1)
                    nc.vector.tensor_tensor(bc_rest, ab[0:3 * BCR, 2, :], bc_parts[:, :], ALU.subtract).then_inc(bc_steps, 1)
                    dve.wait_ge(bc_steps, 5 * n + 1)
                    nc.vector.tensor_copy(bc_mid[:, :], bc_rest).then_inc(bc_steps, 1)
                    dve.wait_ge(bc_steps, 5 * n + 2)
                    nc.vector.tensor_tensor(bc_rest, bc_rest, bc_mid[:, :], ALU.subtract).then_inc(bc_steps, 1)
                    nc.vector.tensor_copy(bc_parts[BCR:2 * BCR, :], bc_mid[BCR:2 * BCR, :]).then_inc(bc_steps, 1)
                    dve.wait_ge(bc_steps, 5 * n + 3)
                    nc.vector.tensor_copy(bc_parts[2 * BCR:3 * BCR, :], bc_rest[2 * BCR:3 * BCR, :]).then_inc(bc_steps, 1)
                for c in range(CN):
                    z = z_tmp[:, c]
                    delta_c = delta[:, c, :].rearrange("p (s t) -> p s t", s=G)
                    delta_x_c = delta_x[:, c, :].rearrange("p (s t) -> p s t", s=G)
                    if step == F_SPLIT + c:
                        dve.wait_ge(z_exped, CN * n + c + 1)
                        nc.vector.tensor_scalar(delta_x_c, z, 1.0, 1.0, ALU.add, ALU.subtract).then_inc(z_split, 1)
                        dve.wait_ge(z_split, 2 * CN * n + 2 * c + 1)
                        nc.vector.tensor_tensor(delta_x_c, z, delta_x_c, ALU.subtract).then_inc(z_split, 1)
                    if step == F_DELTA + c:
                        m = 3 * CN * n + 3 * c
                        dve.wait_ge(z_logged, CN * n + c + 1)
                        nc.vector.scalar_tensor_tensor(delta_c, z, DELTA_MIN, delta_c, ALU.max, ALU.add).then_inc(delta_steps, 1)
                        dve.wait_ge(z_split, 2 * CN * n + 2 * c + 2)
                        dve.wait_ge(delta_steps, m + 1)
                        nc.vector.tensor_tensor(delta_c, delta_c, delta_x_c, ALU.add).then_inc(delta_steps, 1)
                        dve.wait_ge(delta_steps, m + 2)
                        nc.vector.tensor_tensor(delta_x[:, c, :], delta[:, c, :], xs[:, c, :], ALU.mult).then_inc(delta_steps, 1)

            def drive_step(layer, i):
                n, l, odd = layer[:3]
                dve.wait_ge(b_ready, NS * n + i + 1)
                if i == 0:
                    dve.wait_ge(delta_steps, 3 * CN * n + 3 * CN)
                if i >= RING or later(n):
                    dve.wait_ge(y_added, NS * n + i - RING + 1)
                b = mb[:, BANK_B, :].unsqueeze(1).to_broadcast([P, CN, T])
                nc.vector.tensor_tensor(state[:, i % RING], sets(odd)[3], b, ALU.mult).then_inc(driven, 1)

            def gating(out):
                n, odd = out[0], out[4]
                gate = sets(odd)[0]
                dve.wait_ge(y_added, NS * n + NS)
                dve.wait_ge(gate_ready, CN * n + CN)
                nc.vector.tensor_tensor(gate, mb[:, 0:CN, :], gate, ALU.mult).then_inc(gated, 1)

            def residual(out, half):
                n, l, src, keeps, _ = out
                dve.wait_ge(mixed, 2 * n + half + 1)
                if half == 0:
                    dve.wait_ge(input_kept, keeps)
                if half == 0 and l and not (isinstance(n, int) and n == 2):
                    dve.wait_ge(res_steps, n - 1 if isinstance(n, int) and n == 2 * GROUPS - 1 else n - 2)
                pair = slice(2 * half, 2 * half + 2)
                nc.vector.tensor_tensor((mid, mamba_out)[l][:, pair, :].rearrange("p s d -> p (s d)"),
                                        src[:, pair, :].rearrange("p s d -> p (s d)"),
                                        ab[:, 2, 0:2 * DM], ALU.add).then_inc(layer_done if half else half_added, 1)

            def run(kind, scan, ahead, out, a):
                def aside(place):
                    if out and place in (AT_OUT_PROJ + 1, AT_OUT_PROJ + 2):
                        residual(out, place - AT_OUT_PROJ - 1)
                    if ahead:
                        front(kind, ahead, place)
                    if a is not None:
                        attention(a, kind * PLACES + place)

                for i in range(NS):
                    if scan:
                        n = scan[0]
                        dve.wait_ge(decayed, NS * n + i + 1)
                        dve.wait_ge(driven, NS * n + i + 1)
                        nc.vector.tensor_tensor_scan(state[:, i % RING].rearrange("p c t -> p (c t)"),
                                                     decay[:, i % 2].rearrange("p c t -> p (c t)"),
                                                     state[:, i % RING].rearrange("p c t -> p (c t)"),
                                                     0.0, ALU.mult, ALU.add).then_inc(scanned, 1)
                    aside(3 * i)
                    if scan and i + 1 < NS:
                        drive_step(scan, i + 1)
                    elif scan and ahead:
                        drive_step(ahead, 0)
                    if i == 0 and out:
                        gating(out)
                    aside(3 * i + 1)
                    if scan:
                        dve.wait_ge(scanned, NS * n + i + 1)
                        dve.wait_ge(c_ready, NS * n + i + 1)
                        cc = mb[:, BANK_C, :].unsqueeze(1).to_broadcast([P, CN, T])
                        nc.vector.tensor_tensor(state[:, i % RING], state[:, i % RING], cc, ALU.mult).then_inc(read_out, 1)
                    aside(3 * i + 2)
                if ahead and not scan:
                    drive_step(ahead, 0)

            def measure(a, i, src):
                for s in range(G):
                    ins = nc.vector.bn_stats(stats[:, s, :], src[:, s, :])
                ins.then_inc(stats_part, 1)
                dve.wait_ge(stats_part, 4 * a + i + 1)
                nc.vector.memset(spare[:, 0:1], 0.0)
                for s in range(G):
                    ins = nc.vector.bn_aggr(mv[:, s, :], stats[:, s, :])
                ins.then_inc(stats_done, 1)

            def normalize(a, i, dst, src, done):
                dve.wait_ge(var_done, 4 * a + i + 1)
                for s in range(G):
                    ins = nc.vector.tensor_scalar(dst[:, s, :], src[:, s, :], mv[:, s, 0:1], a_rstd[:, s:s + 1],
                                                  ALU.subtract, ALU.mult)
                ins.then_inc(done, 1)

            def attention(a, unit):
                if unit == AT_STATS[0]:
                    dve.wait_ge(layer_done, 2 * GROUPS if isinstance(a, int) and a == GROUPS - 1 else 2 * a + 3)
                    measure(a, 0, mamba_out)
                if unit == AT_NORM[0]:
                    normalize(a, 0, x_a, mamba_out, x_ready)
                    dve.wait_ge(x_ready, a + 1)
                    measure(a, 1, x_a)
                if unit == AT_NORM[1]:
                    normalize(a, 1, normed, x_a, ln_ready)
                pair, _, _ = head_pair(unit, AT_HEADS + 1)
                if pair is not None:
                    dve.wait_ge(scored, PAIRS * a + pair + 1)
                    if pair >= 2:
                        dve.wait_ge(exped, PAIRS * a + pair - 1)
                    nc.vector.tensor_reduce(top[:, pair % 2, :], ab[:, 0, :].rearrange("p (q m) -> p q m", q=4), AX.X,
                                            ALU.max, negate=True).then_inc(top_found, 1)
                t = head_slot(unit, AT_HEADS_SUM)
                if t is not None and t % BATCH == BATCH - 1:
                    first = t // BATCH * BATCH // 2
                    h, s0, heads = first % H, first // H * 2, BATCH // 2
                    m = 4 * (BATCHES * a + t // BATCH)
                    dve.wait_ge(o_taken, BATCHES * a + t // BATCH + 1)
                    if t >= BATCH or not isinstance(a, int) or a:
                        dve.wait_ge(o_steps, m)
                    nc.vector.reciprocal(o_scale[:, :, :], o_raw[:, :, :, HD]).then_inc(o_steps, 1)
                    dve.wait_ge(o_steps, m + 1)
                    second = o_scale[:, :, 1].rearrange("p (h s) -> p h s", h=heads)
                    nc.vector.tensor_tensor(second, second, neg_lam[:, h:h + heads].unsqueeze(2).to_broadcast([P, heads, 2]),
                                            ALU.mult).then_inc(o_steps, 1)
                    dve.wait_ge(o_steps, m + 2)
                    nc.vector.tensor_tensor(o_parts, o_raw[:, :, :, 0:HD],
                                            o_scale[:, :, :].unsqueeze(3).to_broadcast([P, BATCH, 2, HD]),
                                            ALU.mult).then_inc(o_steps, 1)
                    dve.wait_ge(o_steps, m + 3)
                    if t < BATCH and (not isinstance(a, int) or a):
                        dve.wait_ge(stored, 16 * a)
                    nc.vector.tensor_tensor(o_sb[:, s0:s0 + 2, h:h + heads, :].rearrange("p s h d -> p h s d"),
                                            o_parts[:, :, 0, :].rearrange("p (h s) d -> p h s d", h=heads),
                                            o_parts[:, :, 1, :].rearrange("p (h s) d -> p h s d", h=heads), ALU.add).then_inc(o_steps, 1)
                if unit == AT_RMS_NORM:
                    nc.vector.memset(enc[ER:ER + 1, :], 1.0).then_inc(ones_set, 1)
                    dve.wait_ge(o_rstd, a + 1)
                    dve.wait_ge(o_steps, 4 * BATCHES * (a + 1))
                    for s in range(G):
                        ins = nc.vector.tensor_scalar(normed[:, s, :], o_sb[:, s, :, :].rearrange("p h d -> p (h d)"),
                                                      a_rstd[:, s:s + 1], None, ALU.mult)
                    ins.then_inc(o_normed, 1)
                pair = ab[:, 0:2, 0:2 * DM]
                if unit == AT_STATS[2]:
                    dve.wait_ge(proj_ready, a + 1)
                    dve.wait_ge(bias_added, a + 1)
                    nc.vector.tensor_tensor(x_2[:, :, :].rearrange("p (b s) d -> p b (s d)", b=2), pair,
                                            x_2[:, :, :].rearrange("p (b s) d -> p b (s d)", b=2), ALU.add).then_inc(x2_ready, 1)
                    dve.wait_ge(x2_ready, a + 1)
                    measure(a, 2, x_2)
                if unit == AT_NORM[2]:
                    normalize(a, 2, normed, x_2, ln_ready)
                if unit == AT_STATS[3]:
                    dve.wait_ge(fc2_ready, 2 * a + 2)
                    dve.wait_ge(res_steps, 2 * a + 2)
                    nc.vector.tensor_tensor(h_3[:, :, :].rearrange("p (b s) d -> p b (s d)", b=2), pair,
                                            h_3[:, :, :].rearrange("p (b s) d -> p b (s d)", b=2), ALU.add).then_inc(h3_ready, 1)
                    dve.wait_ge(h3_ready, a + 1)
                    measure(a, 3, h_3)
                if unit == AT_NORM[3]:
                    normalize(a, 3, normed, h_3, ln_ready)
                if unit == AT_LOGITS + 1:
                    dve.wait_ge(logits_ready, a + 1)
                    lg = ab[:, 1, 0:G * EX].rearrange("p (s e) -> p s e", s=G)
                    nc.vector.tensor_reduce(gmax[:, :], lg, AX.X, ALU.max).then_inc(route_steps, 1)
                    dve.wait_ge(route_steps, 6 * a + 1)
                    nc.vector.tensor_tensor(gsub[:, :, :], lg, gmax[:, :].unsqueeze(2).to_broadcast([P, G, EX]), ALU.subtract).then_inc(gate_shift, 1)
                    dve.wait_ge(gate_shift, a + 1)
                    rank = vec("rank", 0, EX).unsqueeze(1).to_broadcast([P, G, EX])
                    nc.vector.tensor_scalar(gmask[:, :, :], gsub[:, :, :], 0.0, None, ALU.is_ge).then_inc(route_steps, 1)
                    dve.wait_ge(route_steps, 6 * a + 2)
                    nc.vector.tensor_tensor(gcand[:, :, :], gmask[:, :, :], rank, ALU.mult).then_inc(route_steps, 1)
                    dve.wait_ge(route_steps, 6 * a + 3)
                    nc.vector.tensor_reduce(gbest[:, :], gcand[:, :, :], AX.X, ALU.max).then_inc(route_steps, 1)
                    dve.wait_ge(route_steps, 6 * a + 4)
                    nc.vector.tensor_tensor(onehot[:, :, :], gcand[:, :, :], gbest[:, :].unsqueeze(2).to_broadcast([P, G, EX]),
                                            ALU.is_equal).then_inc(onehot_ready, 1)
                if unit == AT_ROUTE_SUM:
                    dve.wait_ge(gate_exp, a + 1)
                    nc.vector.tensor_reduce(gsum[:, :], gexp[:, :, :], AX.X, ALU.add).then_inc(route_steps, 1)
                    dve.wait_ge(route_steps, 6 * a + 5)
                    nc.vector.reciprocal(gprob[:, :], gsum[:, :]).then_inc(route_steps, 1)
                for j in range(EC):
                    if unit == AT_MASKS[j // 2]:
                        dve.wait_ge(masks_ready, EC * a + j + 1)
                        dve.wait_ge(ex_gelu, EC * a + j + 1)
                        nc.vector.tensor_tensor(hidden[:, j, :], ab[:, j % 2, :], hidden[:, j, :], ALU.mult).then_inc(ex_masked, 1)
                if unit == AT_OUT + 1:
                    dve.wait_ge(out_ready, 2 * a + 2)
                    dve.wait_ge(route_steps, 6 * a + 6)
                    for s in range(G):
                        ins = nc.vector.scalar_tensor_tensor(result[:, s, :], ab[:, s // 2, (s % 2) * DM:(s % 2 + 1) * DM],
                                                             gprob[:, s:s + 1], h_3[:, s, :], ALU.mult, ALU.add)
                    ins.then_inc(result_ready, 1)

            phases(run, dve.Fori)


def kernel(**inputs):
    import concourse.bacc as bacc
    import ml_dtypes
    import numpy as np
    from concourse.bass_utils import run_bass_kernel_spmd

    x = {k.replace("L0_", ""): np.asarray(v) for k, v in inputs.items()}

    def chunks(a, rows):
        a = a.reshape(a.shape[:-2] + (a.shape[-2] // rows, rows, a.shape[-1]))
        return np.moveaxis(a, -2, 0).reshape(rows, -1)

    def per_channel(a, rows):
        return np.moveaxis(a.reshape(a.shape[:-1] + (a.shape[-1] // rows, rows)), -1, 0).reshape(rows, -1)

    xp = x["tok_x_proj_w"]
    bc = xp[:, :, RANK:]
    q1, k1, v1 = x["attn_qkv1_w"].reshape(3, 3, 4, HD, DM)
    q2, k2, _ = x["attn_qkv2_w"].reshape(3, 3, 4, HD, DM)
    qk = np.zeros((2, 3, 4, 2, HD, DM), np.float32)
    qk[0, :, :, 0], qk[0, :, :, 1] = q1, q2
    qk[1, :, :, 0], qk[1, :, :, 1] = k1, k2
    sw = np.concatenate([x["ffn_sw_w"], x["ffn_sw_b"][None]], 0)
    enc_b = np.zeros((P, 1), np.float32)
    enc_b[:ER, 0] = x["ffn_enc_b"]
    vectors = {
        "dt_b": per_channel(x["tok_dt_proj_b"], P),
        "conv_w": np.moveaxis(x["tok_conv_w"].reshape(LAYERS, CN, P, TAPS), 2, 0).reshape(P, -1),
        "conv_b": per_channel(x["tok_conv_b"], P), "D": per_channel(x["tok_D"], P),
        "A_log": np.moveaxis(x["tok_A_log"].reshape(LAYERS, CN, P, NS), 2, 0).reshape(P, -1),
        "lam1": np.broadcast_to(x["attn_lam1"].reshape(1, H), (P, H)),
        "lam2": np.broadcast_to(x["attn_lam2"].reshape(1, H), (P, H)),
        "fc1_b": per_channel(x["attn_fc1_b"], P), "proj_b": np.broadcast_to(x["attn_proj_b"], (P, DM)),
        "fc2_b": np.broadcast_to(x["attn_fc2_b"], (P, DM)), "enc_b": enc_b,
        "b1": per_channel(x["ffn_b1"].reshape(-1), P),
        "set": np.tile(np.repeat(np.eye(2, dtype=np.float32), HD, 0), (P // (2 * HD), 1)),
        "rank": np.broadcast_to(np.arange(EX, 0, -1, dtype=np.float32), (P, EX)),
    }
    mvectors = {"norm0": x["tok_norm_w"][0], "norm1": x["tok_norm_w"][1], "ln1_w": x["attn_ln1_w"], "ln1_b": x["attn_ln1_b"],
                "rms_w": x["attn_rms_w"], "ln2_w": x["attn_ln2_w"], "ln2_b": x["attn_ln2_b"]}
    sel_bc = np.tile(np.eye(BCR, dtype=ml_dtypes.bfloat16), (3, 1))
    sel_ex = np.zeros((EX, EC, P // ER, ER), ml_dtypes.bfloat16)
    for e in range(EX):
        sel_ex[e, e // (P // ER), e % (P // ER)] = 1
    arrays = {
        "w_in": chunks(x["tok_in_proj_w"], KC), "w_x": chunks(np.concatenate([bc, bc, bc, xp[:, :, :RANK]], -1), P),
        "w_dt": np.moveaxis(x["tok_dt_proj_w"], 1, 0).reshape(RANK, -1), "w_out": chunks(x["tok_out_proj_w"], P),
        "w_qk": chunks(qk.reshape(6 * P, DM).T, KC), "w_v": chunks(v1.reshape(DM, DM).T, KC),
        "w_proj": chunks(x["attn_proj_w"].T, KC), "w_fc1": chunks(x["attn_fc1_w"].T, KC),
        "w_fc2": chunks(x["attn_fc2_w"].T, P), "w_enc": chunks(x["ffn_enc_w"], KC), "w_sw": sw,
        "w_1": chunks(np.moveaxis(x["ffn_w1"], 0, 1).reshape(DM, EX * ER), KC),
        "w_2": chunks(x["ffn_w2"].reshape(EX * ER, DM), P), "b_2": x["ffn_b2"], "ident": np.eye(P, dtype=np.float32),
        "vec": np.concatenate([vectors[n] for n in VEC], 1), "mvec": np.concatenate([per_channel(mvectors[n], KC) for n in MVEC], 1),
        "sel_bc": sel_bc, "sel_ex": sel_ex.reshape(EX, -1),
    }
    arrays["ids"] = x["x"].T
    arrays["emb_rows"] = x["tok_emb"]
    arrays = {k: np.ascontiguousarray(v) for k, v in arrays.items()}
    nc = bacc.Bacc("TRN2", target_bir_lowering=False, num_devices=1)
    drams = {k: nc.dram_tensor(k + "_dram", v.shape, mybir.dt.from_np(v.dtype), kind="ExternalInput").ap() for k, v in arrays.items()}
    out = nc.dram_tensor("out_dram", (SEQS, L, DM), F32, kind="ExternalOutput").ap()
    build(nc, drams["ids"], drams["emb_rows"], drams, out.rearrange("(g s) p d -> g p s d", s=G))
    r = run_bass_kernel_spmd(nc, [{k + "_dram": v for k, v in arrays.items()}], core_ids=[0])
    return r.results[0]["out_dram"]
```
